# Optimizing a Trainium2 kernel written in Bass

```python
import numpy as np
import jax
import jax.numpy as jnp

def _softmax(x, axis=-1):
    return jax.nn.softmax(x, axis=axis)

def _gelu(x):
    return jax.nn.gelu(x, approximate=True)

def _silu(x):
    return jax.nn.silu(x)

def _sigmoid(x):
    return jax.nn.sigmoid(x)

def _layernorm(x, axis=-1, eps=1e-05):
    m = jnp.mean(x, axis=axis, keepdims=True)
    v = jnp.var(x, axis=axis, keepdims=True)
    return (x - m) / jnp.sqrt(v + eps)

def _scatter_add(tgt, idx, src, axis=0):
    return tgt.at[idx].add(src)

def _segment_sum(src, seg, n):
    return jax.ops.segment_sum(src, seg, n)
kernel_name = 'mk_sandwich_d1_jaxref_r4_4d6cee'

def setup_inputs(seed: int=0):
    np.random.seed(seed)
    _w = jnp.asarray

    def _L0_attn_setup():
        import jax, jax.numpy as jnp
        import numpy as np
        D_MODEL = 256
        D_STATE = 16
        D_CONV = 4
        D_INNER = 2 * D_MODEL
        B, T = (4, 1024)
        EPS = 1e-05

        def _layernorm(x, w, b):
            mu = jnp.mean(x, axis=-1, keepdims=True)
            var = jnp.mean(jnp.square(x - mu), axis=-1, keepdims=True)
            return (x - mu) * jax.lax.rsqrt(var + EPS) * w + b

        def _silu(x):
            return x * jax.nn.sigmoid(x)
        key = jax.random.key(seed)
        ks = jax.random.split(key, 8)
        s = lambda k, shape, fan: jax.random.normal(k, shape, jnp.float32) * (1.0 / np.sqrt(fan))
        return {'x': jax.random.normal(ks[0], (B, T, D_MODEL), jnp.float32), 'norm_w': jnp.ones((D_MODEL,), jnp.float32), 'norm_b': jnp.zeros((D_MODEL,), jnp.float32), 'in_w': s(ks[1], (D_INNER * 2, D_MODEL), D_MODEL), 'in_b': jnp.zeros((D_INNER * 2,), jnp.float32), 'conv_w': s(ks[2], (D_INNER, 1, D_CONV), D_CONV), 'conv_b': jnp.zeros((D_INNER,), jnp.float32), 'xproj_w': s(ks[3], (2 * D_STATE + 1, D_INNER), D_INNER), 'A_log': jnp.log(jnp.arange(1, D_STATE + 1, dtype=jnp.float32)), 'D': jnp.ones((D_INNER,), jnp.float32), 'out_w': s(ks[4], (D_MODEL, D_INNER), D_INNER), 'out_b': jnp.zeros((D_MODEL,), jnp.float32)}
    _L0_attn_in = _L0_attn_setup()

    def _L0_ffn_setup():
        import jax, jax.numpy as jnp
        import numpy as np
        DIM = 256
        HEADS = 16
        HD = DIM // HEADS
        M = 64
        E = 4
        K = 2
        HID = 512
        MID = 512
        LB = 0.01
        EPS = 1.1920929e-07

        def _rms(x, w):
            return x * jax.lax.rsqrt(jnp.mean(x * x, axis=-1, keepdims=True) + EPS) * w

        def _gelu(x):
            return jax.nn.gelu(x, approximate=False)
        key = jax.random.key(seed)
        ks = jax.random.split(key, 20)
        d = DIM
        w = lambda k, s: jax.random.normal(k, s, jnp.float32) * 0.02
        return {'x': jax.random.normal(ks[0], (4, 256, d), jnp.float32), 'n1_w': jnp.ones((d,), jnp.float32), 'n2_w': jnp.ones((d,), jnp.float32), 'wq': w(ks[1], (d, d)), 'wk': w(ks[2], (d, d)), 'wv': w(ks[3], (d, d)), 'wo': w(ks[4], (d, d)), 'qn_w': jnp.ones((HD,), jnp.float32), 'kn_w': jnp.ones((HD,), jnp.float32), 'gate_w': w(ks[5], (E, d)), 'e0_up': w(ks[6], (HID, d)), 'e0_down': w(ks[7], (d, HID)), 'e1_w1': w(ks[8], (HID, d)), 'e1_w2': w(ks[9], (HID, d)), 'e1_down': w(ks[10], (d, HID)), 'e2_l1': w(ks[11], (MID, d)), 'e2_l2': w(ks[12], (HID, MID)), 'e2_l3': w(ks[13], (MID, HID)), 'e2_l4': w(ks[14], (d, MID)), 'e3_down': w(ks[15], (d, d)), 'e3_up': w(ks[16], (HID, d)), 'e3_out': w(ks[17], (d, HID))}
    _L0_ffn_in = _L0_ffn_setup()
    _d = {'L0_attn_x': _L0_attn_in['x'], 'L0_attn_norm_w': _L0_attn_in['norm_w'], 'L0_attn_norm_b': _L0_attn_in['norm_b'], 'L0_attn_in_w': _L0_attn_in['in_w'], 'L0_attn_in_b': _L0_attn_in['in_b'], 'L0_attn_conv_w': _L0_attn_in['conv_w'], 'L0_attn_conv_b': _L0_attn_in['conv_b'], 'L0_attn_xproj_w': _L0_attn_in['xproj_w'], 'L0_attn_A_log': _L0_attn_in['A_log'], 'L0_attn_D': _L0_attn_in['D'], 'L0_attn_out_w': _L0_attn_in['out_w'], 'L0_attn_out_b': _L0_attn_in['out_b'], 'L0_ffn_n1_w': _L0_ffn_in['n1_w'], 'L0_ffn_n2_w': _L0_ffn_in['n2_w'], 'L0_ffn_wq': _L0_ffn_in['wq'], 'L0_ffn_wk': _L0_ffn_in['wk'], 'L0_ffn_wv': _L0_ffn_in['wv'], 'L0_ffn_wo': _L0_ffn_in['wo'], 'L0_ffn_qn_w': _L0_ffn_in['qn_w'], 'L0_ffn_kn_w': _L0_ffn_in['kn_w'], 'L0_ffn_gate_w': _L0_ffn_in['gate_w'], 'L0_ffn_e0_up': _L0_ffn_in['e0_up'], 'L0_ffn_e0_down': _L0_ffn_in['e0_down'], 'L0_ffn_e1_w1': _L0_ffn_in['e1_w1'], 'L0_ffn_e1_w2': _L0_ffn_in['e1_w2'], 'L0_ffn_e1_down': _L0_ffn_in['e1_down'], 'L0_ffn_e2_l1': _L0_ffn_in['e2_l1'], 'L0_ffn_e2_l2': _L0_ffn_in['e2_l2'], 'L0_ffn_e2_l3': _L0_ffn_in['e2_l3'], 'L0_ffn_e2_l4': _L0_ffn_in['e2_l4'], 'L0_ffn_e3_down': _L0_ffn_in['e3_down'], 'L0_ffn_e3_up': _L0_ffn_in['e3_up'], 'L0_ffn_e3_out': _L0_ffn_in['e3_out']}
    _x0 = _d['L0_attn_x']
    _d['L0_attn_x'] = jax.random.normal(jax.random.fold_in(jax.random.key(seed), 1), (8, 512, 256), dtype=_x0.dtype)
    del _x0
    return _d

def reference(L0_attn_x, L0_attn_norm_w, L0_attn_norm_b, L0_attn_in_w, L0_attn_in_b, L0_attn_conv_w, L0_attn_conv_b, L0_attn_xproj_w, L0_attn_A_log, L0_attn_D, L0_attn_out_w, L0_attn_out_b, L0_ffn_n1_w, L0_ffn_n2_w, L0_ffn_wq, L0_ffn_wk, L0_ffn_wv, L0_ffn_wo, L0_ffn_qn_w, L0_ffn_kn_w, L0_ffn_gate_w, L0_ffn_e0_up, L0_ffn_e0_down, L0_ffn_e1_w1, L0_ffn_e1_w2, L0_ffn_e1_down, L0_ffn_e2_l1, L0_ffn_e2_l2, L0_ffn_e2_l3, L0_ffn_e2_l4, L0_ffn_e3_down, L0_ffn_e3_up, L0_ffn_e3_out):

    def _L0_attn_ref(x, norm_w, norm_b, in_w, in_b, conv_w, conv_b, xproj_w, A_log, D, out_w, out_b):
        import jax, jax.numpy as jnp
        import numpy as np
        D_MODEL = 256
        D_STATE = 16
        D_CONV = 4
        D_INNER = 2 * D_MODEL
        B, T = (4, 1024)
        EPS = 1e-05

        def _layernorm(x, w, b):
            mu = jnp.mean(x, axis=-1, keepdims=True)
            var = jnp.mean(jnp.square(x - mu), axis=-1, keepdims=True)
            return (x - mu) * jax.lax.rsqrt(var + EPS) * w + b

        def _silu(x):
            return x * jax.nn.sigmoid(x)
        residual = x
        xn = _layernorm(x, norm_w, norm_b)
        xz = xn @ in_w.T + in_b
        xi, z = jnp.split(xz, 2, axis=-1)
        xc = jax.lax.conv_general_dilated(jnp.transpose(xi, (0, 2, 1)), conv_w, window_strides=(1,), padding=[(D_CONV - 1, 0)], dimension_numbers=('NCH', 'OIH', 'NCH'), feature_group_count=D_INNER) + conv_b[None, :, None]
        xc = _silu(jnp.transpose(xc, (0, 2, 1)))
        xp = xc @ xproj_w.T
        C = xp[..., 1 + D_STATE:]
        gate = jax.nn.sigmoid(jnp.mean(C, axis=-1, keepdims=True))
        y = xc * gate + D * xc
        y = y * _silu(z)
        y = y @ out_w.T + out_b
        return y + residual

    def _L0_ffn_ref(x, n1_w, n2_w, wq, wk, wv, wo, qn_w, kn_w, gate_w, e0_up, e0_down, e1_w1, e1_w2, e1_down, e2_l1, e2_l2, e2_l3, e2_l4, e3_down, e3_up, e3_out):
        import jax, jax.numpy as jnp
        import numpy as np
        DIM = 256
        HEADS = 16
        HD = DIM // HEADS
        M = 64
        E = 4
        K = 2
        HID = 512
        MID = 512
        LB = 0.01
        EPS = 1.1920929e-07

        def _rms(x, w):
            return x * jax.lax.rsqrt(jnp.mean(x * x, axis=-1, keepdims=True) + EPS) * w

        def _gelu(x):
            return jax.nn.gelu(x, approximate=False)
        B, T, C = x.shape
        h = _rms(x, n1_w)
        heads = lambda w_: (h @ w_.T).reshape(B, T, HEADS, HD).transpose(0, 2, 1, 3)
        q = _rms(heads(wq), qn_w)
        k = _rms(heads(wk), kn_w)
        v = heads(wv)
        scores = jnp.einsum('bhqd,bhkd->bhqk', q, k) * HD ** (-0.5)
        causal = jnp.tril(jnp.ones((T, T), bool))
        scores = jnp.where(causal[None, None], scores, -jnp.inf)
        attn = jax.nn.softmax(scores, axis=-1)
        ao = jnp.einsum('bhqk,bhkd->bhqd', attn, v).transpose(0, 2, 1, 3).reshape(B, T, C) @ wo.T
        ao = ao.at[:, :, :M].set(0.0)
        x = x + ao
        xf = _rms(x, n2_w).reshape(-1, C)
        N = xf.shape[0]
        logits = jnp.nan_to_num(xf @ gate_w.T)
        probs = jax.nn.softmax(logits, axis=-1)
        topv, topi = jax.lax.top_k(probs, K)
        topv = topv / (topv.sum(-1, keepdims=True) + 1e-08)
        wts = jnp.zeros((N, E), x.dtype).at[jnp.arange(N)[:, None], topi].add(topv)
        o0 = _gelu(xf @ e0_up.T) @ e0_down.T
        o1 = jax.nn.silu(xf @ e1_w1.T) * (xf @ e1_w2.T) @ e1_down.T
        o2 = _gelu(_gelu(_gelu(xf @ e2_l1.T) @ e2_l2.T) @ e2_l3.T) @ e2_l4.T
        o3 = _gelu(_gelu(xf @ e3_down.T) @ e3_up.T) @ e3_out.T
        moe = wts[:, 0:1] * o0 + wts[:, 1:2] * o1 + wts[:, 2:3] * o2 + wts[:, 3:4] * o3
        moe = moe.reshape(B, T, C).at[:, :, :M].set(0.0)
        return x + moe
    x = L0_attn_x
    x = x + _layernorm(_L0_attn_ref(_layernorm(x, axis=-1), L0_attn_norm_w, L0_attn_norm_b, L0_attn_in_w, L0_attn_in_b, L0_attn_conv_w, L0_attn_conv_b, L0_attn_xproj_w, L0_attn_A_log, L0_attn_D, L0_attn_out_w, L0_attn_out_b), axis=-1)
    x = x + _layernorm(_L0_ffn_ref(_layernorm(x, axis=-1), L0_ffn_n1_w, L0_ffn_n2_w, L0_ffn_wq, L0_ffn_wk, L0_ffn_wv, L0_ffn_wo, L0_ffn_qn_w, L0_ffn_kn_w, L0_ffn_gate_w, L0_ffn_e0_up, L0_ffn_e0_down, L0_ffn_e1_w1, L0_ffn_e1_w2, L0_ffn_e1_down, L0_ffn_e2_l1, L0_ffn_e2_l2, L0_ffn_e2_l3, L0_ffn_e2_l4, L0_ffn_e3_down, L0_ffn_e3_up, L0_ffn_e3_out), axis=-1)
    return x

_drawn_inputs = setup_inputs


def setup_inputs(seed=0):
    import zlib

    import numpy as np

    out = dict(_drawn_inputs(seed))
    spreads = {'L0_attn_norm_w': (1.0, 0.2),
     'L0_attn_norm_b': (0.0, 0.1),
     'L0_attn_in_b': (0.0, 0.1),
     'L0_attn_conv_b': (0.0, 0.298),
     'L0_attn_D': (1.0, 0.2),
     'L0_attn_out_b': (0.0, 0.1),
     'L0_ffn_n1_w': (1.0, 0.6),
     'L0_ffn_n2_w': (1.0, 0.6),
     'L0_ffn_qn_w': (1.0, 0.6),
     'L0_ffn_kn_w': (1.0, 0.6)}
    factors = {'L0_attn_xproj_w': 8.0,
     'L0_ffn_wq': 8.0,
     'L0_ffn_wk': 8.0,
     'L0_ffn_wv': 8.0,
     'L0_ffn_wo': 8.0,
     'L0_ffn_gate_w': 8.0,
     'L0_ffn_e0_up': 6.757,
     'L0_ffn_e0_down': 6.638,
     'L0_ffn_e1_w1': 8.0,
     'L0_ffn_e1_w2': 8.0,
     'L0_ffn_e1_down': 8.0,
     'L0_ffn_e2_l1': 8.0,
     'L0_ffn_e2_l2': 8.0,
     'L0_ffn_e2_l3': 8.0,
     'L0_ffn_e2_l4': 8.0,
     'L0_ffn_e3_down': 8.0,
     'L0_ffn_e3_up': 8.0,
     'L0_ffn_e3_out': 8.0}
    for name, (base, spread) in spreads.items():
        noise = np.random.default_rng([zlib.crc32(name.encode()), seed]).standard_normal(out[name].shape)
        drawn = base * np.exp(spread * noise) if base else spread * noise
        out[name] = jnp.asarray(drawn.astype(out[name].dtype))
    for name, factor in factors.items():
        out[name] = (out[name] * factor).astype(out[name].dtype)
    return out
```

```python
from contextlib import ExitStack

import concourse.bass as bass
from concourse import mybir

F32 = mybir.dt.float32
F32R = mybir.dt.float32r
BF16 = mybir.dt.bfloat16
U32 = mybir.dt.uint32
ACT = mybir.ActivationFunctionType
ALU = mybir.AluOpType
AX = mybir.AxisListType

P = 128
EPS_LN = 1e-5
EPS_RMS = 1.1920929e-07
MASKED = -1e30


class Links:

    def __init__(self, eng, sem, per):
        self.eng, self.sem, self.per, self.base, self.k = eng, sem, per, 0, 0

    def batch(self, b):
        assert self.k in (0, self.per), (self.k, self.per)
        self.base, self.k = b * self.per, 0

    def __call__(self, ins):
        self.k += 1
        ins.then_inc(self.sem, 1)
        self.eng.wait_ge(self.sem, self.base + self.k)


class Banks:

    def __init__(self, tiles, full, moved, per_batch):
        self.tiles, self.full, self.moved = tiles, full, moved
        self.n = len(tiles)
        assert per_batch % self.n == 0
        self.per = per_batch // self.n

    def wait_free(self, eng, b, n):
        eng.wait_ge(self.moved[n % self.n], b * self.per + n // self.n + 1)
        return self.tiles[n % self.n]

    def wait_full(self, eng, b, n):
        eng.wait_ge(self.full[n % self.n], b * self.per + n // self.n + 1)
        return self.tiles[n % self.n]

    def wait_moved(self, eng, b, n):
        eng.wait_ge(self.moved[n % self.n], b * self.per + n // self.n + 2)

    def now_full(self, ins, n):
        ins.then_inc(self.full[n % self.n], 1)

    def now_moved(self, ins, n):
        ins.then_inc(self.moved[n % self.n], 1)


def alone(eng, passed):
    eng.sem_inc(passed, 1)


def of_batch(t, b):
    return t[b] if isinstance(b, int) else t[bass.ds(b, 1)].rearrange("b p i d -> (b p) i d")


def mixer_attention_experts(nc, d, scratch, out):
    B, T, D = d["x"].shape
    NT = T // P
    KC = D // P
    DI = d["out_w"].shape[1] * P
    IC = DI // P
    HD = 16
    H = D // HD
    CH = P // HD
    NPAIR = H // 2
    NQUAD = H // 4
    ZM = 64
    DO = D - ZM
    SR = 96
    SLOTS = 4
    PTS = 20
    UNITS = 5

    x_dram, out_dram = (t.rearrange("b (i p) d -> b p i d", p=P) for t in (d["x"], out))
    x1_dram, xr_dram = (t.rearrange("b (i p) d -> b p i d", p=P) for t in scratch)

    with ExitStack() as ctx:
        def sem(name):
            return ctx.enter_context(nc.semaphore(name))

        def psum(name):
            return ctx.enter_context(nc.psum_tensor(name, [P, T], F32))

        banks = [psum(f"bank{i}") for i in range(8)]

        with ExitStack() as first:
            def sb(name, shape, dt=F32):
                return first.enter_context(nc.sbuf_tensor(name, shape, dt))

            ident = sb("ident", [P, P])
            ident16 = sb("ident16", [P, P], BF16)
            mask_q = sb("mask_q", [P, P], BF16)
            mask_k = sb("mask_k", [P, P], BF16)
            minus_half = sb("minus_half", [P, 32])
            win_h, win_l = sb("win_h", [P, KC, 2 * DI], F32R), sb("win_l", [P, KC, 2 * DI], F32R)
            wqkv_h, wqkv_l = sb("wqkv_h", [P, KC, 3 * D], F32R), sb("wqkv_l", [P, KC, 3 * D], F32R)
            wout = sb("wout", [P, IC, D])
            wo = sb("wo", [P, KC, DO])
            wgate = sb("wgate", [P, IC, P])
            wc = sb("wc", [P, IC, HD])
            gate_col = sb("gate_col", [P, IC])
            vecs = sb("vecs", [P, d["vecs"].shape[1]])
            at = {}
            col = 0
            for name, n in (("norm_w", KC), ("norm_b", KC), ("in_b", 2 * IC), ("conv_w", 4 * IC),
                            ("conv_b", IC), ("D", IC), ("n1_w", KC), ("qn_w", 1), ("kn_w", 1)):
                at[name] = vecs[:, col:col + n]
                col += n
            b_in = sb("b_in", [P, 2 * IC])
            d2 = sb("d2", [P, IC])
            out_b = sb("out_b", [P, D])

            x = sb("x_sb", [P, NT, D])
            u = sb("u", [P, NT, D])
            z = sb("z", [P, NT, D])
            zT_h, zT_l = sb("zT_h", [P, KC, T], F32R), sb("zT_l", [P, KC, T], F32R)
            xi = sb("xi", [P, IC, T + 3])
            xc = sb("xc", [P, IC, T])
            sz = sb("sz", [P, IC, T])
            th = sb("th", [P, T])
            sq = sb("sq", [P, T])
            st6 = sb("st6", [P, NT, 6])
            mv = sb("mv", [P, NT, 2])
            mv1 = sb("mv1", [P, NT, 2])
            mvf = sb("mvf", [P, NT, 2])
            sm = sb("sm", [P, 8, NT])
            ss, ssc, rqk = sb("ss", [P, NT, 32]), sb("ssc", [P, NT, 32]), sb("rqk", [P, NT, 32])
            qT_h, qT_l = sb("qT_h", [P, 4, T], F32R), sb("qT_l", [P, 4, T], F32R)
            v = sb("v", [P, NT, H, 32])
            xin = sb("xin", [P, NT, D])
            qkn = xc[:, :, :]

            qS, kS = sb("qS", [P, SLOTS, 2, T], F32R), sb("kS", [P, SLOTS, 2, T], F32R)
            mxs = sb("mxs", [P, 2, 8])
            nm_h, nm_l = sb("nm_h", [8, 2, P], F32R), sb("nm_l", [8, 2, P], F32R)
            pt = sb("pt", [P, PTS, T])
            oTs = sb("oTs", [P, T])
            rc = sb("rc", [P, NT, 4])
            otok = sb("otok", [P, NT, D])
            oT = sb("oT", [P, KC, T])

            w_stage = pt[:, 0:8, :].rearrange("p s t -> p (s t)")
            win_f = w_stage[:, 0:KC * 2 * DI].rearrange("p (k n) -> p k n", k=KC)
            wqkv_f = w_stage[:, KC * 2 * DI:KC * 2 * DI + KC * 3 * D].rearrange("p (k n) -> p k n", k=KC)

            F_USES, A_USES = 27, 20
            fb = Banks(banks[0:3], [sem(f"front_full{i}") for i in range(3)],
                       [sem(f"front_moved{i}") for i in range(3)], F_USES)
            ob = Banks(banks[3:4], [sem("o_full")], [sem("o_moved")], A_USES)
            mx_bank, st_bank = banks[4:6], banks[6:8]
            mx_full, mx_read = sem("mx_full"), sem("mx_read")
            st_full, exp_done = sem("st_full"), sem("exp_done")

            w_loaded, consts, w_hi, bias_mm, w_ready = (
                sem(n) for n in ("w_loaded", "consts", "w_hi", "bias_mm", "w_ready"))
            x_loaded, x_stored, xr_stored = sem("x_loaded"), sem("x_stored"), sem("xr_stored")
            stats, scales, z_ready, hi_ready = sem("stats"), sem("scales"), sem("z_ready"), sem("hi_ready")
            conv_done, silu_done, p_ready, y_ready = (
                sem(n) for n in ("conv_done", "silu_done", "p_ready", "y_ready"))
            ub_ready, x1_ready, xin_ready = sem("ub_ready"), sem("x1_ready"), sem("xin_ready")
            sq_ready, sq_summed, qk_scale, qT_hi = sem("sq_ready"), sem("sq_summed"), sem("qk_scale"), sem("qT_hi")
            stacked = [sem(f"stacked{i}") for i in range(SLOTS)]
            nm_hi = sem("nm_hi")
            rows = [sem("rows0"), sem("rows1")]
            dve_front, dve_att, dve_pre = sem("dve_front"), sem("dve_att"), sem("dve_pre")
            pool_front, pool_pre = sem("pool_front"), sem("pool_pre")

            passed = sem("passed")
            o_order = ["mt0", "mt1", "mt2", "mt3", "pv0", "mt4", "ot0", "mt5", "pv1", "mt6", "ot1",
                       "mt7", "pv2", "ot2", "pv3", "ot3", "t0", "t1", "wo0", "wo1"]
            O = {name: n for n, name in enumerate(o_order)}
            F_ZT, F_IN, F_GATE, F_OUT, F_HT, F_QK, F_QT, F_V = 0, 2, 10, 11, 13, 15, 19, 23

            def units(descending):
                w = (lambda i: (i + 1) * P) if descending else (lambda j: (NT - j) * P)
                full, three, two, one = (3, 2, 1, 0) if descending else (0, 1, 2, 3)
                res = []
                for h in range(2):
                    res.append([(h, full, 0, w(full))])
                    res.append([(h, three, 0, w(three)), (h, one, w(three), w(one))])
                res.append([(0, two, 0, w(two)), (1, two, w(two), w(two))])
                return res

            MAX_UNITS, ST_UNITS = units(True), units(False)
            PU = NPAIR * UNITS
            pt_at = {}
            for n, unit in enumerate(ST_UNITS):
                for h, j, c, w in unit:
                    pt_at[h, j] = (n, c, w)

            with nc.Block() as block:

                @block.sync
                def _(sp):
                    for dst, src in ((win_f, d["in_w"]), (wqkv_f, d["wqkv"]), (wout[:], d["out_w"]),
                                     (wo[:], d["wo"]), (wc[:], d["xproj_w"][:, :, 1 + HD:1 + 2 * HD]),
                                     (vecs[:], d["vecs"]), (out_b[:], d["out_b"])):
                        sp.dma_start(dst, src).then_inc(w_loaded, 16)

                    def store_x1(b):
                        sp.wait_ge(x1_ready, b + 1)
                        alone(sp, passed)
                        sp.dma_start(of_batch(x1_dram, b), x[:]).then_inc(x_stored, 16)

                    def stack(b, pair):
                        s = pair % SLOTS
                        if pair == 0:
                            for c in range(4):
                                fb.wait_moved(sp, b, F_QT + c)
                                alone(sp, passed)
                        if pair >= SLOTS:
                            sp.wait_ge(st_full, b * PU + (pair - SLOTS + 1) * UNITS)
                        lane = slice(HD * pair, HD * (pair + 1))
                        for dst, chunk, places in ((qS, 0, ((qT_h, 0), (qT_h, 16), (qT_l, 32), (qT_l, 48))),
                                                   (kS, 2, ((qT_h, 0), (qT_h, 32), (qT_l, 16), (qT_l, 48)))):
                            for src, row in places:
                                sp.dma_start(dst[row:row + HD, s, :, :].bitcast(F32),
                                             src[lane, chunk:chunk + 2, :].bitcast(F32)).then_inc(stacked[s], 16)

                    def max_rows(b, pair):
                        ob.wait_moved(sp, b, O[f"mt{pair}"])
                        for r, src in enumerate((nm_h, nm_l)):
                            sp.dma_start(qS[SR + r:SR + r + 1, pair % SLOTS, :, :].bitcast(F32),
                                         src[:, pair % 2, :].bitcast(F32)).then_inc(rows[pair % 2], 16)

                    def turn(a, f):
                        if f is not None:
                            if a is not None:
                                sp.wait_ge(xin_ready, a + 1)
                                sp.wait_ge(x_stored, 16 * a + 16)
                                alone(sp, passed)
                            sp.dma_start(x[:], of_batch(x_dram, f)).then_inc(x_loaded, 16)
                        if a is None:
                            store_x1(f)
                            return
                        for pair in range(3):
                            stack(a, pair)
                        max_rows(a, 0)
                        for pair in range(NPAIR):
                            if pair + 1 < NPAIR:
                                max_rows(a, pair + 1)
                            if pair + 3 < NPAIR:
                                stack(a, pair + 3)
                        if f is not None:
                            store_x1(f)
                        ob.wait_moved(sp, a, O["wo1"])
                        alone(sp, passed)
                        sp.dma_start(of_batch(xr_dram, a), xin[:]).then_inc(xr_stored, 16)

                    turn(None, 0)
                    with sp.Fori(0, B - 1) as a:
                        turn(a, a + 1)
                    turn(B - 1, None)
                    sp.wait_ge(xr_stored, 16 * B)
                    sp.wait_ge(x_stored, 16 * B)

                @block.gpsimd
                def _(pool):
                    nc.gpsimd.memset(ident[:], 0.0)
                    nc.gpsimd.memset(mask_q[:], 0.0)
                    nc.gpsimd.memset(mask_k[:], 0.0)
                    nc.gpsimd.memset(minus_half[:], -0.5)
                    nc.gpsimd.memset(v[:], 1.0)
                    nc.gpsimd.memset(xi[:], 0.0).then_inc(pool_pre, 1)
                    pool.wait_ge(pool_pre, 1)
                    nc.gpsimd.affine_select(out=ident[:], in_=ident[:], compare_op=ALU.not_equal, fill=1.0,
                                            base=0, pattern=[[-1, P]], channel_multiplier=1)
                    nc.gpsimd.affine_select(out=mask_q[:], in_=mask_q[:], compare_op=ALU.is_ge, fill=MASKED,
                                            base=0, pattern=[[-1, P]], channel_multiplier=1)
                    nc.gpsimd.affine_select(out=mask_k[:], in_=mask_k[:], compare_op=ALU.is_ge, fill=MASKED,
                                            base=0, pattern=[[1, P]], channel_multiplier=-1).then_inc(pool_pre, 1)
                    pool.wait_ge(pool_pre, 2)
                    nc.gpsimd.tensor_copy(ident16[:], ident[:]).then_inc(consts, 1)
                    link = Links(pool, pool_front, 17)
                    tt, ts = nc.gpsimd.tensor_tensor, nc.gpsimd.tensor_scalar
                    half = minus_half

                    def two_norms(m_v, r0, rs, eps_out):
                        var, e, t = m_v[:, :, 1], sm[:, 6, :], sm[:, 7, :]
                        link(ts(e, var, EPS_LN, None, op0=ALU.add))
                        link(tt(r0, e, half[:, 0:NT], ALU.pow))
                        link(tt(t, var, r0, ALU.mult))
                        link(tt(e, t, r0, ALU.mult))
                        alone(pool, passed)
                        link(ts(t, e, eps_out, None, op0=ALU.add))
                        link(tt(e, t, half[:, 0:NT], ALU.pow))
                        tt(rs, e, r0, ALU.mult).then_inc(scales, 1)

                    def front(b):
                        link.batch(b)
                        pool.wait_ge(stats, b * 3 + 1)
                        alone(pool, passed)
                        two_norms(mv, sm[:, 0, :], sm[:, 1, :], EPS_LN)
                        pool.wait_ge(z_ready, b * 2 + 1)
                        for i in range(NT):
                            last = tt(u[:, i, :], u[:, i, :], out_b[:], ALU.add)
                        last.then_inc(ub_ready, 1)
                        pool.wait_ge(silu_done, b + 1)
                        for c in range(IC):
                            last = tt(sz[:, c, :], sz[:, c, :], xc[:, c, :], ALU.mult)
                        last.then_inc(p_ready, 1)
                        pool.wait_ge(stats, b * 3 + 2)
                        alone(pool, passed)
                        link(ts(sm[:, 6, :], mvf[:, :, 1], EPS_LN, None, op0=ALU.add))
                        tt(sm[:, 2, :], sm[:, 6, :], half[:, 0:NT], ALU.pow).then_inc(scales, 1)
                        pool.wait_ge(stats, b * 3 + 3)
                        alone(pool, passed)
                        two_norms(mv1, sm[:, 3, :], sm[:, 4, :], EPS_RMS)
                        for i in range(NT):
                            pool.wait_ge(sq_summed, b * NT + i + 2)
                            alone(pool, passed)
                            link(ts(ssc[:, i, :], ss[:, i, :], 1.0 / HD, EPS_RMS, op0=ALU.mult, op1=ALU.add))
                            tt(rqk[:, i, :], ssc[:, i, :], half[:, 0:32], ALU.pow).then_inc(qk_scale, 1)

                    front(0)
                    with pool.Fori(0, B - 1) as a:
                        front(a + 1)

                @block.scalar
                def _(act):
                    activation, copy = nc.scalar.activation, ACT.Copy
                    for s in fb.moved + ob.moved:
                        act.sem_inc(s, 1)
                    act.sem_inc(exp_done, 2)
                    act.wait_ge(w_loaded, 16 * 7)
                    activation(win_h[:], win_f, copy)
                    activation(wqkv_h[:], wqkv_f, copy).then_inc(w_hi, 1)
                    act.wait_ge(w_ready, 1)

                    def move_hi(b, n, dst, w, ready):
                        t = fb.wait_full(act, b, n)
                        activation(dst, t[:], copy, scale=w).then_inc(ready, 1)

                    def in_proj(b, m):
                        t = fb.wait_full(act, b, F_IN + m)
                        dst = xi[:, m, 3:] if m < IC else sz[:, m - IC, :]
                        fb.now_moved(activation(dst, t[:], ACT.Identity, bias=b_in[:, m:m + 1]), F_IN + m)

                    def silus(b):
                        act.wait_ge(conv_done, b + 1)
                        fb.wait_moved(act, b, F_IN + 2 * IC - 1)
                        fb.wait_moved(act, b, F_IN + 2 * IC - 2)
                        fb.wait_moved(act, b, F_IN + 2 * IC - 3)
                        activation(sz[:], sz[:], ACT.Silu)
                        activation(xc[:], xc[:], ACT.Silu).then_inc(silu_done, 1)

                    def gate(b):
                        t = fb.wait_full(act, b, F_GATE)
                        fb.now_moved(activation(th[:], t[:], ACT.Tanh, scale=0.5), F_GATE)

                    def squares(b, i):
                        t = fb.wait_full(act, b, F_QK + i)
                        act.wait_ge(sq_summed, b * NT + i + 1)
                        activation(sq[:], t[:], ACT.Square).then_inc(sq_ready, 1)

                    def qk_transposed(b, c):
                        if c == 0 and not (isinstance(b, int) and b == 0):
                            for s in stacked:
                                act.wait_ge(s, b * (NPAIR // SLOTS * 8 * 16))
                        move_hi(b, F_QT + c, qT_h[:, c, :], at["qn_w"] if c < 2 else at["kn_w"], qT_hi)

                    def values(b):
                        for i in range(NT):
                            t = fb.wait_full(act, b, F_V + i)
                            ins = activation(v[:, i, :, 0:HD], t[:, 0:D].rearrange("p (h d) -> p h d", d=HD), copy)
                            fb.now_moved(ins, F_V + i)

                    def minus_max(b, pair):
                        t = ob.wait_full(act, b, O[f"mt{pair}"])
                        if pair >= 2:
                            act.wait_ge(rows[pair % 2], b * (NPAIR * 16) + (pair // 2) * 32)
                        activation(nm_h[:, pair % 2, :], t[0:8, 0:P], copy, scale=-1.0).then_inc(nm_hi, 1)

                    def exps(b, pair, n):
                        k = pair * UNITS + n
                        act.wait_ge(st_full, b * PU + k + 1)
                        activation(pt[:, k % PTS, :], st_bank[k % 2][:], ACT.Exp).then_inc(exp_done, 1)

                    def o_move(b, name, dst):
                        t = ob.wait_full(act, b, O[name])
                        ob.now_moved(activation(dst, t[:], copy), O[name])

                    def turn(a, f):
                        att, front = a is not None, f is not None
                        if front:
                            for c in range(KC):
                                move_hi(f, F_ZT + c, zT_h[:, c, :], at["norm_w"][:, c:c + 1], hi_ready)
                        if att:
                            minus_max(a, 0)
                        for p in range(NPAIR):
                            for n in range(UNITS):
                                if att:
                                    exps(a, p, n)
                                    if n == 1 and p + 1 < NPAIR:
                                        minus_max(a, p + 1)
                                if front:
                                    if p < 2 and n < 4:
                                        in_proj(f, p * 4 + n)
                                    if p == 3 and n == 0:
                                        silus(f)
                                    if p == 3 and n == 4:
                                        gate(f)
                                    if p == 6 and n in (1, 2):
                                        move_hi(f, F_HT + n - 1, zT_h[:, n - 1, :], at["n1_w"][:, n - 1:n], hi_ready)
                                    if p == 7 and n < 4:
                                        squares(f, n)
                            if att and p in (2, 4, 6):
                                o_move(a, f"pv{p // 2 - 1}", oTs[:])
                        if att:
                            o_move(a, "pv3", oTs[:])
                        if front:
                            for c in range(4):
                                qk_transposed(f, c)
                            values(f)
                        if att:
                            for c in range(KC):
                                o_move(a, f"t{c}", oT[:, c, :])

                    turn(None, 0)
                    with act.Fori(0, B - 1) as a:
                        turn(a, a + 1)
                    turn(B - 1, None)

                @block.vector
                def _(dve):
                    link, alink = Links(dve, dve_front, 7), Links(dve, dve_att, 4)
                    tt, ts, stt = nc.vector.tensor_tensor, nc.vector.tensor_scalar, nc.vector.scalar_tensor_tensor
                    dve.sem_inc(mx_read, 2)
                    dve.sem_inc(sq_summed, 1)
                    nc.vector.memset(qS[:].bitcast(F32), 0.0)
                    nc.vector.memset(kS[0:SR].bitcast(F32), 0.0)
                    nc.vector.memset(kS[SR:P].bitcast(F32), 1.0)
                    dve.wait_ge(w_loaded, 16 * 7)
                    ts(wout[:], wout[:], 0.5, None, op0=ALU.mult)
                    ts(d2[:], at["D"], 2.0, 1.0, op0=ALU.mult, op1=ALU.add)
                    ts(at["qn_w"], at["qn_w"], float(HD) ** -0.5, None, op0=ALU.mult)
                    nc.vector.tensor_reduce(gate_col[:], wc[:], AX.X, ALU.add).then_inc(dve_pre, 1)
                    dve.wait_ge(dve_pre, 1)
                    for c in range(IC):
                        ts(wgate[:, c, :], gate_col[:, c:c + 1].to_broadcast([P, P]), 1.0 / HD, None, op0=ALU.mult)
                    dve.wait_ge(w_hi, 1)
                    tt(win_l[:], win_f, win_h[:].bitcast(F32), ALU.subtract)
                    tt(wqkv_l[:], wqkv_f, wqkv_h[:].bitcast(F32), ALU.subtract)
                    dve.wait_ge(bias_mm, 1)
                    tt(b_in[:], mx_bank[0][:, 0:2 * IC], at["in_b"], ALU.add).then_inc(w_ready, 1)

                    def normed(dst, src, m_v, scale):
                        for i in range(NT):
                            last = ts(dst[:, i, :], src[:, i, :], m_v[:, i, 0:1], sm[:, scale, i:i + 1],
                                      op0=ALU.subtract, op1=ALU.mult)
                        return last

                    def row_stats(src, m_v):
                        for i in range(NT):
                            last = nc.vector.bn_stats(st6[:, i, :], src[:, i, :])
                        link(last)
                        alone(dve, passed)
                        for i in range(NT):
                            last = nc.vector.bn_aggr(m_v[:, i, :], st6[:, i, :])
                        last.then_inc(stats, 1)

                    def norm_in(b):
                        dve.wait_ge(x_loaded, 16 * (b + 1))
                        row_stats(x, mv)

                    def u_and_z(b):
                        dve.wait_ge(scales, b * 3 + 1)
                        normed(u, x, mv, 0)
                        normed(z, x, mv, 1).then_inc(z_ready, 1)

                    def move_lo(b, n, dst, hi, w, ready, count):
                        t = fb.wait_full(dve, b, n)
                        dve.wait_ge(ready, count)
                        fb.now_moved(stt(dst, t[:], w, hi.bitcast(F32), ALU.mult, ALU.subtract), n)

                    def conv(b, j):
                        for m in range(IC):
                            if j == 0:
                                fb.wait_moved(dve, b, F_IN + m)
                            w = at["conv_w"][:, 4 * m + j:4 * m + j + 1]
                            if j == 0:
                                last = ts(xc[:, m, :], xi[:, m, 0:T], w, at["conv_b"][:, m:m + 1], op0=ALU.mult, op1=ALU.add)
                            else:
                                last = stt(xc[:, m, :], xi[:, m, j:j + T], w, xc[:, m, :], ALU.mult, ALU.add)
                        if j < 3:
                            link(last)
                        else:
                            last.then_inc(conv_done, 1)

                    def y(b):
                        fb.wait_moved(dve, b, F_GATE)
                        dve.wait_ge(p_ready, b + 1)
                        for c in range(IC):
                            last = stt(sz[:, c, :], th[:], d2[:, c:c + 1], sz[:, c, :], ALU.add, ALU.mult)
                        last.then_inc(y_ready, 1)

                    def mixer_out(b):
                        dve.wait_ge(ub_ready, b + 1)
                        for k in range(2):
                            t = fb.wait_full(dve, b, F_OUT + k)
                            fb.now_moved(tt(z[:, 2 * k:2 * k + 2, :], t[:].rearrange("p (i d) -> p i d", d=D),
                                            u[:, 2 * k:2 * k + 2, :], ALU.add), F_OUT + k)
                        fb.wait_moved(dve, b, F_OUT)
                        fb.wait_moved(dve, b, F_OUT + 1)
                        row_stats(z, mvf)

                    def make_x1(b):
                        dve.wait_ge(scales, b * 3 + 2)
                        link(normed(z, z, mvf, 2))
                        tt(x[:], x[:], z[:], ALU.add).then_inc(x1_ready, 1)
                        dve.wait_ge(x1_ready, b + 1)
                        row_stats(x, mv1)

                    def make_h(b):
                        dve.wait_ge(scales, b * 3 + 3)
                        normed(z, x, mv1, 4).then_inc(z_ready, 1)

                    def sum_squares(b, i):
                        dve.wait_ge(sq_ready, b * NT + i + 1)
                        nc.vector.tensor_reduce(ss[:, i, :], sq[:].rearrange("p (h d) -> p h d", d=HD), AX.X,
                                                ALU.add).then_inc(sq_summed, 1)

                    def scale_qk(b, i):
                        dve.wait_ge(qk_scale, b * NT + i + 1)
                        t = fb.wait_full(dve, b, F_QK + i)
                        fb.now_moved(tt(qkn[:, i, :].rearrange("p (h d) -> p h d", d=HD),
                                        t[:].rearrange("p (h d) -> p h d", d=HD),
                                        rqk[:, i, :].unsqueeze(2).to_broadcast([P, 32, HD]), ALU.mult), F_QK + i)

                    def make_xin(b):
                        if not (isinstance(b, int) and b == 0):
                            dve.wait_ge(xr_stored, b * 16)
                        normed(xin, x, mv1, 3).then_inc(xin_ready, 1)

                    def maxima(b, pair, n):
                        k = pair * UNITS + n
                        dve.wait_ge(mx_full, b * PU + k + 1)
                        t, m = mx_bank[k % 2], mxs[:, pair % 2, :]
                        if n == 4:
                            last = nc.vector.tensor_reduce(m.rearrange("p (h i) -> p h i", h=2)[:, :, 1],
                                                           t[:].rearrange("p (h c) -> p h c", h=2), AX.X, ALU.max)
                        else:
                            for h, i, c, w in MAX_UNITS[n]:
                                last = nc.vector.tensor_reduce(m[:, h * 4 + i:h * 4 + i + 1], t[:, c:c + w], AX.X, ALU.max)
                        last.then_inc(mx_read, 1)

                    def minus_max_lo(b, pair):
                        t = ob.wait_full(dve, b, O[f"mt{pair}"])
                        dve.wait_ge(nm_hi, b * NPAIR + pair + 1)
                        ob.now_moved(stt(nm_l[:, pair % 2, :], t[0:8, 0:P], -1.0, nm_h[:, pair % 2, :].bitcast(F32),
                                         ALU.mult, ALU.subtract), O[f"mt{pair}"])

                    def o_norm(b, g):
                        t = ob.wait_full(dve, b, O[f"ot{g}"])[:].rearrange("p (i q e) -> p i q e", q=4, e=32)
                        alink(nc.vector.reciprocal(rc[:], t[:, :, :, HD]))
                        for e in range(2):
                            pair = 2 * g + e
                            dst = otok[:].rearrange("p i (h f) -> p i h f", h=2)[:, :, :, HD * pair:HD * (pair + 1)]
                            last = tt(dst, t[:, :, 2 * e:2 * e + 2, 0:HD],
                                      rc[:, :, 2 * e:2 * e + 2].unsqueeze(3).to_broadcast([P, NT, 2, HD]), ALU.mult)
                        ob.now_moved(last, O[f"ot{g}"])

                    def wo_add(b, k):
                        t = ob.wait_full(dve, b, O[f"wo{k}"])
                        dst = xin[:, 2 * k:2 * k + 2, ZM:]
                        ob.now_moved(tt(dst, t[:, 0:2 * DO].rearrange("p (i d) -> p i d", d=DO), dst, ALU.add), O[f"wo{k}"])

                    def turn(a, f):
                        att, front = a is not None, f is not None
                        if att:
                            alink.batch(a)
                        if front:
                            link.batch(f)
                            norm_in(f)
                        if att:
                            for n in range(UNITS):
                                maxima(a, 0, n)
                        if front:
                            u_and_z(f)
                        if att:
                            for n in range(UNITS):
                                maxima(a, 1, n)
                        if front:
                            for c in range(KC):
                                move_lo(f, F_ZT + c, zT_l[:, c, :], zT_h[:, c, :], at["norm_w"][:, c:c + 1],
                                        hi_ready, f * 4 + c + 1)
                        if att:
                            minus_max_lo(a, 0)
                        for p in range(NPAIR):
                            for n in range(UNITS):
                                if att and p + 2 < NPAIR:
                                    maxima(a, p + 2, n)
                                if att and n == 1 and p + 1 < NPAIR:
                                    minus_max_lo(a, p + 1)
                                if front:
                                    if p == 1 and n < 4:
                                        conv(f, n)
                                    if p == 5 and n == 2:
                                        make_x1(f)
                                    if p == 6 and n in (1, 2):
                                        move_lo(f, F_HT + n - 1, zT_l[:, n - 1, :], zT_h[:, n - 1, :],
                                                at["n1_w"][:, n - 1:n], hi_ready, f * 4 + 2 + n)
                                    if p == 7 and n < 4:
                                        sum_squares(f, n)
                                        if n > 0:
                                            scale_qk(f, n - 1)
                            if front:
                                if p == 3:
                                    y(f)
                                if p == 4:
                                    mixer_out(f)
                                if p == 5:
                                    make_h(f)
                                if p == 7:
                                    scale_qk(f, 3)
                            if att and p in (3, 5, 7):
                                o_norm(a, p // 2 - 1)
                        if att:
                            o_norm(a, 3)
                        if front:
                            for c in range(4):
                                w = at["qn_w"] if c < 2 else at["kn_w"]
                                move_lo(f, F_QT + c, qT_l[:, c, :], qT_h[:, c, :], w, qT_hi, f * 4 + c + 1)
                        if att:
                            wo_add(a, 0)
                            wo_add(a, 1)
                        if front:
                            make_xin(f)

                    turn(None, 0)
                    with dve.Fori(0, B - 1) as a:
                        turn(a, a + 1)
                    turn(B - 1, None)

                @block.tensor
                def _(pe):
                    mm = nc.tensor.matmul

                    def split(out_ap, stat, mov, more_before=False):
                        for c in range(KC):
                            (sh, sl), (mh, ml) = stat(c), mov(c)
                            for s, m in ((sh, mh), (sh, ml), (sl, mh)):
                                last = mm(out_ap, s, m, start=(c == 0 and s is sh and m is mh), stop=(c == KC - 1 and s is sl))
                        return last

                    def transposes(bank, sources):
                        for i, src in enumerate(sources):
                            last = nc.tensor.transpose(bank[:, i * P:(i + 1) * P], src, ident[:])
                        return last

                    pe.wait_ge(w_loaded, 16 * 7)
                    pe.wait_ge(consts, 1)
                    for m in range(2 * IC):
                        for c in range(KC):
                            last = mm(mx_bank[0][:, m:m + 1], win_f[:, c, m * P:(m + 1) * P], at["norm_b"][:, c:c + 1],
                                      start=(c == 0), stop=(c == KC - 1))
                    last.then_inc(bias_mm, 1)
                    pe.wait_ge(w_ready, 1)

                    def z_transposes(b, first_use, z_count):
                        pe.wait_ge(z_ready, z_count)
                        for c in range(KC):
                            t = fb.wait_free(pe, b, first_use + c)
                            fb.now_full(transposes(t, [z[:, i, c * P:(c + 1) * P] for i in range(NT)]), first_use + c)

                    def in_proj(b, m):
                        if m == 0:
                            for c in range(KC):
                                fb.wait_moved(pe, b, F_ZT + c)
                        t = fb.wait_free(pe, b, F_IN + m)
                        cols = slice(m * P, (m + 1) * P)
                        fb.now_full(split(t[:], lambda c: (win_h[:, c, cols], win_l[:, c, cols]),
                                          lambda c: (zT_h[:, c, :], zT_l[:, c, :])), F_IN + m)

                    def gate(b):
                        pe.wait_ge(silu_done, b + 1)
                        t = fb.wait_free(pe, b, F_GATE)
                        for c in range(IC):
                            last = mm(t[:], wgate[:, c, :], xc[:, c, :], start=(c == 0), stop=(c == IC - 1))
                        fb.now_full(last, F_GATE)

                    def out_proj(b, k):
                        pe.wait_ge(y_ready, b + 1)
                        t = fb.wait_free(pe, b, F_OUT + k)
                        for i in range(2):
                            tok = slice((2 * k + i) * P, (2 * k + i + 1) * P)
                            for c in range(IC):
                                last = mm(t[:, i * D:(i + 1) * D], sz[:, c, tok], wout[:, c, :], start=(c == 0), stop=(c == IC - 1))
                        fb.now_full(last, F_OUT + k)

                    def qkv(b, use, i, cols):
                        t = fb.wait_free(pe, b, use)
                        tok = slice(i * P, (i + 1) * P)
                        n = cols.stop - cols.start
                        fb.now_full(split(t[:, 0:n], lambda c: (zT_h[:, c, tok], zT_l[:, c, tok]),
                                          lambda c: (wqkv_h[:, c, cols], wqkv_l[:, c, cols])), use)

                    def qk(b, i):
                        if i == 0:
                            for c in range(KC):
                                fb.wait_moved(pe, b, F_HT + c)
                        qkv(b, F_QK + i, i, slice(0, 2 * D))

                    def qk_transposes(b):
                        for i in range(NT):
                            fb.wait_moved(pe, b, F_QK + i)
                        for c in range(4):
                            t = fb.wait_free(pe, b, F_QT + c)
                            fb.now_full(transposes(t, [qkn[:, i, c * P:(c + 1) * P] for i in range(NT)]), F_QT + c)

                    def scores_for_max(b, pair, n):
                        s, k = pair % SLOTS, pair * UNITS + n
                        if n == 0:
                            pe.wait_ge(stacked[s], b * (NPAIR // SLOTS * 128) + (pair // SLOTS + 1) * 128)
                        pe.wait_ge(mx_read, b * PU + k + 1)
                        t = mx_bank[k % 2]
                        for h, i, c, w in MAX_UNITS[n]:
                            mm(t[:, c:c + w], qS[0:SR, s, h, i * P:(i + 1) * P], kS[0:SR, s, h, 0:w], start=True, stop=False)
                            last = mm(t[:, c + i * P:c + w], ident16[:], mask_q[:], start=False, stop=True)
                        last.then_inc(mx_full, 1)

                    def max_transposed(b, pair):
                        pe.wait_ge(mx_read, b * PU + (pair + 1) * UNITS + 2)
                        t = ob.wait_free(pe, b, O[f"mt{pair}"])
                        ob.now_full(nc.tensor.transpose(t[0:8, 0:P], mxs[:, pair % 2, :], ident[:]), O[f"mt{pair}"])

                    def scores(b, pair, n):
                        s, k = pair % SLOTS, pair * UNITS + n
                        if n == 0:
                            pe.wait_ge(rows[pair % 2], b * (NPAIR * 16) + (pair // 2 + 1) * 32)
                        pe.wait_ge(exp_done, b * PU + k + 1)
                        t = st_bank[k % 2]
                        for h, j, c, w in ST_UNITS[n]:
                            mm(t[:, c:c + w], kS[0:SR + 2, s, h, j * P:(j + 1) * P], qS[0:SR + 2, s, h, j * P:T], start=True, stop=False)
                            last = mm(t[:, c:c + P], ident16[:], mask_k[:], start=False, stop=True)
                        last.then_inc(st_full, 1)

                    def values_summed(b, g):
                        pe.wait_ge(exp_done, b * PU + (2 * g + 2) * UNITS + 2)
                        if g == 0:
                            for i in range(NT):
                                fb.wait_moved(pe, b, F_V + i)
                        t = ob.wait_free(pe, b, O[f"pv{g}"])
                        for j in range(NT):
                            for q in range(4):
                                pair, h = 2 * g + q // 2, q % 2
                                n, c, w = pt_at[h, j]
                                last = mm(t[32 * q:32 * (q + 1), j * P:T], v[:, j, h * CH + pair, :],
                                          pt[:, (pair * UNITS + n) % PTS, c:c + w], start=(j == 0), stop=(j == NT - 1))
                        ob.now_full(last, O[f"pv{g}"])

                    def o_back(b, g):
                        ob.wait_moved(pe, b, O[f"pv{g}"])
                        t = ob.wait_free(pe, b, O[f"ot{g}"])
                        ob.now_full(transposes(t, [oTs[:, i * P:(i + 1) * P] for i in range(NT)]), O[f"ot{g}"])

                    def o_proj(b):
                        for c in range(KC):
                            t = ob.wait_free(pe, b, O[f"t{c}"])
                            ob.now_full(transposes(t, [otok[:, i, c * P:(c + 1) * P] for i in range(NT)]), O[f"t{c}"])
                        for k in range(2):
                            t = ob.wait_free(pe, b, O[f"wo{k}"])
                            for i in range(2):
                                tok = slice((2 * k + i) * P, (2 * k + i + 1) * P)
                                for c in range(KC):
                                    last = mm(t[:, i * DO:(i + 1) * DO], oT[:, c, tok], wo[:, c, :], start=(c == 0), stop=(c == KC - 1))
                            ob.now_full(last, O[f"wo{k}"])

                    def turn(a, f):
                        att, front = a is not None, f is not None
                        if att:
                            for pair in range(2):
                                for n in range(UNITS):
                                    scores_for_max(a, pair, n)
                        if front:
                            z_transposes(f, F_ZT, f * 2 + 1)
                        if att:
                            max_transposed(a, 0)
                        for p in range(NPAIR):
                            for n in range(UNITS):
                                if att:
                                    scores(a, p, n)
                                    if p + 2 < NPAIR:
                                        scores_for_max(a, p + 2, n)
                                    if n == 1 and p + 1 < NPAIR:
                                        max_transposed(a, p + 1)
                                if front:
                                    if p < 2 and n < 4:
                                        in_proj(f, p * 4 + n)
                                    if p == 3 and n == 4:
                                        gate(f)
                                    if p == 4 and n in (3, 4):
                                        out_proj(f, n - 3)
                                    if p == 6 and n == 1:
                                        z_transposes(f, F_HT, f * 2 + 2)
                                    if p == 7 and n < 4:
                                        qk(f, n)
                            if att and p in (2, 4, 6):
                                values_summed(a, p // 2 - 1)
                            if att and p in (3, 5, 7):
                                o_back(a, p // 2 - 1)
                        if att:
                            values_summed(a, 3)
                            o_back(a, 3)
                        if front:
                            qk_transposes(f)
                            for i in range(NT):
                                qkv(f, F_V + i, i, slice(2 * D, 3 * D))
                        if att:
                            o_proj(a)

                    turn(None, 0)
                    with pe.Fori(0, B - 1) as a:
                        turn(a, a + 1)
                    turn(B - 1, None)

        experts(nc, ctx, d, banks, x1_dram, xr_dram, out_dram)


def experts(nc, ctx, d, banks, x1_dram, xr_dram, out_dram):
    B, _, NT, D = out_dram.shape
    T = NT * P
    KC = D // P
    HC = d["e0_down"].shape[1]
    DO = d["e0_down"].shape[2]
    ZM = D - DO
    E = 4
    LARGEST = 3.4028234663852886e38

    def sb(name, shape, dt=F32):
        return ctx.enter_context(nc.sbuf_tensor(name, shape, dt))

    def sem(name):
        return ctx.enter_context(nc.semaphore(name))

    UPS = ["e2_l1", "e0_up", "e2_l2", "e3_down", "e1_w1", "e1_w2", "e2_l3", "e3_up"]
    DOWNS = ["e0_down", "e1_down", "e2_l4", "e3_out"]
    up_h = {n: sb(n + "_h", [P, *d[n].shape[1:]], F32R) for n in UPS}
    up_l = {n: sb(n + "_l", [P, *d[n].shape[1:]], F32R) for n in UPS}
    down = {n: sb(n + "_sb", [P, HC, DO]) for n in DOWNS}
    gate_w = sb("gate_w_sb", [P, KC, E])
    n2_w = sb("n2_w_sb", [P, KC])
    ident = sb("ident2", [P, P])
    minus_half = sb("minus_half2", [P, NT])

    WORK = 4 * HC * T + 5 * T
    work = sb("work", [P, max(WORK, sum(d[n].shape[1] * d[n].shape[2] for n in UPS))])
    hid = [work[:, e * HC * T:(e + 1) * HC * T].rearrange("p (c t) -> p c t", t=T) for e in range(4)]
    gates = work[:, 4 * HC * T:4 * HC * T + 2 * T].rearrange("p (s t) -> p s t", t=T)
    exact = work[:, 4 * HC * T + 2 * T:4 * HC * T + 5 * T].rearrange("p (s t) -> p s t", t=T)
    stage, at = {}, 0
    for n in UPS:
        size = d[n].shape[1] * d[n].shape[2]
        stage[n] = work[:, at:at + size].rearrange("p (k n) -> p k n", k=d[n].shape[1])
        at += size
    h1 = sb("h1_h", [P, HC, T], F32R), sb("h1_l", [P, HC, T], F32R)
    h2 = sb("h2_h", [P, HC, T], F32R), sb("h2_l", [P, HC, T], F32R)
    h3 = sb("h3_h", [P, KC, T], F32R), sb("h3_l", [P, KC, T], F32R)
    xf = sb("xf_h", [P, KC, T], F32R), sb("xf_l", [P, KC, T], F32R)
    xr = sb("xr_sb", [P, 2, NT, D])
    x1 = sb("x1_sb", [P, 2, NT, D])
    xz = sb("xz", [P, NT, D])
    ssx, e1, r2, rf, ef = (sb(n, [P, NT]) for n in ("ssx", "e_rms", "r_rms", "r_f", "e_f"))
    st6, mvf = sb("st6_f", [P, NT, 6]), sb("mv_f", [P, NT, 2])
    raw, lg, dl, ex, pr, wts = (sb(n, [P, NT, E]) for n in ("raw", "lg", "dl", "ex", "pr", "wts"))
    finite = sb("finite", [P, NT, E], U32)
    beats = sb("beats", [P, NT, E, E])
    rank = sb("rank", [P, NT, E])
    m1, s1, i1, s2, i2 = (sb(n, [P, NT]) for n in ("m1", "s1", "i1", "s2", "i2"))

    up_units = [("e2_l1", m, "xf", "split") for m in range(HC)] + [("e0_up", m, "xf", 0) for m in range(HC)]
    up_units += [("e2_l2", m, "h1", "split") for m in range(HC)] + [("e3_down", m, "xf", "split") for m in range(KC)]
    for m in range(HC):
        up_units += [("e1_w1", m, "xf", "silu"), ("e1_w2", m, "xf", "times")]
    up_units += [("e2_l3", m, "h2", 2) for m in range(HC)] + [("e3_up", m, "h3", 3) for m in range(HC)]
    moving = {"xf": xf, "h1": h1, "h2": h2, "h3": h3}
    split_into = {"e2_l1": h1, "e2_l2": h2, "e3_down": h3}
    UB = Banks(banks[0:4], [sem(f"up_full{i}") for i in range(4)], [sem(f"up_moved{i}") for i in range(4)],
               2 + len(up_units))
    DB = Banks(banks[4:7], [sem(f"down_full{i}") for i in range(3)], [sem(f"down_moved{i}") for i in range(3)], 9)
    down_order = [0, 1, 3, 2]
    D_USE = {(e, k): 1 + 2 * n + k for n, e in enumerate(down_order) for k in range(2)}

    w_in = [sem(f"w_in{i}") for i in range(len(UPS))]
    w2_loaded, consts2, w_hi2, w_lo2 = sem("w2_loaded"), sem("consts2"), sem("w_hi2"), sem("w_lo2")
    x_in = [sem("x_in0"), sem("x_in1")]
    sq_in, rms_scale, xz_ready, xf_hi = sem("sq_in"), sem("rms_scale"), sem("xz_ready"), sem("xf_hi")
    exact_ready, lo_ready = sem("exact_ready"), sem("lo_ready")
    shifted, ex_ready = sem("shifted"), sem("ex_ready")
    f_stats, f_scale, out_ready = sem("f_stats"), sem("f_scale"), sem("out_ready")
    stored = [sem("stored0"), sem("stored1")]
    dve2, pool_e1, pool_ef = sem("dve2"), sem("pool_e1"), sem("pool_ef")
    passed2 = sem("passed2")
    SPLITS = 2 * HC + KC

    def each_batch(eng, turn):
        with eng.Fori(0, B // 2 - 1) as k:
            turn(2 * k, 2 * k + 1, 0)
            turn(2 * k + 1, 2 * k + 2, 1)
        turn(B - 2, B - 1, 0)
        turn(B - 1, None, 1)

    with nc.Block() as block:

        @block.sync
        def _(sp):
            for n, s in zip(UPS, w_in):
                sp.dma_start(stage[n], d[n]).then_inc(s, 16)
            for dst, src in [(down[n][:], d[n]) for n in DOWNS] + [(gate_w[:], d["gate_w"]), (n2_w[:], d["n2_w"])]:
                sp.dma_start(dst, src).then_inc(w2_loaded, 16)

            def load(b, par):
                sp.dma_start(xr[:, par, :, :], of_batch(xr_dram, b)).then_inc(x_in[par], 16)
                sp.dma_start(x1[:, par, :, :], of_batch(x1_dram, b)).then_inc(x_in[par], 16)

            load(0, 0)
            load(1, 1)
            with sp.Fori(0, B // 2 - 1) as k:
                for par in range(2):
                    b = 2 * k + par
                    sp.wait_ge(out_ready, b + 1)
                    alone(sp, passed2)
                    sp.dma_start(of_batch(out_dram, b), x1[:, par, :, :]).then_inc(stored[par], 16)
                    sp.wait_ge(stored[par], 16 * k + 16)
                    alone(sp, passed2)
                    load(b + 2, par)
            for par in range(2):
                sp.wait_ge(out_ready, B - 2 + par + 1)
                sp.dma_start(of_batch(out_dram, B - 2 + par), x1[:, par, :, :]).then_inc(stored[par], 16)
            for par in range(2):
                sp.wait_ge(stored[par], 16 * (B // 2))

        def wait_loaded(eng, b, par):
            eng.wait_ge(x_in[par], 16 * b - 16 * par + 32)

        @block.gpsimd
        def _(pool):
            nc.gpsimd.memset(ident[:], 0.0)
            nc.gpsimd.memset(minus_half[:], -0.5)
            nc.gpsimd.memset(beats[:], 0.0).then_inc(consts2, 1)
            pool.wait_ge(consts2, 1)
            nc.gpsimd.affine_select(out=ident[:], in_=ident[:], compare_op=ALU.not_equal, fill=1.0,
                                    base=0, pattern=[[-1, P]], channel_multiplier=1).then_inc(consts2, 1)
            tt, ts = nc.gpsimd.tensor_tensor, nc.gpsimd.tensor_scalar

            def head(b):
                pool.wait_ge(sq_in, b + 1)
                alone(pool, passed2)
                ts(e1[:], ssx[:], 1.0 / D, EPS_RMS, op0=ALU.mult, op1=ALU.add).then_inc(pool_e1, 1)
                pool.wait_ge(pool_e1, b + 1)
                tt(r2[:], e1[:], minus_half[:], ALU.pow).then_inc(rms_scale, 1)

            def turn(b, nxt, par):
                if nxt is not None:
                    head(nxt)
                pool.wait_ge(f_stats, b + 1)
                alone(pool, passed2)
                ts(ef[:], mvf[:, :, 1], EPS_LN, None, op0=ALU.add).then_inc(pool_ef, 1)
                pool.wait_ge(pool_ef, b + 1)
                tt(rf[:], ef[:], minus_half[:], ALU.pow).then_inc(f_scale, 1)

            head(0)
            each_batch(pool, turn)

        @block.scalar
        def _(act):
            activation, copy = nc.scalar.activation, ACT.Copy
            for s in UB.moved + DB.moved:
                act.sem_inc(s, 1)

            def head(b, par):
                wait_loaded(act, b, par)
                for i in range(NT):
                    ins = activation(xz[:, i, :], xr[:, par, i, :], ACT.Square, accum_out=ssx[:, i:i + 1])
                ins.then_inc(sq_in, 1)

            def move_xf_hi(b):
                for c in range(KC):
                    t = UB.wait_full(act, b, c)
                    activation(xf[0][:, c, :], t[:], copy, scale=n2_w[:, c:c + 1]).then_inc(xf_hi, 1)

            def up(b, n, count):
                name, m, _, kind = up_units[n]
                t = UB.wait_full(act, b, 2 + n)
                if kind == "split":
                    k = count["split"]
                    count["split"] += 1
                    act.wait_ge(lo_ready, b * SPLITS + k + 1)
                    activation(exact[:, k % 2, :], t[:], ACT.Gelu).then_inc(exact_ready, 1)
                    UB.now_moved(activation(split_into[name][0][:, m, :], t[:], ACT.Gelu), 2 + n)
                elif kind == "silu":
                    if m >= 2:
                        UB.wait_moved(act, b, 2 + n - 3)
                    UB.now_moved(activation(gates[:, m % 2, :], t[:], ACT.Silu), 2 + n)
                elif kind != "times":
                    UB.now_moved(activation(hid[kind][:, m, :], t[:], ACT.Gelu), 2 + n)

            def turn(b, nxt, par):
                count = {"split": 0}
                for n in range(3 * HC + KC):
                    up(b, n, count)
                act.wait_ge(shifted, b + 1)
                activation(ex[:], dl[:], ACT.Exp).then_inc(ex_ready, 1)
                if nxt is not None:
                    head(nxt, 1 - par)
                for n in range(3 * HC + KC, len(up_units)):
                    up(b, n, count)
                if nxt is not None:
                    move_xf_hi(nxt)

            for n, s in zip(UPS, w_in):
                act.wait_ge(s, 16)
                activation(up_h[n][:], stage[n], copy).then_inc(w_hi2, 1)
            act.wait_ge(w2_loaded, 16 * (len(DOWNS) + 2))
            act.wait_ge(w_lo2, len(UPS))
            head(0, 0)
            move_xf_hi(0)
            each_batch(act, turn)

        @block.vector
        def _(dve):
            tt, ts, stt = nc.vector.tensor_tensor, nc.vector.tensor_scalar, nc.vector.scalar_tensor_tensor
            reduce = nc.vector.tensor_reduce
            link = Links(dve, dve2, 16)
            dve.sem_inc(lo_ready, 2)

            def head(b, par):
                dve.wait_ge(rms_scale, b + 1)
                wait_loaded(dve, b, par)
                for i in range(NT):
                    last = ts(xz[:, i, :], xr[:, par, i, :], r2[:, i:i + 1], None, op0=ALU.mult)
                last.then_inc(xz_ready, 1)

            def move_xf_lo(b):
                for c in range(KC):
                    t = UB.wait_full(dve, b, c)
                    dve.wait_ge(xf_hi, b * KC + c + 1)
                    UB.now_moved(stt(xf[1][:, c, :], t[:], n2_w[:, c:c + 1], xf[0][:, c, :].bitcast(F32),
                                     ALU.mult, ALU.subtract), c)

            def wide(a):
                return a.unsqueeze(2).to_broadcast([P, NT, E])

            def logits(b):
                t = DB.wait_full(dve, b, 0)
                nc.vector.memset(lg[:], 0.0)
                ins = nc.vector.tensor_copy(raw[:], t[:, 0:NT * E].rearrange("p (i e) -> p i e", e=E))
                DB.now_moved(ins, 0)
                DB.wait_moved(dve, b, 0)
                link(tt(finite[:], raw[:], raw[:], ALU.is_equal))
                alone(dve, passed2)
                link(nc.vector.copy_predicated(lg[:], finite[:], raw[:]))
                link(ts(lg[:], lg[:], LARGEST, -LARGEST, op0=ALU.min, op1=ALU.max))
                link(reduce(m1[:], lg[:], AX.X, ALU.max))
                tt(dl[:], lg[:], wide(m1[:]), ALU.subtract).then_inc(shifted, 1)

            def choose(b):
                dve.wait_ge(ex_ready, b + 1)
                link(reduce(s1[:], ex[:], AX.X, ALU.add))
                link(nc.vector.reciprocal(i1[:], s1[:]))
                link(tt(pr[:], ex[:], wide(i1[:]), ALU.mult))
                for e in range(E):
                    if e > 0:
                        last = tt(beats[:, :, e, 0:e], pr[:, :, 0:e], pr[:, :, e:e + 1].to_broadcast([P, NT, e]), ALU.is_ge)
                    if e < E - 1:
                        last = tt(beats[:, :, e, e + 1:], pr[:, :, e + 1:], pr[:, :, e:e + 1].to_broadcast([P, NT, E - 1 - e]), ALU.is_gt)
                link(last)
                link(reduce(rank[:], beats[:], AX.X, ALU.add))
                link(stt(wts[:], rank[:], 2.0, pr[:], ALU.is_lt, ALU.mult))
                link(reduce(s2[:], wts[:], AX.X, ALU.add))
                link(ts(s2[:], s2[:], 1e-8, None, op0=ALU.add))
                link(nc.vector.reciprocal(i2[:], s2[:]))
                link(tt(wts[:], wts[:], wide(i2[:]), ALU.mult))

            def up(b, n, count):
                name, m, _, kind = up_units[n]
                if kind == "split":
                    k = count["split"]
                    count["split"] += 1
                    dve.wait_ge(exact_ready, b * SPLITS + k + 1)
                    UB.wait_moved(dve, b, 2 + n)
                    tt(split_into[name][1][:, m, :], exact[:, k % 2, :], split_into[name][0][:, m, :].bitcast(F32),
                       ALU.subtract).then_inc(lo_ready, 1)
                elif kind == "times":
                    t = UB.wait_full(dve, b, 2 + n)
                    UB.wait_moved(dve, b, 1 + n)
                    UB.now_moved(tt(hid[1][:, m, :], t[:], gates[:, m % 2, :], ALU.mult), 2 + n)

            def combine(b, par):
                for n, e in enumerate(down_order):
                    for k in range(2):
                        t = DB.wait_full(dve, b, D_USE[e, k])
                        if n > 0:
                            DB.wait_moved(dve, b, D_USE[down_order[n - 1], k])
                        for i in range(2):
                            acc = xr[:, par, 2 * k + i, ZM:]
                            last = stt(acc, t[:, i * DO:(i + 1) * DO], wts[:, 2 * k + i, e:e + 1], acc, ALU.mult, ALU.add)
                        DB.now_moved(last, D_USE[e, k])

            def last_norm(b, par):
                for k in range(2):
                    DB.wait_moved(dve, b, D_USE[down_order[-1], k])
                for i in range(NT):
                    last = nc.vector.bn_stats(st6[:, i, :], xr[:, par, i, :])
                link(last)
                alone(dve, passed2)
                for i in range(NT):
                    last = nc.vector.bn_aggr(mvf[:, i, :], st6[:, i, :])
                last.then_inc(f_stats, 1)
                dve.wait_ge(f_scale, b + 1)
                for i in range(NT):
                    last = ts(xr[:, par, i, :], xr[:, par, i, :], mvf[:, i, 0:1], rf[:, i:i + 1], op0=ALU.subtract, op1=ALU.mult)
                link(last)
                tt(x1[:, par, :, :], x1[:, par, :, :], xr[:, par, :, :], ALU.add).then_inc(out_ready, 1)

            def turn(b, nxt, par):
                link.batch(b)
                count = {"split": 0}
                logits(b)
                for n in range(3 * HC + KC):
                    up(b, n, count)
                choose(b)
                if nxt is not None:
                    head(nxt, 1 - par)
                for n in range(3 * HC + KC, len(up_units)):
                    up(b, n, count)
                if nxt is not None:
                    move_xf_lo(nxt)
                combine(b, par)
                last_norm(b, par)

            dve.wait_ge(consts2, 2)
            for n, name in enumerate(UPS):
                dve.wait_ge(w_hi2, n + 1)
                tt(up_l[name][:], stage[name], up_h[name][:].bitcast(F32), ALU.subtract).then_inc(w_lo2, 1)
            head(0, 0)
            move_xf_lo(0)
            each_batch(dve, turn)

        @block.tensor
        def _(pe):
            mm = nc.tensor.matmul

            def xf_transposes(b):
                pe.wait_ge(xz_ready, b + 1)
                for c in range(KC):
                    t = UB.wait_free(pe, b, c)
                    for i in range(NT):
                        last = nc.tensor.transpose(t[:, i * P:(i + 1) * P], xz[:, i, c * P:(c + 1) * P], ident[:])
                    UB.now_full(last, c)

            def gate(b):
                for c in range(KC):
                    UB.wait_moved(pe, b, c)
                t = DB.wait_free(pe, b, 0)
                for i in range(NT):
                    for c in range(KC):
                        for s in range(2):
                            last = mm(t[:, i * E:(i + 1) * E], xf[s][:, c, i * P:(i + 1) * P].bitcast(F32), gate_w[:, c, :],
                                      start=(c == 0 and s == 0), stop=(c == KC - 1 and s == 1))
                DB.now_full(last, 0)

            def up(b, n):
                name, m, source, _ = up_units[n]
                if m == 0 and source == "h1":
                    pe.wait_ge(lo_ready, b * SPLITS + HC + 2)
                if m == 0 and source == "h2":
                    pe.wait_ge(lo_ready, b * SPLITS + 2 * HC + 2)
                if m == 0 and source == "h3":
                    pe.wait_ge(lo_ready, b * SPLITS + SPLITS + 2)
                t = UB.wait_free(pe, b, 2 + n)
                cols, chunks = slice(m * P, (m + 1) * P), d[name].shape[1]
                for c in range(chunks):
                    for j, (s, v) in enumerate(((0, 0), (0, 1), (1, 0))):
                        w = (up_h, up_l)[s][name][:, c, cols]
                        last = mm(t[:], w, moving[source][v][:, c, :], start=(c == 0 and j == 0), stop=(c == chunks - 1 and j == 2))
                UB.now_full(last, 2 + n)

            def downs(b, e):
                units = [n for n, u in enumerate(up_units) if u[3] == (e if e != 1 else "times")]
                for n in {(2 + n) % UB.n: n for n in units}.values():
                    UB.wait_moved(pe, b, 2 + n)
                w = down[DOWNS[e]]
                for k in range(2):
                    t = DB.wait_free(pe, b, D_USE[e, k])
                    for i in range(2):
                        tok = slice((2 * k + i) * P, (2 * k + i + 1) * P)
                        for c in range(HC):
                            last = mm(t[:, i * DO:(i + 1) * DO], hid[e][:, c, tok], w[:, c, :], start=(c == 0), stop=(c == HC - 1))
                    DB.now_full(last, D_USE[e, k])

            def turn(b, nxt, par):
                gate(b)
                for n in range(len(up_units)):
                    up(b, n)
                if nxt is not None:
                    xf_transposes(nxt)
                for e in down_order:
                    downs(b, e)

            pe.wait_ge(consts2, 2)
            pe.wait_ge(w2_loaded, 16 * (len(DOWNS) + 2))
            pe.wait_ge(w_lo2, len(UPS))
            xf_transposes(0)
            each_batch(pe, turn)


_FFN = ["e0_up", "e0_down", "e1_w1", "e1_w2", "e1_down", "e2_l1", "e2_l2", "e2_l3", "e2_l4", "e3_down", "e3_up", "e3_out"]


def kernel(**inputs):
    import numpy as np
    import concourse.bacc as bacc
    from concourse.bass_utils import run_bass_kernel_spmd

    a = {n[3:]: np.asarray(v) for n, v in inputs.items()}

    def by_partition(w):
        return np.ascontiguousarray(w.reshape(w.shape[0] // P, P, -1).transpose(1, 0, 2))

    def columns(v):
        return v.reshape(-1, P).T

    zm = 64
    conv = a["attn_conv_w"][:, 0, :].reshape(-1, P, 4).transpose(1, 0, 2).reshape(P, -1)
    arrays = {
        "x": np.ascontiguousarray(a["attn_x"]),
        "in_w": by_partition(a["attn_in_w"].T),
        "wqkv": by_partition(np.concatenate([a["ffn_wq"].T, a["ffn_wk"].T, a["ffn_wv"].T], axis=1)),
        "out_w": by_partition(a["attn_out_w"].T),
        "wo": by_partition(a["ffn_wo"].T[:, zm:]),
        "xproj_w": by_partition(a["attn_xproj_w"].T),
        "vecs": np.ascontiguousarray(np.concatenate([
            columns(a["attn_norm_w"]), columns(a["attn_norm_b"]), columns(a["attn_in_b"]), conv,
            columns(a["attn_conv_b"]), columns(a["attn_D"]), columns(a["ffn_n1_w"]),
            np.tile(a["ffn_qn_w"], 8)[:, None], np.tile(a["ffn_kn_w"], 8)[:, None]], axis=1)),
        "out_b": np.ascontiguousarray(np.broadcast_to(a["attn_out_b"], (P, a["attn_out_b"].shape[0]))),
        "gate_w": by_partition(a["ffn_gate_w"].T),
        "n2_w": np.ascontiguousarray(columns(a["ffn_n2_w"])),
    }
    for n in _FFN:
        w = a["ffn_" + n].T
        arrays[n] = by_partition(w[:, zm:] if n in ("e0_down", "e1_down", "e2_l4", "e3_out") else w)

    nc = bacc.Bacc("TRN2", target_bir_lowering=False, num_devices=1)
    d = {n: nc.dram_tensor("in_" + n, v.shape, F32, kind="ExternalInput").ap() for n, v in arrays.items()}
    shape = arrays["x"].shape
    scratch = [nc.dram_tensor(n, shape, F32, kind="Internal").ap() for n in ("x1_dram", "xr_dram")]
    out = nc.dram_tensor("out", shape, F32, kind="ExternalOutput").ap()
    mixer_attention_experts(nc, d, scratch, out)
    r = run_bass_kernel_spmd(nc, [{"in_" + n: v for n, v in arrays.items()}], core_ids=[0])
    return r.results[0]["out"]
```

```python
from contextlib import ExitStack

import concourse.bass as bass
from concourse import mybir

F32 = mybir.dt.float32
F32R = mybir.dt.float32r
BF16 = mybir.dt.bfloat16
U32 = mybir.dt.uint32
I32 = mybir.dt.int32
ACT = mybir.ActivationFunctionType
ALU = mybir.AluOpType
AX = mybir.AxisListType

P = 128
EPS_LN = 1e-5
EPS_RMS = 1.1920929e-07
MASKED = -1e30


class Links:

    def __init__(self, eng, sem, per):
        self.eng, self.sem, self.per, self.base, self.k = eng, sem, per, 0, 0

    def batch(self, b):
        assert self.k in (0, self.per), (self.k, self.per)
        self.base, self.k = b * self.per, 0

    def __call__(self, ins):
        self.k += 1
        ins.then_inc(self.sem, 1)
        self.eng.wait_ge(self.sem, self.base + self.k)


class Banks:

    def __init__(self, tiles, full, moved, uses):
        self.tiles, self.full, self.moved = tiles, full, moved
        self.n = len(tiles)
        self.order = {} if isinstance(uses, int) else {name: n for n, name in enumerate(uses)}
        self.uses = len(self.order) or uses
        assert self.uses % self.n == 0
        self.per = self.uses // self.n
        self.turn, self.next = None, None

    def at(self, use):
        n = self.order.get(use, use)
        return n % self.n, n // self.n

    def tile(self, use):
        return self.tiles[self.at(use)[0]]

    def wait_free(self, eng, b, use):
        if self.next is not None:
            self.pass_over(eng, self.order[use])
            self.next += 1
        i, k = self.at(use)
        eng.wait_ge(self.moved[i], b * self.per + k + 1)
        return self.tiles[i]

    def wait_full(self, eng, b, use):
        i, k = self.at(use)
        eng.wait_ge(self.full[i], b * self.per + k + 1)
        return self.tiles[i]

    def wait_moved(self, eng, b, use):
        i, k = self.at(use)
        eng.wait_ge(self.moved[i], b * self.per + k + 2)

    def now_full(self, ins, use):
        ins.then_inc(self.full[self.at(use)[0]], 1)

    def now_moved(self, ins, use):
        ins.then_inc(self.moved[self.at(use)[0]], 1)

    def start(self, eng, b):
        self.turn, self.next = b, 0

    def pass_over(self, eng, upto):
        for n in range(self.next, upto):
            i, k = self.at(n)
            eng.wait_ge(self.moved[i], self.turn * self.per + k + 1)
            eng.sem_inc(self.full[i], 1)
            eng.sem_inc(self.moved[i], 1)
        assert self.next <= upto
        self.next = upto

    def finish(self, eng):
        self.pass_over(eng, self.uses)


def alone(eng, passed):
    eng.sem_inc(passed, 1)


def one(b):
    return slice(b, b + 1) if isinstance(b, int) else bass.ds(b, 1)


def of_batch(t, b):
    return t[b] if isinstance(b, int) else t[bass.ds(b, 1)].rearrange("b p i d -> (b p) i d")


def mixer_attention_experts(nc, d, scratch, out):
    B, T, D = d["x"].shape
    NT = T // P
    KC = D // P
    DI = d["out_w"].shape[1] * P
    IC = DI // P
    HD = 16
    H = D // HD
    CH = P // HD
    NPAIR = H // 2
    NQUAD = H // 4
    ZM = 64
    DO = D - ZM
    SR = 96
    SLOTS = 4
    PTS = 20
    UNITS = 5

    x_dram, out_dram = (t.rearrange("b (i p) d -> b p i d", p=P) for t in (d["x"], out))
    x1_dram, xr_dram = (t.rearrange("b (i p) d -> b p i d", p=P) for t in scratch[0:2])
    q_dram, k_dram = scratch[2:4]

    with ExitStack() as ctx:
        def sem(name):
            return ctx.enter_context(nc.semaphore(name))

        def psum(name):
            return ctx.enter_context(nc.psum_tensor(name, [P, T], F32))

        banks = [psum(f"bank{i}") for i in range(8)]

        with ExitStack() as first:
            def sb(name, shape, dt=F32):
                return first.enter_context(nc.sbuf_tensor(name, shape, dt))

            ident = sb("ident", [P, P])
            ident16 = sb("ident16", [P, P], BF16)
            mask_q = sb("mask_q", [P, P], BF16)
            mask_k = sb("mask_k", [P, P], BF16)
            minus_half = sb("minus_half", [P, 32])
            win_h, win_l = sb("win_h", [P, KC, 2 * DI], F32R), sb("win_l", [P, KC, 2 * DI], F32R)
            wqkv_h, wqkv_l = sb("wqkv_h", [P, KC, 3 * D], F32R), sb("wqkv_l", [P, KC, 3 * D], F32R)
            wout = sb("wout", [P, IC, D])
            wo = sb("wo", [P, KC, DO])
            wgate = sb("wgate", [P, IC, P])
            gate_col = sb("gate_col", [P, IC])
            vecs = sb("vecs", [P, d["vecs"].shape[1]])
            at = {}
            col = 0
            for name, n in (("norm_w", KC), ("norm_b", KC), ("in_b", 2 * IC), ("conv_w", 4 * IC),
                            ("conv_b", IC), ("D", IC), ("n1_w", KC), ("qn_w", 1), ("kn_w", 1)):
                at[name] = vecs[:, col:col + n]
                col += n
            b_in = sb("b_in", [P, 2 * IC])
            d2 = sb("d2", [P, IC])
            out_b = sb("out_b", [P, D])

            x = sb("x_sb", [P, NT, D])
            u = sb("u", [P, NT, D])
            z = sb("z", [P, NT, D])
            zT_h, zT_l = sb("zT_h", [P, KC, T], F32R), sb("zT_l", [P, KC, T], F32R)
            xi = sb("xi", [P, IC, T + 3])
            xc = sb("xc", [P, IC, T])
            sz = sb("sz", [P, IC, T])
            th = sb("th", [P, T])
            st6 = sb("st6", [P, NT, 6])
            mv = sb("mv", [P, NT, 2])
            mv1 = sb("mv1", [P, NT, 2])
            mvf = sb("mvf", [P, NT, 2])
            sm = sb("sm", [P, 8, NT])

            hz = sb("hz", [P, NT, D])
            qk_raw = sb("qk_raw", [P, NT, 2 * D])
            sq = sb("sq", [P, 2, T])
            ms, rqk, nt = (sb(n, [P, NT * 2 * H]) for n in ("ms", "rqk", "nt"))
            qkT = sb("qkT", [P, 2, 2, T], F32R)
            v2 = sb("v2", [P, NT, D])

            v = sb("v", [P, NT, H, 32])
            qS, kS = sb("qS", [P, SLOTS, 2, T], F32R), sb("kS", [P, SLOTS, 2, T], F32R)
            mxs = sb("mxs", [P, 2, 8])
            nm_h, nm_l = sb("nm_h", [8, 2, P], F32R), sb("nm_l", [8, 2, P], F32R)
            pt = sb("pt", [P, PTS, T])
            oTs = sb("oTs", [P, T])
            rc = sb("rc", [P, NT, 4])
            otok = sb("otok", [P, NT, D])
            oT = sb("oT", [P, KC, T])

            w_stage = pt[:, 0:8, :].rearrange("p s t -> p (s t)")
            win_f = w_stage[:, 0:KC * 2 * DI].rearrange("p (k n) -> p k n", k=KC)
            wqkv_f = w_stage[:, KC * 2 * DI:KC * 2 * DI + KC * 3 * D].rearrange("p (k n) -> p k n", k=KC)
            wc = pt[:, 8:8 + IC * HD // T + 1, :].rearrange("p s t -> p (s t)")[:, 0:IC * HD].rearrange("p (c d) -> p c d", c=IC)

            S_ZT, S_IN, S_HT, S_QK, S_GATE, S_V, S_OUT, S_QT = 3, 5, 13, 15, 19, 20, (22, 25), 23
            f_order = ["zt0", "zt1"] + [f"in{m}" for m in range(2 * IC)] + ["ht0", "ht1"]
            f_order += [f"qk{i}" for i in range(NT)] + ["gate"] + [f"v{i}" for i in range(NT)]
            f_order += ["out0", "qt0", "qt1", "qt2", "qt3", "out1"]
            o_order = ["pv3-", "mt1", "ot3-", "t0-", "t1-", "mt2", "wo0-", "wo1-", "pv0", "mt3", "ot0", "mt4",
                       "pv1", "mt5", "ot1", "mt6", "pv2", "mt7", "ot2", "mt8"]
            fb = Banks(banks[0:3], [sem(f"front_full{i}") for i in range(3)],
                       [sem(f"front_moved{i}") for i in range(3)], f_order)
            ob = Banks(banks[3:4], [sem("o_full")], [sem("o_moved")], o_order)
            mx_bank, st_bank = banks[4:6], banks[6:8]
            mx_full, mx_read = sem("mx_full"), sem("mx_read")
            st_full, exp_done = sem("st_full"), sem("exp_done")

            w_loaded, consts, w_hi, bias_mm, w_ready = (
                sem(n) for n in ("w_loaded", "consts", "w_hi", "bias_mm", "w_ready"))
            x_loaded, x1_stored, xin_stored = sem("x_loaded"), sem("x1_stored"), sem("xin_stored")
            stats, scales, z_ready, z_hi = sem("stats"), sem("scales"), sem("z_ready"), sem("z_hi")
            conv_done, silu_done, p_ready, y_ready = (
                sem(n) for n in ("conv_done", "silu_done", "p_ready", "y_ready"))
            ub_ready, x1_ready, xin_ready, hz_ready = sem("ub_ready"), sem("x1_ready"), sem("xin_ready"), sem("hz_ready")
            h_hi, sq_summed, qk_normed, qk_hi = sem("h_hi"), sem("sq_summed"), sem("qk_normed"), sem("qk_hi")
            qk_out = [sem("qk_out0"), sem("qk_out1")]
            v_placed = sem("v_placed")
            stacked = [sem(f"stacked{i}") for i in range(SLOTS)]
            nm_hi = sem("nm_hi")
            rows = [sem("rows0"), sem("rows1")]
            o_sums, res_loaded, xr_stored = sem("o_sums"), sem("res_loaded"), sem("xr_stored")
            dve_mix, dve_qk, dve_pre = sem("dve_mix"), sem("dve_qk"), sem("dve_pre")
            pool_mix, pool_pre = sem("pool_mix"), sem("pool_pre")
            passed = sem("passed")

            def units(descending):
                w = (lambda i: (i + 1) * P) if descending else (lambda j: (NT - j) * P)
                full, three, two, one = (3, 2, 1, 0) if descending else (0, 1, 2, 3)
                res = []
                for h in range(2):
                    res.append([(h, full, 0, w(full))])
                    res.append([(h, three, 0, w(three)), (h, one, w(three), w(one))])
                res.append([(0, two, 0, w(two)), (1, two, w(two), w(two))])
                return res

            MAX_UNITS, ST_UNITS = units(True), units(False)
            PU = NPAIR * UNITS
            pt_at = {}
            for n, unit in enumerate(ST_UNITS):
                for h, j, c, w in unit:
                    pt_at[h, j] = (n, c, w)

            def all_turns(eng, turn):
                assert B > 4
                turn(0, None, None, None, None, 0)
                turn(1, None, None, 0, 0, 1)
                turn(2, None, 0, 1, 1, 2)
                with eng.Fori(1, B - 3) as a:
                    turn(a + 2, a - 1, a, a + 1, a + 1, a + 2)
                turn(B - 1, B - 4, B - 3, B - 2, B - 2, B - 1)
                turn(B, B - 3, B - 2, B - 1, B - 1, None)
                turn(B + 1, B - 2, B - 1, None, None, None)
                turn(B + 2, B - 1, None, None, None, None)

            def of_pair(att, nxt, pair):
                if pair < NPAIR:
                    return None if att is None else (att, pair)
                return None if nxt is None else (nxt, pair - NPAIR)

            def is_first(b):
                return isinstance(b, int) and b == 0

            with nc.Block() as block:

                @block.sync
                def _(sp):
                    for dst, src in ((win_f, d["in_w"]), (wqkv_f, d["wqkv"]), (wout[:], d["out_w"]),
                                     (wo[:], d["wo"]), (wc, d["xproj_w"][:, :, 1 + HD:1 + 2 * HD]),
                                     (vecs[:], d["vecs"]), (out_b[:], d["out_b"])):
                        sp.dma_start(dst, src).then_inc(w_loaded, 16)

                    def load_x(b):
                        if not is_first(b):
                            sp.wait_ge(hz_ready, b)
                            alone(sp, passed)
                            sp.wait_ge(xin_ready, b)
                            alone(sp, passed)
                            sp.wait_ge(x1_stored, 16 * b)
                            alone(sp, passed)
                        sp.dma_start(x[:], of_batch(x_dram, b)).then_inc(x_loaded, 16)

                    def store_x1(b):
                        sp.wait_ge(x1_ready, b + 1)
                        alone(sp, passed)
                        sp.dma_start(of_batch(x1_dram, b), x[:]).then_inc(x1_stored, 16)

                    def store_xin(b):
                        sp.wait_ge(xin_ready, b + 1)
                        alone(sp, passed)
                        sp.dma_start(of_batch(xr_dram, b), u[:]).then_inc(xin_stored, 16)

                    def store_qk(t, b):
                        for c in range(4):
                            fb.wait_moved(sp, t, f"qt{c}")
                            alone(sp, passed)
                            for part in range(2):
                                if c < 2:
                                    dst = q_dram[one(b), :, part, :, c, :].rearrange("b r d t -> (b r) d t")
                                else:
                                    dst = k_dram[one(b), :, :, part, c - 2, :].rearrange("b r d t -> (b r) d t")
                                sp.dma_start(dst, qkT[:, c % 2, part, :].bitcast(F32)).then_inc(qk_out[c % 2], 16)

                    def stack(b, pair):
                        s = pair % SLOTS
                        if pair == 0:
                            sp.wait_ge(qk_out[0], 64 * b + 64)
                            sp.wait_ge(qk_out[1], 64 * b + 64)
                            alone(sp, passed)
                        if pair >= SLOTS or not is_first(b):
                            sp.wait_ge(st_full, b * PU + (pair - SLOTS + 1) * UNITS)
                            alone(sp, passed)
                        q = q_dram[one(b), pair].rearrange("b l d h t -> (b l d) (h t)").unsqueeze(1)
                        k = k_dram[one(b), pair].rearrange("b d l h t -> b (d l) (h t)")
                        sp.dma_start(qS[0:4 * HD, s, :, :].bitcast(F32), q.to_broadcast([2 * HD, 2, 2 * T])).then_inc(stacked[s], 16)
                        sp.dma_start(kS[0:4 * HD, s, :, :].bitcast(F32), k.to_broadcast([2, 2 * HD, 2 * T])).then_inc(stacked[s], 16)

                    def max_rows(t, pair, slot_pair):
                        ob.wait_moved(sp, t, f"mt{slot_pair}")
                        for r, src in enumerate((nm_h, nm_l)):
                            sp.dma_start(qS[SR + r:SR + r + 1, pair % SLOTS, :, :].bitcast(F32),
                                         src[:, pair % 2, :].bitcast(F32)).then_inc(rows[pair % 2], 16)

                    def load_residual(t, b):
                        ob.wait_full(sp, t, "t1-")
                        alone(sp, passed)
                        sp.wait_ge(xin_stored, 16 * (b + 1))
                        alone(sp, passed)
                        sp.dma_start(otok[:], of_batch(xr_dram, b)).then_inc(res_loaded, 16)

                    def store_xr(t, b):
                        ob.wait_moved(sp, t, "wo1-")
                        alone(sp, passed)
                        sp.dma_start(of_batch(xr_dram, b), otok[:]).then_inc(xr_stored, 16)

                    def turn(t, tail, att, nxt, qkv, mix):
                        if is_first(mix):
                            load_x(mix)
                        for p in range(NPAIR):
                            if p == 4 and qkv is not None and att is None:
                                store_qk(t, qkv)
                            if of_pair(att, nxt, p + 1) is not None:
                                max_rows(t, (p + 1) % NPAIR, p + 1)
                            if p == 4 and qkv is not None and att is not None:
                                store_qk(t, qkv)
                            if p == 7 and mix is not None:
                                if isinstance(mix, int) and mix == B - 1:
                                    pass
                                else:
                                    load_x(mix + 1)
                            if of_pair(att, nxt, p + 4) is not None:
                                stack(*of_pair(att, nxt, p + 4))
                            if p == 6 and mix is not None:
                                store_x1(mix)
                                store_xin(mix)
                            if p == 0 and tail is not None:
                                load_residual(t, tail)
                            if p == 1 and tail is not None:
                                store_xr(t, tail)

                    all_turns(sp, turn)
                    sp.wait_ge(xr_stored, 16 * B)
                    sp.wait_ge(x1_stored, 16 * B)
                    sp.wait_ge(xin_stored, 16 * B)

                @block.gpsimd
                def _(pool):
                    nc.gpsimd.memset(ident[:], 0.0)
                    nc.gpsimd.memset(mask_q[:], 0.0)
                    nc.gpsimd.memset(mask_k[:], 0.0)
                    nc.gpsimd.memset(minus_half[:], -0.5)
                    nc.gpsimd.memset(v[:], 1.0)
                    nc.gpsimd.memset(xi[:], 0.0).then_inc(pool_pre, 1)
                    pool.wait_ge(pool_pre, 1)
                    nc.gpsimd.affine_select(out=ident[:], in_=ident[:], compare_op=ALU.not_equal, fill=1.0,
                                            base=0, pattern=[[-1, P]], channel_multiplier=1)
                    nc.gpsimd.affine_select(out=mask_q[:], in_=mask_q[:], compare_op=ALU.is_ge, fill=MASKED,
                                            base=0, pattern=[[-1, P]], channel_multiplier=1)
                    nc.gpsimd.affine_select(out=mask_k[:], in_=mask_k[:], compare_op=ALU.is_ge, fill=MASKED,
                                            base=0, pattern=[[1, P]], channel_multiplier=-1).then_inc(pool_pre, 1)
                    pool.wait_ge(pool_pre, 2)
                    nc.gpsimd.tensor_copy(ident16[:], ident[:]).then_inc(consts, 1)
                    link = Links(pool, pool_mix, 13)
                    tt, ts = nc.gpsimd.tensor_tensor, nc.gpsimd.tensor_scalar
                    half = minus_half

                    def two_norms(m_v, r0, rs, eps_out):
                        var, e, t = m_v[:, :, 1], sm[:, 6, :], sm[:, 7, :]
                        link(ts(e, var, EPS_LN, None, op0=ALU.add))
                        link(tt(r0, e, half[:, 0:NT], ALU.pow))
                        link(tt(t, var, r0, ALU.mult))
                        link(tt(e, t, r0, ALU.mult))
                        alone(pool, passed)
                        link(ts(t, e, eps_out, None, op0=ALU.add))
                        link(tt(e, t, half[:, 0:NT], ALU.pow))
                        tt(rs, e, r0, ALU.mult).then_inc(scales, 1)

                    def place_v(t, b, tail):
                        fb.wait_moved(pool, t - 1, "v3")
                        fb.wait_moved(pool, t - 1, "v2")
                        fb.wait_moved(pool, t - 1, "v1")
                        if tail is not None:
                            ob.wait_full(pool, t, "pv3-")
                        alone(pool, passed)
                        for i in range(NT):
                            last = nc.gpsimd.tensor_copy(v[:, i, :, 0:HD], v2[:, i, :].rearrange("p (h d) -> p h d", d=HD))
                        last.then_inc(v_placed, 1)

                    def turn(t, tail, att, nxt, qkv, mix):
                        if mix is not None:
                            b = mix
                            link.batch(b)
                            pool.wait_ge(stats, b * 3 + 1)
                            alone(pool, passed)
                            two_norms(mv, sm[:, 0, :], sm[:, 1, :], EPS_LN)
                        if att is not None:
                            place_v(t, att, tail)
                        if mix is not None:
                            pool.wait_ge(z_ready, b + 1)
                            for i in range(NT):
                                last = tt(u[:, i, :], u[:, i, :], out_b[:], ALU.add)
                            last.then_inc(ub_ready, 1)
                            pool.wait_ge(silu_done, b + 1)
                            for c in range(IC):
                                last = tt(sz[:, c, :], sz[:, c, :], xc[:, c, :], ALU.mult)
                            last.then_inc(p_ready, 1)
                            pool.wait_ge(stats, b * 3 + 2)
                            alone(pool, passed)
                            link(ts(sm[:, 6, :], mvf[:, :, 1], EPS_LN, None, op0=ALU.add))
                            tt(sm[:, 2, :], sm[:, 6, :], half[:, 0:NT], ALU.pow).then_inc(scales, 1)
                            pool.wait_ge(stats, b * 3 + 3)
                            alone(pool, passed)
                            two_norms(mv1, sm[:, 3, :], sm[:, 4, :], EPS_RMS)

                    all_turns(pool, turn)

                @block.scalar
                def _(act):
                    activation, copy = nc.scalar.activation, ACT.Copy
                    for s in fb.moved + ob.moved:
                        act.sem_inc(s, 1)
                    act.sem_inc(exp_done, 2)
                    act.wait_ge(w_loaded, 16 * 7)
                    activation(win_h[:], win_f, copy)
                    activation(wqkv_h[:], wqkv_f, copy).then_inc(w_hi, 1)
                    act.wait_ge(w_ready, 1)

                    def move_hi(t, use, dst, w, ready):
                        bank = fb.wait_full(act, t, use)
                        activation(dst, bank[:], copy, scale=w).then_inc(ready, 1)

                    def in_proj(t, m):
                        bank = fb.wait_full(act, t, f"in{m}")
                        dst = xi[:, m, 3:] if m < IC else sz[:, m - IC, :]
                        fb.now_moved(activation(dst, bank[:], ACT.Identity, bias=b_in[:, m:m + 1]), f"in{m}")

                    def silus(t, b):
                        act.wait_ge(conv_done, b + 1)
                        for m in range(3):
                            fb.wait_moved(act, t, f"in{2 * IC - 1 - m}")
                        activation(sz[:], sz[:], ACT.Silu)
                        activation(xc[:], xc[:], ACT.Silu).then_inc(silu_done, 1)

                    def gate(t):
                        bank = fb.wait_full(act, t, "gate")
                        fb.now_moved(activation(th[:], bank[:], ACT.Tanh, scale=0.5), "gate")

                    def raw_and_squares(t, b, i):
                        bank = fb.wait_full(act, t, f"qk{i}")
                        activation(qk_raw[:, i, :], bank[:], copy)
                        act.wait_ge(sq_summed, b * NT + i + 1)
                        fb.now_moved(activation(sq[:, i % 2, :], bank[:], ACT.Square), f"qk{i}")

                    def qk_transposed(t, b, c):
                        if c >= 2 or not is_first(b):
                            act.wait_ge(qk_out[c % 2], b * 64 + (c // 2) * 32)
                        move_hi(t, f"qt{c}", qkT[:, c % 2, 0, :], at["qn_w"] if c < 2 else at["kn_w"], qk_hi)

                    def values(t, b, i):
                        bank = fb.wait_full(act, t, f"v{i}")
                        if i == 0 and not is_first(b):
                            act.wait_ge(v_placed, b)
                        fb.now_moved(activation(v2[:, i, :], bank[:, 0:D], copy), f"v{i}")

                    def minus_max(t, b, pair, slot_pair):
                        bank = ob.wait_full(act, t, f"mt{slot_pair}")
                        if pair >= 2 or not is_first(b):
                            act.wait_ge(rows[pair % 2], b * (NPAIR * 16) + (pair // 2) * 32)
                        activation(nm_h[:, pair % 2, :], bank[0:8, 0:P], copy, scale=-1.0).then_inc(nm_hi, 1)

                    def exps(b, pair, n):
                        k = pair * UNITS + n
                        act.wait_ge(st_full, b * PU + k + 1)
                        activation(pt[:, k % PTS, :], st_bank[k % 2][:], ACT.Exp).then_inc(exp_done, 1)

                    def o_move(t, use, dst):
                        bank = ob.wait_full(act, t, use)
                        ob.now_moved(activation(dst, bank[:], copy), use)

                    def turn(t, tail, att, nxt, qkv, mix):
                        for slot in range(PU):
                            p, n = slot // UNITS, slot % UNITS
                            if att is not None:
                                exps(att, p, n)
                            if tail is not None and slot == 1:
                                o_move(t, "pv3-", oTs[:])
                            if att is not None and slot in (11, 21, 31):
                                o_move(t, f"pv{slot // 10 - 1}", oTs[:])
                            if tail is not None and slot in (5, 6):
                                o_move(t, f"t{slot - 5}-", oT[:, slot - 5, :])
                            if n == 1 and of_pair(att, nxt, p + 1) is not None:
                                minus_max(t, *of_pair(att, nxt, p + 1), p + 1)
                            if mix is not None:
                                if slot == S_ZT + 1:
                                    for c in range(KC):
                                        move_hi(t, f"zt{c}", zT_h[:, c, :], at["norm_w"][:, c:c + 1], z_hi)
                                if S_IN < slot <= S_IN + 2 * IC:
                                    in_proj(t, slot - S_IN - 1)
                                if slot == S_HT + 2:
                                    silus(t, mix)
                                if slot == S_GATE + 1:
                                    gate(t)
                            if qkv is not None:
                                if slot == S_HT + 1:
                                    for c in range(KC):
                                        move_hi(t, f"ht{c}", zT_h[:, c, :], at["n1_w"][:, c:c + 1], h_hi)
                                if S_QK < slot <= S_QK + NT:
                                    raw_and_squares(t, qkv, slot - S_QK - 1)
                                if slot in (S_V + 1, S_V + 2):
                                    for i in range(2):
                                        values(t, qkv, 2 * (slot - S_V - 1) + i)
                                if slot in (S_QT + 1, S_QT + 2):
                                    for c in range(2):
                                        qk_transposed(t, qkv, 2 * (slot - S_QT - 1) + c)

                    all_turns(act, turn)

                @block.vector
                def _(dve):
                    link, qlink = Links(dve, dve_mix, 3 + 6 + 1), Links(dve, dve_qk, 11)
                    tt, ts, stt = nc.vector.tensor_tensor, nc.vector.tensor_scalar, nc.vector.scalar_tensor_tensor
                    dve.sem_inc(mx_read, 2)
                    dve.sem_inc(sq_summed, 2)
                    nc.vector.memset(qS[:].bitcast(F32), 0.0)
                    nc.vector.memset(kS[0:SR].bitcast(F32), 0.0)
                    nc.vector.memset(kS[SR:P].bitcast(F32), 1.0)
                    dve.wait_ge(w_loaded, 16 * 7)
                    ts(wout[:], wout[:], 0.5, None, op0=ALU.mult)
                    ts(d2[:], at["D"], 2.0, 1.0, op0=ALU.mult, op1=ALU.add)
                    ts(at["qn_w"], at["qn_w"], float(HD) ** -0.5, None, op0=ALU.mult)
                    nc.vector.tensor_reduce(gate_col[:], wc, AX.X, ALU.add).then_inc(dve_pre, 1)
                    dve.wait_ge(dve_pre, 1)
                    for c in range(IC):
                        ts(wgate[:, c, :], gate_col[:, c:c + 1].to_broadcast([P, P]), 1.0 / HD, None, op0=ALU.mult)
                    dve.wait_ge(w_hi, 1)
                    tt(win_l[:], win_f, win_h[:].bitcast(F32), ALU.subtract)
                    tt(wqkv_l[:], wqkv_f, wqkv_h[:].bitcast(F32), ALU.subtract)
                    dve.wait_ge(bias_mm, 1)
                    tt(b_in[:], mx_bank[0][:, 0:2 * IC], at["in_b"], ALU.add).then_inc(w_ready, 1)

                    def normed(dst, src, m_v, scale):
                        for i in range(NT):
                            last = ts(dst[:, i, :], src[:, i, :], m_v[:, i, 0:1], sm[:, scale, i:i + 1],
                                      op0=ALU.subtract, op1=ALU.mult)
                        return last

                    def row_stats(src, m_v):
                        for i in range(NT):
                            last = nc.vector.bn_stats(st6[:, i, :], src[:, i, :])
                        link(last)
                        alone(dve, passed)
                        for i in range(NT):
                            last = nc.vector.bn_aggr(m_v[:, i, :], st6[:, i, :])
                        last.then_inc(stats, 1)

                    def norm_in(b):
                        dve.wait_ge(x_loaded, 16 * (b + 1))
                        row_stats(x, mv)

                    def u_and_z(b):
                        if not is_first(b):
                            dve.wait_ge(xin_stored, 16 * b)
                        dve.wait_ge(scales, b * 3 + 1)
                        normed(u, x, mv, 0)
                        normed(z, x, mv, 1).then_inc(z_ready, 1)

                    def move_lo(t, use, dst, hi, w, ready, count):
                        bank = fb.wait_full(dve, t, use)
                        dve.wait_ge(ready, count)
                        fb.now_moved(stt(dst, bank[:], w, hi.bitcast(F32), ALU.mult, ALU.subtract), use)

                    def conv(t, step):
                        for m in range(IC):
                            j = step - m
                            if not 0 <= j < 4:
                                continue
                            if j == 0:
                                fb.wait_moved(dve, t, f"in{m}")
                            w = at["conv_w"][:, 4 * m + j:4 * m + j + 1]
                            if j == 0:
                                last = ts(xc[:, m, :], xi[:, m, 0:T], w, at["conv_b"][:, m:m + 1], op0=ALU.mult, op1=ALU.add)
                            else:
                                last = stt(xc[:, m, :], xi[:, m, j:j + T], w, xc[:, m, :], ALU.mult, ALU.add)
                        if step < IC + 2:
                            link(last)
                        else:
                            last.then_inc(conv_done, 1)

                    def y(t, b):
                        fb.wait_moved(dve, t, "gate")
                        dve.wait_ge(p_ready, b + 1)
                        for c in range(IC):
                            last = stt(sz[:, c, :], th[:], d2[:, c:c + 1], sz[:, c, :], ALU.add, ALU.mult)
                        last.then_inc(y_ready, 1)

                    def mixer_out(t, b, k):
                        dve.wait_ge(ub_ready, b + 1)
                        bank = fb.wait_full(dve, t, f"out{k}")
                        fb.now_moved(tt(z[:, 2 * k:2 * k + 2, :], bank[:].rearrange("p (i d) -> p i d", d=D),
                                        u[:, 2 * k:2 * k + 2, :], ALU.add), f"out{k}")

                    def out_stats(t):
                        fb.wait_moved(dve, t, "out0")
                        fb.wait_moved(dve, t, "out1")
                        row_stats(z, mvf)

                    def make_x1(b):
                        dve.wait_ge(scales, b * 3 + 2)
                        link(normed(z, z, mvf, 2))
                        tt(x[:], x[:], z[:], ALU.add).then_inc(x1_ready, 1)
                        dve.wait_ge(x1_ready, b + 1)
                        row_stats(x, mv1)

                    def make_h(b):
                        dve.wait_ge(scales, b * 3 + 3)
                        normed(hz, x, mv1, 4).then_inc(hz_ready, 1)
                        normed(u, x, mv1, 3).then_inc(xin_ready, 1)

                    def sum_squares(t, i):
                        fb.wait_moved(dve, t, f"qk{i}")
                        nc.vector.tensor_reduce(ms[:, i * 2 * H:(i + 1) * 2 * H], sq[:, i % 2, :].rearrange("p (h d) -> p h d", d=HD),
                                                AX.X, ALU.add).then_inc(sq_summed, 1)

                    def guess_rsqrt(b):
                        dve.wait_ge(sq_summed, b * NT + NT + 2)
                        qlink(ts(ms[:], ms[:], 1.0 / HD, EPS_RMS, op0=ALU.mult, op1=ALU.add))
                        qlink(ts(rqk[:].bitcast(I32), ms[:].bitcast(I32), -0.5, float(0x5f3759df), op0=ALU.mult, op1=ALU.add))

                    def newton(b, step):
                        qlink(tt(nt[:], rqk[:], rqk[:], ALU.mult))
                        qlink(stt(nt[:], nt[:], -0.5, ms[:], ALU.mult, ALU.mult))
                        qlink(stt(rqk[:], nt[:], 1.5, rqk[:], ALU.add, ALU.mult))

                    def scale_qk():
                        for i in range(NT):
                            a = qk_raw[:, i, :].rearrange("p (h d) -> p h d", d=HD)
                            last = tt(a, a, rqk[:, i * 2 * H:(i + 1) * 2 * H].unsqueeze(2).to_broadcast([P, 2 * H, HD]), ALU.mult)
                        last.then_inc(qk_normed, 1)

                    def maxima(b, pair, n):
                        k = pair * UNITS + n
                        dve.wait_ge(mx_full, b * PU + k + 1)
                        t, m = mx_bank[k % 2], mxs[:, pair % 2, :]
                        if n == 4:
                            last = nc.vector.tensor_reduce(m.rearrange("p (h i) -> p h i", h=2)[:, :, 1],
                                                           t[:].rearrange("p (h c) -> p h c", h=2), AX.X, ALU.max)
                        else:
                            for h, i, c, w in MAX_UNITS[n]:
                                last = nc.vector.tensor_reduce(m[:, h * 4 + i:h * 4 + i + 1], t[:, c:c + w], AX.X, ALU.max)
                        last.then_inc(mx_read, 1)

                    def minus_max_lo(t, b, pair, slot_pair):
                        bank = ob.wait_full(dve, t, f"mt{slot_pair}")
                        dve.wait_ge(nm_hi, b * NPAIR + pair + 1)
                        ob.now_moved(stt(nm_l[:, pair % 2, :], bank[0:8, 0:P], -1.0, nm_h[:, pair % 2, :].bitcast(F32),
                                         ALU.mult, ALU.subtract), f"mt{slot_pair}")

                    def o_norm(t, b, g, use):
                        bank = ob.wait_full(dve, t, use)[:].rearrange("p (i q e) -> p i q e", q=4, e=32)
                        if g == 0 and not is_first(b):
                            dve.wait_ge(xr_stored, 16 * b)
                        nc.vector.reciprocal(rc[:], bank[:, :, :, HD]).then_inc(o_sums, 1)
                        dve.wait_ge(o_sums, 4 * b + g + 1)
                        for e in range(2):
                            pair = 2 * g + e
                            dst = otok[:].rearrange("p i (h f) -> p i h f", h=2)[:, :, :, HD * pair:HD * (pair + 1)]
                            last = tt(dst, bank[:, :, 2 * e:2 * e + 2, 0:HD],
                                      rc[:, :, 2 * e:2 * e + 2].unsqueeze(3).to_broadcast([P, NT, 2, HD]), ALU.mult)
                        ob.now_moved(last, use)

                    def wo_add(t, b, k):
                        bank = ob.wait_full(dve, t, f"wo{k}-")
                        dve.wait_ge(res_loaded, 16 * (b + 1))
                        dst = otok[:, 2 * k:2 * k + 2, ZM:]
                        ob.now_moved(tt(dst, bank[:, 0:2 * DO].rearrange("p (i d) -> p i d", d=DO), dst, ALU.add), f"wo{k}-")

                    def turn(t, tail, att, nxt, qkv, mix):
                        if mix is not None:
                            link.batch(mix)
                        if qkv is not None:
                            qlink.batch(qkv)
                        for slot in range(PU):
                            p, n = slot // UNITS, slot % UNITS
                            if of_pair(att, nxt, p + 2) is not None:
                                maxima(*of_pair(att, nxt, p + 2), n)
                            if n == 1 and of_pair(att, nxt, p + 1) is not None:
                                minus_max_lo(t, *of_pair(att, nxt, p + 1), p + 1)
                            if tail is not None:
                                if slot == 3:
                                    o_norm(t, tail, 3, "ot3-")
                                if slot in (8, 9):
                                    wo_add(t, tail, slot - 8)
                            if att is not None and slot in (13, 23, 33):
                                o_norm(t, att, slot // 10 - 1, f"ot{slot // 10 - 1}")
                            if mix is not None:
                                if slot == 0:
                                    norm_in(mix)
                                if slot == S_ZT - 1:
                                    u_and_z(mix)
                                if slot == S_ZT + 1:
                                    for c in range(KC):
                                        move_lo(t, f"zt{c}", zT_l[:, c, :], zT_h[:, c, :], at["norm_w"][:, c:c + 1],
                                                z_hi, mix * KC + c + 1)
                                if S_IN + 2 <= slot < S_IN + 2 + IC + 3:
                                    conv(t, slot - S_IN - 2)
                                if slot == S_GATE + 2:
                                    y(t, mix)
                                if slot == S_OUT[0] + 2:
                                    mixer_out(t, mix, 0)
                                if slot == S_OUT[1] + 2:
                                    mixer_out(t, mix, 1)
                                    out_stats(t)
                                if slot == S_OUT[1] + 3:
                                    make_x1(mix)
                                if slot == S_OUT[1] + 6:
                                    make_h(mix)
                            if qkv is not None:
                                if slot == S_HT + 1:
                                    for c in range(KC):
                                        move_lo(t, f"ht{c}", zT_l[:, c, :], zT_h[:, c, :], at["n1_w"][:, c:c + 1],
                                                h_hi, qkv * KC + c + 1)
                                if S_QK < slot <= S_QK + NT:
                                    sum_squares(t, slot - S_QK - 1)
                                if slot == S_QK + NT:
                                    guess_rsqrt(qkv)
                                    newton(qkv, 0)
                                if slot == S_QK + NT + 1:
                                    newton(qkv, 1)
                                    newton(qkv, 2)
                                if slot == S_QK + NT + 2:
                                    scale_qk()
                                if slot in (S_QT + 1, S_QT + 2):
                                    for c in range(2 * (slot - S_QT - 1), 2 * (slot - S_QT)):
                                        w = at["qn_w"] if c < 2 else at["kn_w"]
                                        move_lo(t, f"qt{c}", qkT[:, c % 2, 1, :], qkT[:, c % 2, 0, :], w, qk_hi, qkv * 4 + c + 1)

                    all_turns(dve, turn)

                @block.tensor
                def _(pe):
                    mm = nc.tensor.matmul

                    def split(out_ap, stat, mov):
                        for c in range(KC):
                            (sh, sl), (mh, ml) = stat(c), mov(c)
                            for s, m in ((sh, mh), (sh, ml), (sl, mh)):
                                last = mm(out_ap, s, m, start=(c == 0 and s is sh and m is mh), stop=(c == KC - 1 and s is sl))
                        return last

                    def transposes(bank, sources):
                        for i, src in enumerate(sources):
                            last = nc.tensor.transpose(bank[:, i * P:(i + 1) * P], src, ident[:])
                        return last

                    pe.wait_ge(w_loaded, 16 * 7)
                    pe.wait_ge(consts, 1)
                    for m in range(2 * IC):
                        for c in range(KC):
                            last = mm(mx_bank[0][:, m:m + 1], win_f[:, c, m * P:(m + 1) * P], at["norm_b"][:, c:c + 1],
                                      start=(c == 0), stop=(c == KC - 1))
                    last.then_inc(bias_mm, 1)
                    pe.wait_ge(w_ready, 1)

                    def z_transposes(t, b, src, name, ready):
                        pe.wait_ge(ready, b + 1)
                        for c in range(KC):
                            bank = fb.wait_free(pe, t, f"{name}{c}")
                            fb.now_full(transposes(bank, [src[:, i, c * P:(c + 1) * P] for i in range(NT)]), f"{name}{c}")

                    def in_proj(t, m):
                        if m == 0:
                            for c in range(KC):
                                fb.wait_moved(pe, t, f"zt{c}")
                        bank = fb.wait_free(pe, t, f"in{m}")
                        cols = slice(m * P, (m + 1) * P)
                        fb.now_full(split(bank[:], lambda c: (win_h[:, c, cols], win_l[:, c, cols]),
                                          lambda c: (zT_h[:, c, :], zT_l[:, c, :])), f"in{m}")

                    def gate(t, b):
                        pe.wait_ge(silu_done, b + 1)
                        bank = fb.wait_free(pe, t, "gate")
                        for c in range(IC):
                            last = mm(bank[:], wgate[:, c, :], xc[:, c, :], start=(c == 0), stop=(c == IC - 1))
                        fb.now_full(last, "gate")

                    def out_proj(t, b, k, i):
                        if i == 0:
                            pe.wait_ge(y_ready, b + 1)
                            fb.wait_free(pe, t, f"out{k}")
                        bank = fb.tile(f"out{k}")
                        tok = slice((2 * k + i) * P, (2 * k + i + 1) * P)
                        for c in range(IC):
                            last = mm(bank[:, i * D:(i + 1) * D], sz[:, c, tok], wout[:, c, :], start=(c == 0), stop=(c == IC - 1))
                        if i == 1:
                            fb.now_full(last, f"out{k}")

                    def qkv_product(t, use, i, cols):
                        bank = fb.wait_free(pe, t, use)
                        tok = slice(i * P, (i + 1) * P)
                        n = cols.stop - cols.start
                        fb.now_full(split(bank[:, 0:n], lambda c: (zT_h[:, c, tok], zT_l[:, c, tok]),
                                          lambda c: (wqkv_h[:, c, cols], wqkv_l[:, c, cols])), use)

                    def qk(t, i):
                        if i == 0:
                            for c in range(KC):
                                fb.wait_moved(pe, t, f"ht{c}")
                        qkv_product(t, f"qk{i}", i, slice(0, 2 * D))

                    def qk_transposes(t, b, c):
                        if c == 0:
                            pe.wait_ge(qk_normed, b + 1)
                        bank = fb.wait_free(pe, t, f"qt{c}")
                        fb.now_full(transposes(bank, [qk_raw[:, i, c * P:(c + 1) * P] for i in range(NT)]), f"qt{c}")

                    def scores_for_max(b, pair, n):
                        s, k = pair % SLOTS, pair * UNITS + n
                        if n == 0:
                            pe.wait_ge(stacked[s], b * (NPAIR // SLOTS * 32) + (pair // SLOTS + 1) * 32)
                        pe.wait_ge(mx_read, b * PU + k + 1)
                        t = mx_bank[k % 2]
                        for h, i, c, w in MAX_UNITS[n]:
                            mm(t[:, c:c + w], qS[0:SR, s, h, i * P:(i + 1) * P], kS[0:SR, s, h, 0:w], start=True, stop=False)
                            last = mm(t[:, c + i * P:c + w], ident16[:], mask_q[:], start=False, stop=True)
                        last.then_inc(mx_full, 1)

                    def max_transposed(t, b, pair, slot_pair):
                        pe.wait_ge(mx_read, b * PU + (pair + 1) * UNITS + 2)
                        bank = ob.wait_free(pe, t, f"mt{slot_pair}")
                        ob.now_full(nc.tensor.transpose(bank[0:8, 0:P], mxs[:, pair % 2, :], ident[:]), f"mt{slot_pair}")

                    def scores(b, pair, n):
                        s, k = pair % SLOTS, pair * UNITS + n
                        if n == 0:
                            pe.wait_ge(rows[pair % 2], b * (NPAIR * 16) + (pair // 2 + 1) * 32)
                        pe.wait_ge(exp_done, b * PU + k + 1)
                        t = st_bank[k % 2]
                        for h, j, c, w in ST_UNITS[n]:
                            mm(t[:, c:c + w], kS[0:SR + 2, s, h, j * P:(j + 1) * P], qS[0:SR + 2, s, h, j * P:T], start=True, stop=False)
                            last = mm(t[:, c:c + P], ident16[:], mask_k[:], start=False, stop=True)
                        last.then_inc(st_full, 1)

                    def values_summed(t, b, g, use):
                        pe.wait_ge(exp_done, b * PU + (2 * g + 2) * UNITS + 2)
                        if g == 0:
                            pe.wait_ge(v_placed, b + 1)
                        bank = ob.wait_free(pe, t, use)
                        for j in range(NT):
                            for q in range(4):
                                pair, h = 2 * g + q // 2, q % 2
                                n, c, w = pt_at[h, j]
                                last = mm(bank[32 * q:32 * (q + 1), j * P:T], v[:, j, h * CH + pair, :],
                                          pt[:, (pair * UNITS + n) % PTS, c:c + w], start=(j == 0), stop=(j == NT - 1))
                        ob.now_full(last, use)

                    def o_back(t, pv, use):
                        ob.wait_moved(pe, t, pv)
                        bank = ob.wait_free(pe, t, use)
                        ob.now_full(transposes(bank, [oTs[:, i * P:(i + 1) * P] for i in range(NT)]), use)

                    def o_transposed(t, c):
                        if c == 0:
                            ob.wait_moved(pe, t, "ot3-")
                        bank = ob.wait_free(pe, t, f"t{c}-")
                        ob.now_full(transposes(bank, [otok[:, i, c * P:(c + 1) * P] for i in range(NT)]), f"t{c}-")

                    def o_proj(t, k):
                        if k == 0:
                            for c in range(KC):
                                ob.wait_moved(pe, t, f"t{c}-")
                        bank = ob.wait_free(pe, t, f"wo{k}-")
                        for i in range(2):
                            tok = slice((2 * k + i) * P, (2 * k + i + 1) * P)
                            for c in range(KC):
                                last = mm(bank[:, i * DO:(i + 1) * DO], oT[:, c, tok], wo[:, c, :], start=(c == 0), stop=(c == KC - 1))
                        ob.now_full(last, f"wo{k}-")

                    def turn(t, tail, att, nxt, qkv, mix):
                        fb.start(pe, t)
                        ob.start(pe, t)
                        for slot in range(PU):
                            p, n = slot // UNITS, slot % UNITS
                            if att is not None:
                                scores(att, p, n)
                            if of_pair(att, nxt, p + 2) is not None:
                                scores_for_max(*of_pair(att, nxt, p + 2), n)
                            if slot == 0 and tail is not None:
                                values_summed(t, tail, 3, "pv3-")
                            if n == 0 and p in (2, 4, 6) and att is not None:
                                values_summed(t, att, p // 2 - 1, f"pv{p // 2 - 1}")
                            if n == 1 and of_pair(att, nxt, p + 1) is not None:
                                max_transposed(t, *of_pair(att, nxt, p + 1), p + 1)
                            if slot == 2 and tail is not None:
                                o_back(t, "pv3-", "ot3-")
                            if n == 2 and p in (2, 4, 6) and att is not None:
                                o_back(t, f"pv{p // 2 - 1}", f"ot{p // 2 - 1}")
                            if slot in (4, 5) and tail is not None:
                                o_transposed(t, slot - 4)
                            if slot in (7, 8) and tail is not None:
                                o_proj(t, slot - 7)
                            if mix is not None:
                                if slot == S_ZT:
                                    z_transposes(t, mix, z, "zt", z_ready)
                                if S_IN <= slot < S_IN + 2 * IC:
                                    in_proj(t, slot - S_IN)
                                if slot == S_GATE:
                                    gate(t, mix)
                                for k in range(2):
                                    if slot == S_OUT[k]:
                                        out_proj(t, mix, k, 0)
                                        out_proj(t, mix, k, 1)
                            if qkv is not None:
                                if slot == S_HT:
                                    z_transposes(t, qkv, hz, "ht", hz_ready)
                                if S_QK <= slot < S_QK + NT:
                                    qk(t, slot - S_QK)
                                if slot in (S_V, S_V + 1):
                                    for i in range(2 * (slot - S_V), 2 * (slot - S_V) + 2):
                                        qkv_product(t, f"v{i}", i, slice(2 * D, 3 * D))
                                if slot in (S_QT, S_QT + 1):
                                    for c in range(2 * (slot - S_QT), 2 * (slot - S_QT) + 2):
                                        qk_transposes(t, qkv, c)
                        fb.finish(pe)
                        ob.finish(pe)

                    all_turns(pe, turn)

        experts(nc, ctx, d, banks, x1_dram, xr_dram, out_dram)


def experts(nc, ctx, d, banks, x1_dram, xr_dram, out_dram):
    B, _, NT, D = out_dram.shape
    T = NT * P
    KC = D // P
    HC = d["e0_down"].shape[1]
    DO = d["e0_down"].shape[2]
    ZM = D - DO
    E = 4
    LARGEST = 3.4028234663852886e38

    def sb(name, shape, dt=F32):
        return ctx.enter_context(nc.sbuf_tensor(name, shape, dt))

    def sem(name):
        return ctx.enter_context(nc.semaphore(name))

    UPS = ["e2_l1", "e0_up", "e2_l2", "e3_down", "e1_w1", "e1_w2", "e2_l3", "e3_up"]
    DOWNS = ["e0_down", "e1_down", "e2_l4", "e3_out"]
    up_h = {n: sb(n + "_h", [P, *d[n].shape[1:]], F32R) for n in UPS}
    up_l = {n: sb(n + "_l", [P, *d[n].shape[1:]], F32R) for n in UPS}
    down = {n: sb(n + "_sb", [P, HC, DO]) for n in DOWNS}
    gate_w = sb("gate_w_sb", [P, KC, E])
    n2_w = sb("n2_w_sb", [P, KC])
    ident = sb("ident2", [P, P])
    minus_half = sb("minus_half2", [P, NT])

    WORK = 4 * HC * T + 5 * T
    work = sb("work", [P, max(WORK, sum(d[n].shape[1] * d[n].shape[2] for n in UPS))])
    hid = [work[:, e * HC * T:(e + 1) * HC * T].rearrange("p (c t) -> p c t", t=T) for e in range(4)]
    gates = work[:, 4 * HC * T:4 * HC * T + 2 * T].rearrange("p (s t) -> p s t", t=T)
    exact = work[:, 4 * HC * T + 2 * T:4 * HC * T + 5 * T].rearrange("p (s t) -> p s t", t=T)
    stage, at = {}, 0
    for n in UPS:
        size = d[n].shape[1] * d[n].shape[2]
        stage[n] = work[:, at:at + size].rearrange("p (k n) -> p k n", k=d[n].shape[1])
        at += size
    h1 = sb("h1_h", [P, HC, T], F32R), sb("h1_l", [P, HC, T], F32R)
    h2 = sb("h2_h", [P, HC, T], F32R), sb("h2_l", [P, HC, T], F32R)
    h3 = sb("h3_h", [P, KC, T], F32R), sb("h3_l", [P, KC, T], F32R)
    xf = sb("xf_h", [P, KC, T], F32R), sb("xf_l", [P, KC, T], F32R)
    xr = sb("xr_sb", [P, 2, NT, D])
    x1 = sb("x1_sb", [P, 2, NT, D])
    xz = sb("xz", [P, NT, D])
    ssx, e1, r2, rf, ef = (sb(n, [P, NT]) for n in ("ssx", "e_rms", "r_rms", "r_f", "e_f"))
    st6, mvf = sb("st6_f", [P, NT, 6]), sb("mv_f", [P, NT, 2])
    raw, lg, dl, ex, pr, wts = (sb(n, [P, NT, E]) for n in ("raw", "lg", "dl", "ex", "pr", "wts"))
    finite = sb("finite", [P, NT, E], U32)
    beats = sb("beats", [P, NT, E, E])
    rank = sb("rank", [P, NT, E])
    m1, s1, i1, s2, i2 = (sb(n, [P, NT]) for n in ("m1", "s1", "i1", "s2", "i2"))

    up_units = [("e2_l1", m, "xf", "split") for m in range(HC)] + [("e0_up", m, "xf", 0) for m in range(HC)]
    up_units += [("e2_l2", m, "h1", "split") for m in range(HC)] + [("e3_down", m, "xf", "split") for m in range(KC)]
    for m in range(HC):
        up_units += [("e1_w1", m, "xf", "silu"), ("e1_w2", m, "xf", "times")]
    up_units += [("e2_l3", m, "h2", 2) for m in range(HC)] + [("e3_up", m, "h3", 3) for m in range(HC)]
    moving = {"xf": xf, "h1": h1, "h2": h2, "h3": h3}
    split_into = {"e2_l1": h1, "e2_l2": h2, "e3_down": h3}
    UB = Banks(banks[0:4], [sem(f"up_full{i}") for i in range(4)], [sem(f"up_moved{i}") for i in range(4)],
               2 + len(up_units))
    DB = Banks(banks[4:7], [sem(f"down_full{i}") for i in range(3)], [sem(f"down_moved{i}") for i in range(3)], 9)
    down_order = [0, 1, 3, 2]
    D_USE = {(e, k): 1 + 2 * n + k for n, e in enumerate(down_order) for k in range(2)}

    w_in = [sem(f"w_in{i}") for i in range(len(UPS))]
    w2_loaded, consts2, w_hi2, w_lo2 = sem("w2_loaded"), sem("consts2"), sem("w_hi2"), sem("w_lo2")
    x_in = [sem("x_in0"), sem("x_in1")]
    sq_in, rms_scale, xz_ready, xf_hi = sem("sq_in"), sem("rms_scale"), sem("xz_ready"), sem("xf_hi")
    exact_ready, lo_ready = sem("exact_ready"), sem("lo_ready")
    shifted, ex_ready = sem("shifted"), sem("ex_ready")
    f_stats, f_scale, out_ready = sem("f_stats"), sem("f_scale"), sem("out_ready")
    stored = [sem("stored0"), sem("stored1")]
    dve2, pool_e1, pool_ef = sem("dve2"), sem("pool_e1"), sem("pool_ef")
    passed2 = sem("passed2")
    SPLITS = 2 * HC + KC

    def each_batch(eng, turn):
        with eng.Fori(0, B // 2 - 1) as k:
            turn(2 * k, 2 * k + 1, 0)
            turn(2 * k + 1, 2 * k + 2, 1)
        turn(B - 2, B - 1, 0)
        turn(B - 1, None, 1)

    with nc.Block() as block:

        @block.sync
        def _(sp):
            for n, s in zip(UPS, w_in):
                sp.dma_start(stage[n], d[n]).then_inc(s, 16)
            for dst, src in [(down[n][:], d[n]) for n in DOWNS] + [(gate_w[:], d["gate_w"]), (n2_w[:], d["n2_w"])]:
                sp.dma_start(dst, src).then_inc(w2_loaded, 16)

            def load(b, par):
                sp.dma_start(xr[:, par, :, :], of_batch(xr_dram, b)).then_inc(x_in[par], 16)
                sp.dma_start(x1[:, par, :, :], of_batch(x1_dram, b)).then_inc(x_in[par], 16)

            load(0, 0)
            load(1, 1)
            with sp.Fori(0, B // 2 - 1) as k:
                for par in range(2):
                    b = 2 * k + par
                    sp.wait_ge(out_ready, b + 1)
                    alone(sp, passed2)
                    sp.dma_start(of_batch(out_dram, b), x1[:, par, :, :]).then_inc(stored[par], 16)
                    sp.wait_ge(stored[par], 16 * k + 16)
                    alone(sp, passed2)
                    load(b + 2, par)
            for par in range(2):
                sp.wait_ge(out_ready, B - 2 + par + 1)
                sp.dma_start(of_batch(out_dram, B - 2 + par), x1[:, par, :, :]).then_inc(stored[par], 16)
            for par in range(2):
                sp.wait_ge(stored[par], 16 * (B // 2))

        def wait_loaded(eng, b, par):
            eng.wait_ge(x_in[par], 16 * b - 16 * par + 32)

        @block.gpsimd
        def _(pool):
            nc.gpsimd.memset(ident[:], 0.0)
            nc.gpsimd.memset(minus_half[:], -0.5)
            nc.gpsimd.memset(beats[:], 0.0).then_inc(consts2, 1)
            pool.wait_ge(consts2, 1)
            nc.gpsimd.affine_select(out=ident[:], in_=ident[:], compare_op=ALU.not_equal, fill=1.0,
                                    base=0, pattern=[[-1, P]], channel_multiplier=1).then_inc(consts2, 1)
            tt, ts = nc.gpsimd.tensor_tensor, nc.gpsimd.tensor_scalar

            def head(b):
                pool.wait_ge(sq_in, b + 1)
                alone(pool, passed2)
                ts(e1[:], ssx[:], 1.0 / D, EPS_RMS, op0=ALU.mult, op1=ALU.add).then_inc(pool_e1, 1)
                pool.wait_ge(pool_e1, b + 1)
                tt(r2[:], e1[:], minus_half[:], ALU.pow).then_inc(rms_scale, 1)

            def turn(b, nxt, par):
                if nxt is not None:
                    head(nxt)
                pool.wait_ge(f_stats, b + 1)
                alone(pool, passed2)
                ts(ef[:], mvf[:, :, 1], EPS_LN, None, op0=ALU.add).then_inc(pool_ef, 1)
                pool.wait_ge(pool_ef, b + 1)
                tt(rf[:], ef[:], minus_half[:], ALU.pow).then_inc(f_scale, 1)

            head(0)
            each_batch(pool, turn)

        @block.scalar
        def _(act):
            activation, copy = nc.scalar.activation, ACT.Copy
            for s in UB.moved + DB.moved:
                act.sem_inc(s, 1)

            def head(b, par):
                wait_loaded(act, b, par)
                for i in range(NT):
                    ins = activation(xz[:, i, :], xr[:, par, i, :], ACT.Square, accum_out=ssx[:, i:i + 1])
                ins.then_inc(sq_in, 1)

            def move_xf_hi(b):
                for c in range(KC):
                    t = UB.wait_full(act, b, c)
                    activation(xf[0][:, c, :], t[:], copy, scale=n2_w[:, c:c + 1]).then_inc(xf_hi, 1)

            def up(b, n, count):
                name, m, _, kind = up_units[n]
                t = UB.wait_full(act, b, 2 + n)
                if kind == "split":
                    k = count["split"]
                    count["split"] += 1
                    act.wait_ge(lo_ready, b * SPLITS + k + 1)
                    activation(exact[:, k % 2, :], t[:], ACT.Gelu).then_inc(exact_ready, 1)
                    UB.now_moved(activation(split_into[name][0][:, m, :], t[:], ACT.Gelu), 2 + n)
                elif kind == "silu":
                    if m >= 2:
                        UB.wait_moved(act, b, 2 + n - 3)
                    UB.now_moved(activation(gates[:, m % 2, :], t[:], ACT.Silu), 2 + n)
                elif kind != "times":
                    UB.now_moved(activation(hid[kind][:, m, :], t[:], ACT.Gelu), 2 + n)

            def turn(b, nxt, par):
                count = {"split": 0}
                for n in range(3 * HC + KC):
                    up(b, n, count)
                act.wait_ge(shifted, b + 1)
                activation(ex[:], dl[:], ACT.Exp).then_inc(ex_ready, 1)
                if nxt is not None:
                    head(nxt, 1 - par)
                for n in range(3 * HC + KC, len(up_units)):
                    up(b, n, count)
                if nxt is not None:
                    move_xf_hi(nxt)

            for n, s in zip(UPS, w_in):
                act.wait_ge(s, 16)
                activation(up_h[n][:], stage[n], copy).then_inc(w_hi2, 1)
            act.wait_ge(w2_loaded, 16 * (len(DOWNS) + 2))
            act.wait_ge(w_lo2, len(UPS))
            head(0, 0)
            move_xf_hi(0)
            each_batch(act, turn)

        @block.vector
        def _(dve):
            tt, ts, stt = nc.vector.tensor_tensor, nc.vector.tensor_scalar, nc.vector.scalar_tensor_tensor
            reduce = nc.vector.tensor_reduce
            link = Links(dve, dve2, 16)
            dve.sem_inc(lo_ready, 2)

            def head(b, par):
                dve.wait_ge(rms_scale, b + 1)
                wait_loaded(dve, b, par)
                for i in range(NT):
                    last = ts(xz[:, i, :], xr[:, par, i, :], r2[:, i:i + 1], None, op0=ALU.mult)
                last.then_inc(xz_ready, 1)

            def move_xf_lo(b):
                for c in range(KC):
                    t = UB.wait_full(dve, b, c)
                    dve.wait_ge(xf_hi, b * KC + c + 1)
                    UB.now_moved(stt(xf[1][:, c, :], t[:], n2_w[:, c:c + 1], xf[0][:, c, :].bitcast(F32),
                                     ALU.mult, ALU.subtract), c)

            def wide(a):
                return a.unsqueeze(2).to_broadcast([P, NT, E])

            def logits(b):
                t = DB.wait_full(dve, b, 0)
                nc.vector.memset(lg[:], 0.0)
                ins = nc.vector.tensor_copy(raw[:], t[:, 0:NT * E].rearrange("p (i e) -> p i e", e=E))
                DB.now_moved(ins, 0)
                DB.wait_moved(dve, b, 0)
                link(tt(finite[:], raw[:], raw[:], ALU.is_equal))
                alone(dve, passed2)
                link(nc.vector.copy_predicated(lg[:], finite[:], raw[:]))
                link(ts(lg[:], lg[:], LARGEST, -LARGEST, op0=ALU.min, op1=ALU.max))
                link(reduce(m1[:], lg[:], AX.X, ALU.max))
                tt(dl[:], lg[:], wide(m1[:]), ALU.subtract).then_inc(shifted, 1)

            def choose(b):
                dve.wait_ge(ex_ready, b + 1)
                link(reduce(s1[:], ex[:], AX.X, ALU.add))
                link(nc.vector.reciprocal(i1[:], s1[:]))
                link(tt(pr[:], ex[:], wide(i1[:]), ALU.mult))
                for e in range(E):
                    if e > 0:
                        last = tt(beats[:, :, e, 0:e], pr[:, :, 0:e], pr[:, :, e:e + 1].to_broadcast([P, NT, e]), ALU.is_ge)
                    if e < E - 1:
                        last = tt(beats[:, :, e, e + 1:], pr[:, :, e + 1:], pr[:, :, e:e + 1].to_broadcast([P, NT, E - 1 - e]), ALU.is_gt)
                link(last)
                link(reduce(rank[:], beats[:], AX.X, ALU.add))
                link(stt(wts[:], rank[:], 2.0, pr[:], ALU.is_lt, ALU.mult))
                link(reduce(s2[:], wts[:], AX.X, ALU.add))
                link(ts(s2[:], s2[:], 1e-8, None, op0=ALU.add))
                link(nc.vector.reciprocal(i2[:], s2[:]))
                link(tt(wts[:], wts[:], wide(i2[:]), ALU.mult))

            def up(b, n, count):
                name, m, _, kind = up_units[n]
                if kind == "split":
                    k = count["split"]
                    count["split"] += 1
                    dve.wait_ge(exact_ready, b * SPLITS + k + 1)
                    UB.wait_moved(dve, b, 2 + n)
                    tt(split_into[name][1][:, m, :], exact[:, k % 2, :], split_into[name][0][:, m, :].bitcast(F32),
                       ALU.subtract).then_inc(lo_ready, 1)
                elif kind == "times":
                    t = UB.wait_full(dve, b, 2 + n)
                    UB.wait_moved(dve, b, 1 + n)
                    UB.now_moved(tt(hid[1][:, m, :], t[:], gates[:, m % 2, :], ALU.mult), 2 + n)

            def combine(b, par):
                for n, e in enumerate(down_order):
                    for k in range(2):
                        t = DB.wait_full(dve, b, D_USE[e, k])
                        if n > 0:
                            DB.wait_moved(dve, b, D_USE[down_order[n - 1], k])
                        for i in range(2):
                            acc = xr[:, par, 2 * k + i, ZM:]
                            last = stt(acc, t[:, i * DO:(i + 1) * DO], wts[:, 2 * k + i, e:e + 1], acc, ALU.mult, ALU.add)
                        DB.now_moved(last, D_USE[e, k])

            def last_norm(b, par):
                for k in range(2):
                    DB.wait_moved(dve, b, D_USE[down_order[-1], k])
                for i in range(NT):
                    last = nc.vector.bn_stats(st6[:, i, :], xr[:, par, i, :])
                link(last)
                alone(dve, passed2)
                for i in range(NT):
                    last = nc.vector.bn_aggr(mvf[:, i, :], st6[:, i, :])
                last.then_inc(f_stats, 1)
                dve.wait_ge(f_scale, b + 1)
                for i in range(NT):
                    last = ts(xr[:, par, i, :], xr[:, par, i, :], mvf[:, i, 0:1], rf[:, i:i + 1], op0=ALU.subtract, op1=ALU.mult)
                link(last)
                tt(x1[:, par, :, :], x1[:, par, :, :], xr[:, par, :, :], ALU.add).then_inc(out_ready, 1)

            def turn(b, nxt, par):
                link.batch(b)
                count = {"split": 0}
                logits(b)
                for n in range(3 * HC + KC):
                    up(b, n, count)
                choose(b)
                if nxt is not None:
                    head(nxt, 1 - par)
                for n in range(3 * HC + KC, len(up_units)):
                    up(b, n, count)
                if nxt is not None:
                    move_xf_lo(nxt)
                combine(b, par)
                last_norm(b, par)

            dve.wait_ge(consts2, 2)
            for n, name in enumerate(UPS):
                dve.wait_ge(w_hi2, n + 1)
                tt(up_l[name][:], stage[name], up_h[name][:].bitcast(F32), ALU.subtract).then_inc(w_lo2, 1)
            head(0, 0)
            move_xf_lo(0)
            each_batch(dve, turn)

        @block.tensor
        def _(pe):
            mm = nc.tensor.matmul

            def xf_transposes(b):
                pe.wait_ge(xz_ready, b + 1)
                for c in range(KC):
                    t = UB.wait_free(pe, b, c)
                    for i in range(NT):
                        last = nc.tensor.transpose(t[:, i * P:(i + 1) * P], xz[:, i, c * P:(c + 1) * P], ident[:])
                    UB.now_full(last, c)

            def gate(b):
                for c in range(KC):
                    UB.wait_moved(pe, b, c)
                t = DB.wait_free(pe, b, 0)
                for i in range(NT):
                    for c in range(KC):
                        for s in range(2):
                            last = mm(t[:, i * E:(i + 1) * E], xf[s][:, c, i * P:(i + 1) * P].bitcast(F32), gate_w[:, c, :],
                                      start=(c == 0 and s == 0), stop=(c == KC - 1 and s == 1))
                DB.now_full(last, 0)

            def up(b, n):
                name, m, source, _ = up_units[n]
                if m == 0 and source == "h1":
                    pe.wait_ge(lo_ready, b * SPLITS + HC + 2)
                if m == 0 and source == "h2":
                    pe.wait_ge(lo_ready, b * SPLITS + 2 * HC + 2)
                if m == 0 and source == "h3":
                    pe.wait_ge(lo_ready, b * SPLITS + SPLITS + 2)
                t = UB.wait_free(pe, b, 2 + n)
                cols, chunks = slice(m * P, (m + 1) * P), d[name].shape[1]
                for c in range(chunks):
                    for j, (s, v) in enumerate(((0, 0), (0, 1), (1, 0))):
                        w = (up_h, up_l)[s][name][:, c, cols]
                        last = mm(t[:], w, moving[source][v][:, c, :], start=(c == 0 and j == 0), stop=(c == chunks - 1 and j == 2))
                UB.now_full(last, 2 + n)

            def downs(b, e):
                units = [n for n, u in enumerate(up_units) if u[3] == (e if e != 1 else "times")]
                for n in {(2 + n) % UB.n: n for n in units}.values():
                    UB.wait_moved(pe, b, 2 + n)
                w = down[DOWNS[e]]
                for k in range(2):
                    t = DB.wait_free(pe, b, D_USE[e, k])
                    for i in range(2):
                        tok = slice((2 * k + i) * P, (2 * k + i + 1) * P)
                        for c in range(HC):
                            last = mm(t[:, i * DO:(i + 1) * DO], hid[e][:, c, tok], w[:, c, :], start=(c == 0), stop=(c == HC - 1))
                    DB.now_full(last, D_USE[e, k])

            def turn(b, nxt, par):
                gate(b)
                for n in range(len(up_units)):
                    up(b, n)
                if nxt is not None:
                    xf_transposes(nxt)
                for e in down_order:
                    downs(b, e)

            pe.wait_ge(consts2, 2)
            pe.wait_ge(w2_loaded, 16 * (len(DOWNS) + 2))
            pe.wait_ge(w_lo2, len(UPS))
            xf_transposes(0)
            each_batch(pe, turn)


_FFN = ["e0_up", "e0_down", "e1_w1", "e1_w2", "e1_down", "e2_l1", "e2_l2", "e2_l3", "e2_l4", "e3_down", "e3_up", "e3_out"]


def kernel(**inputs):
    import numpy as np
    import concourse.bacc as bacc
    from concourse.bass_utils import run_bass_kernel_spmd

    a = {n[3:]: np.asarray(v) for n, v in inputs.items()}

    def by_partition(w):
        return np.ascontiguousarray(w.reshape(w.shape[0] // P, P, -1).transpose(1, 0, 2))

    def columns(v):
        return v.reshape(-1, P).T

    zm = 64
    conv = a["attn_conv_w"][:, 0, :].reshape(-1, P, 4).transpose(1, 0, 2).reshape(P, -1)
    arrays = {
        "x": np.ascontiguousarray(a["attn_x"]),
        "in_w": by_partition(a["attn_in_w"].T),
        "wqkv": by_partition(np.concatenate([a["ffn_wq"].T, a["ffn_wk"].T, a["ffn_wv"].T], axis=1)),
        "out_w": by_partition(a["attn_out_w"].T),
        "wo": by_partition(a["ffn_wo"].T[:, zm:]),
        "xproj_w": by_partition(a["attn_xproj_w"].T),
        "vecs": np.ascontiguousarray(np.concatenate([
            columns(a["attn_norm_w"]), columns(a["attn_norm_b"]), columns(a["attn_in_b"]), conv,
            columns(a["attn_conv_b"]), columns(a["attn_D"]), columns(a["ffn_n1_w"]),
            np.tile(a["ffn_qn_w"], 8)[:, None], np.tile(a["ffn_kn_w"], 8)[:, None]], axis=1)),
        "out_b": np.ascontiguousarray(np.broadcast_to(a["attn_out_b"], (P, a["attn_out_b"].shape[0]))),
        "gate_w": by_partition(a["ffn_gate_w"].T),
        "n2_w": np.ascontiguousarray(columns(a["ffn_n2_w"])),
    }
    for n in _FFN:
        w = a["ffn_" + n].T
        arrays[n] = by_partition(w[:, zm:] if n in ("e0_down", "e1_down", "e2_l4", "e3_out") else w)

    nc = bacc.Bacc("TRN2", target_bir_lowering=False, num_devices=1)
    d = {n: nc.dram_tensor("in_" + n, v.shape, F32, kind="ExternalInput").ap() for n, v in arrays.items()}
    shape = arrays["x"].shape
    scratch = [nc.dram_tensor(n, shape, F32, kind="Internal").ap() for n in ("x1_dram", "xr_dram")]
    heads = (shape[0], 8, 2, 16, 2, shape[1]), (shape[0], 8, 16, 2, 2, shape[1])
    scratch += [nc.dram_tensor(n, s, F32, kind="Internal").ap() for n, s in zip(("q_dram", "k_dram"), heads)]
    out = nc.dram_tensor("out", shape, F32, kind="ExternalOutput").ap()
    mixer_attention_experts(nc, d, scratch, out)
    r = run_bass_kernel_spmd(nc, [{"in_" + n: v for n, v in arrays.items()}], core_ids=[0])
    return r.results[0]["out"]
```

```python
from contextlib import ExitStack

import concourse.bass as bass
from concourse import mybir

F32 = mybir.dt.float32
F32R = mybir.dt.float32r
BF16 = mybir.dt.bfloat16
U32 = mybir.dt.uint32
I32 = mybir.dt.int32
ACT = mybir.ActivationFunctionType
ALU = mybir.AluOpType
AX = mybir.AxisListType

P = 128
EPS_LN = 1e-5
EPS_RMS = 1.1920929e-07
MASKED = -1e30


class Links:

    def __init__(self, eng, sem, per):
        self.eng, self.sem, self.per, self.base, self.k = eng, sem, per, 0, 0

    def batch(self, b):
        assert self.k in (0, self.per), (self.k, self.per)
        self.base, self.k = b * self.per, 0

    def __call__(self, ins):
        self.k += 1
        ins.then_inc(self.sem, 1)
        self.eng.wait_ge(self.sem, self.base + self.k)


class Banks:

    def __init__(self, tiles, full, moved, uses):
        self.tiles, self.full, self.moved = tiles, full, moved
        self.n = len(tiles)
        self.order = {} if isinstance(uses, int) else {name: n for n, name in enumerate(uses)}
        self.uses = len(self.order) or uses
        assert self.uses % self.n == 0
        self.per = self.uses // self.n
        self.turn, self.next = None, None

    def at(self, use):
        n = self.order.get(use, use)
        return n % self.n, n // self.n

    def tile(self, use):
        return self.tiles[self.at(use)[0]]

    def wait_free(self, eng, b, use):
        if self.next is not None:
            self.pass_over(eng, self.order[use])
            self.next += 1
        i, k = self.at(use)
        eng.wait_ge(self.moved[i], b * self.per + k + 1)
        return self.tiles[i]

    def wait_full(self, eng, b, use):
        i, k = self.at(use)
        eng.wait_ge(self.full[i], b * self.per + k + 1)
        return self.tiles[i]

    def wait_moved(self, eng, b, use):
        i, k = self.at(use)
        eng.wait_ge(self.moved[i], b * self.per + k + 2)

    def now_full(self, ins, use):
        ins.then_inc(self.full[self.at(use)[0]], 1)

    def now_moved(self, ins, use):
        ins.then_inc(self.moved[self.at(use)[0]], 1)

    def start(self, eng, b):
        self.turn, self.next = b, 0

    def pass_over(self, eng, upto):
        for n in range(self.next, upto):
            i, k = self.at(n)
            eng.wait_ge(self.moved[i], self.turn * self.per + k + 1)
            eng.sem_inc(self.full[i], 1)
            eng.sem_inc(self.moved[i], 1)
        assert self.next <= upto
        self.next = upto

    def finish(self, eng):
        self.pass_over(eng, self.uses)


def alone(eng, passed):
    eng.sem_inc(passed, 1)


def one(b):
    return slice(b, b + 1) if isinstance(b, int) else bass.ds(b, 1)


def of_batch(t, b):
    return t[b] if isinstance(b, int) else t[bass.ds(b, 1)].rearrange("b p i d -> (b p) i d")


def mixer_attention_experts(nc, d, scratch, out):
    B, T, D = d["x"].shape
    NT = T // P
    KC = D // P
    DI = d["out_w"].shape[1] * P
    IC = DI // P
    HD = 16
    H = D // HD
    CH = P // HD
    NPAIR = H // 2
    NQUAD = H // 4
    ZM = 64
    DO = D - ZM
    SR = 96
    SLOTS = 4
    PTS = 20
    UNITS = 5

    x_dram, out_dram = (t.rearrange("b (i p) d -> b p i d", p=P) for t in (d["x"], out))
    x1_dram, xr_dram = (t.rearrange("b (i p) d -> b p i d", p=P) for t in scratch[0:2])
    q_dram, k_dram = scratch[2:4]

    with ExitStack() as ctx:
        def sem(name):
            return ctx.enter_context(nc.semaphore(name))

        def psum(name):
            return ctx.enter_context(nc.psum_tensor(name, [P, T], F32))

        banks = [psum(f"bank{i}") for i in range(8)]

        with ExitStack() as first:
            def sb(name, shape, dt=F32):
                return first.enter_context(nc.sbuf_tensor(name, shape, dt))

            ident = sb("ident", [P, P])
            ident16 = sb("ident16", [P, P], BF16)
            mask_q = sb("mask_q", [P, P], BF16)
            mask_k = sb("mask_k", [P, P], BF16)
            minus_half = sb("minus_half", [P, NT])
            win_h, win_l = sb("win_h", [P, KC, 2 * DI], F32R), sb("win_l", [P, KC, 2 * DI], F32R)
            wqkv_h, wqkv_l = sb("wqkv_h", [P, KC, 3 * D], F32R), sb("wqkv_l", [P, KC, 3 * D], F32R)
            wout = sb("wout", [P, IC, D])
            wo = sb("wo", [P, KC, DO])
            wgate = sb("wgate", [P, IC, P])
            gate_col = sb("gate_col", [P, IC])
            vecs = sb("vecs", [P, d["vecs"].shape[1]])
            at = {}
            col = 0
            for name, n in (("norm_w", KC), ("norm_b", KC), ("in_b", 2 * IC), ("conv_w", 4 * IC),
                            ("conv_b", IC), ("D", IC), ("n1_w", KC), ("qn_w", 1), ("kn_w", 1)):
                at[name] = vecs[:, col:col + n]
                col += n
            b_in = sb("b_in", [P, 2 * IC])
            d2 = sb("d2", [P, IC])
            out_b = sb("out_b", [P, D])

            x = sb("x_sb", [P, NT, D])
            u = sb("u", [P, NT, D])
            z = sb("z", [P, NT, D])
            zT_h, zT_l = sb("zT_h", [P, KC, T], F32R), sb("zT_l", [P, KC, T], F32R)
            xi = sb("xi", [P, IC, T + 3])
            xc = sb("xc", [P, IC, T])
            xin = xc[:, 0:2, :].rearrange("p c t -> p (c t)").rearrange("p (i d) -> p i d", d=D)
            sz = sb("sz", [P, IC, T])
            th = sb("th", [P, T])
            st6 = sb("st6", [P, NT, 6])
            mv = sb("mv", [P, NT, 2])
            mv1 = sb("mv1", [P, NT, 2])
            mvf = sb("mvf", [P, NT, 2])
            sm = sb("sm", [P, 8, NT])

            hz = sb("hz", [P, NT, D])
            qk_raw = sb("qk_raw", [P, NT, 2 * D])
            sq = sb("sq", [P, 2, T])
            ms, rqk, nt = (sb(n, [P, NT * 2 * H]) for n in ("ms", "rqk", "nt"))
            qkT = sb("qkT", [P, 2, 2, T], F32R)
            v2 = sb("v2", [P, NT, D])

            v = sb("v", [P, NT, H, 32])
            qS, kS = sb("qS", [P, SLOTS, 2, T], F32R), sb("kS", [P, SLOTS, 2, T], F32R)
            mxs = sb("mxs", [P, 2, 8])
            nm = sb("nm", [P, 2, 16], F32R)
            nmT = sb("nmT", [16, 2, P], F32R)
            pt = sb("pt", [P, PTS, T])
            oTs = sb("oTs", [P, T])
            rc = sb("rc", [P, NT, 4])
            otok = sb("otok", [P, NT, D])
            oT = sb("oT", [P, KC, T])

            w_stage = pt[:, 0:8, :].rearrange("p s t -> p (s t)")
            win_f = w_stage[:, 0:KC * 2 * DI].rearrange("p (k n) -> p k n", k=KC)
            wqkv_f = w_stage[:, KC * 2 * DI:KC * 2 * DI + KC * 3 * D].rearrange("p (k n) -> p k n", k=KC)
            wc = pt[:, 8:8 + IC * HD // T + 1, :].rearrange("p s t -> p (s t)")[:, 0:IC * HD].rearrange("p (c d) -> p c d", c=IC)

            MT = 1
            FRONT = {"zt": [0, 0], "in": [2, 3, 4, 5, 6, 7, 8, 9], "ht": [12, 12], "gate": [15],
                     "qk": [14, 14, 14, 16], "v": [26, 27, 28, 29], "qt": [22, 22, 24, 24], "out": [18, 20]}
            ODD = {"pv-": [0], "ot-": [3], "t-": [7, 9], "wo-": [12, 17], "pv": [14, 25, 34], "ot": [22, 28, 37],
                   "mt": [UNITS * p + MT for p in range(NPAIR)]}
            SILU, Y, STATS_OUT, X1, HZ, STATS, NORM = 13, 16, 23, 25, 32, 33, 38
            GUESS, NEWTON, SCALE = 17, (18, 18), 19

            def due(table, name, slot):
                return [i for i, s in enumerate(table[name]) if s == slot]

            def in_order(table):
                return [f"{name}{i}" for slot in range(NPAIR * UNITS) for name in table for i in due(table, name, slot)]

            f_order, o_order = in_order(FRONT), in_order(ODD)
            fb = Banks(banks[0:3], [sem(f"front_full{i}") for i in range(3)],
                       [sem(f"front_moved{i}") for i in range(3)], f_order)
            ob = Banks(banks[3:4], [sem("o_full")], [sem("o_moved")], o_order)
            mx_bank, st_bank = banks[4:6], banks[6:8]
            mx_full, mx_read = sem("mx_full"), sem("mx_read")
            st_full, exp_done = sem("st_full"), sem("exp_done")

            w_loaded, rest_loaded, consts, w_hi, w_lo, bias_mm, w_ready = (
                sem(n) for n in ("w_loaded", "rest_loaded", "consts", "w_hi", "w_lo", "bias_mm", "w_ready"))
            x_loaded, x1_stored, xin_stored = sem("x_loaded"), sem("x1_stored"), sem("xin_stored")
            stats, scales, z_ready, z_hi = sem("stats"), sem("scales"), sem("z_ready"), sem("z_hi")
            conv_done, silu_done, p_ready, y_ready = (
                sem(n) for n in ("conv_done", "silu_done", "p_ready", "y_ready"))
            ub_ready, x1_ready, xin_ready, hz_ready = sem("ub_ready"), sem("x1_ready"), sem("xin_ready"), sem("hz_ready")
            h_hi, sq_summed, qk_normed, qk_hi = sem("h_hi"), sem("sq_summed"), sem("qk_normed"), sem("qk_hi")
            qk_out = [sem("qk_out0"), sem("qk_out1")]
            v_placed = sem("v_placed")
            stacked = [sem(f"stacked{i}") for i in range(SLOTS)]
            nm_ready = sem("nm_ready")
            rows = [sem("rows0"), sem("rows1")]
            o_sums, res_loaded, xr_stored = sem("o_sums"), sem("res_loaded"), sem("xr_stored")
            dve_mix, dve_qk, dve_pre = sem("dve_mix"), sem("dve_qk"), sem("dve_pre")
            pool_mix, pool_pre = sem("pool_mix"), sem("pool_pre")
            pool_x, pool_u, dve_x = sem("pool_x"), sem("pool_u"), sem("dve_x")
            passed = sem("passed")

            def units(descending):
                w = (lambda i: (i + 1) * P) if descending else (lambda j: (NT - j) * P)
                full, three, two, one = (3, 2, 1, 0) if descending else (0, 1, 2, 3)
                res = []
                for h in range(2):
                    res.append([(h, full, 0, w(full))])
                    res.append([(h, three, 0, w(three)), (h, one, w(three), w(one))])
                res.append([(0, two, 0, w(two)), (1, two, w(two), w(two))])
                return res

            MAX_UNITS, ST_UNITS = units(True), units(False)
            PU = NPAIR * UNITS
            pt_at = {}
            for n, unit in enumerate(ST_UNITS):
                for h, j, c, w in unit:
                    pt_at[h, j] = (n, c, w)

            def all_turns(eng, turn):
                assert B > 4
                turn(0, None, None, None, None, 0)
                turn(1, None, None, 0, 0, 1)
                turn(2, None, 0, 1, 1, 2)
                with eng.Fori(1, B - 3) as a:
                    turn(a + 2, a - 1, a, a + 1, a + 1, a + 2)
                turn(B - 1, B - 4, B - 3, B - 2, B - 2, B - 1)
                turn(B, B - 3, B - 2, B - 1, B - 1, None)
                turn(B + 1, B - 2, B - 1, None, None, None)
                turn(B + 2, B - 1, None, None, None, None)

            def of_pair(att, nxt, pair):
                if pair < NPAIR:
                    return None if att is None else (att, pair)
                return None if nxt is None else (nxt, pair - NPAIR)

            def has_next(b):
                return not isinstance(b, int) or b < B - 1

            def is_first(b):
                return isinstance(b, int) and b == 0

            with nc.Block() as block:

                @block.sync
                def _(sp):
                    for dst, src in ((win_f, d["in_w"]), (vecs[:], d["vecs"])):
                        sp.dma_start(dst, src).then_inc(w_loaded, 16)
                    for dst, src in ((out_b[:], d["out_b"]), (wc, d["xproj_w"][:, :, 1 + HD:1 + 2 * HD]),
                                     (wout[:], d["out_w"]), (wqkv_f, d["wqkv"]), (wo[:], d["wo"])):
                        sp.dma_start(dst, src).then_inc(rest_loaded, 16)

                    def store_qk(t, b):
                        for c in range(4):
                            fb.wait_moved(sp, t, f"qt{c}")
                            alone(sp, passed)
                            for part in range(2):
                                if c < 2:
                                    dst = q_dram[one(b), :, part, :, c, :].rearrange("b r d t -> (b r) d t")
                                else:
                                    dst = k_dram[one(b), :, :, part, c - 2, :].rearrange("b r d t -> (b r) d t")
                                sp.dma_start(dst, qkT[:, c % 2, part, :].bitcast(F32)).then_inc(qk_out[c % 2], 16)

                    def stack(b, pair):
                        s = pair % SLOTS
                        if pair == 0:
                            sp.wait_ge(qk_out[0], 64 * b + 64)
                            sp.wait_ge(qk_out[1], 64 * b + 64)
                            alone(sp, passed)
                        if pair >= SLOTS or not is_first(b):
                            sp.wait_ge(st_full, b * PU + (pair - SLOTS + 1) * UNITS)
                            alone(sp, passed)
                        q = q_dram[one(b), pair].rearrange("b l d h t -> (b l d) (h t)").unsqueeze(1)
                        k = k_dram[one(b), pair].rearrange("b d l h t -> b (d l) (h t)")
                        sp.dma_start(qS[0:4 * HD, s, :, :].bitcast(F32), q.to_broadcast([2 * HD, 2, 2 * T])).then_inc(stacked[s], 16)
                        sp.dma_start(kS[0:4 * HD, s, :, :].bitcast(F32), k.to_broadcast([2, 2 * HD, 2 * T])).then_inc(stacked[s], 16)

                    def max_rows(t, pair, slot_pair):
                        ob.wait_moved(sp, t, f"mt{slot_pair - 1}")
                        sp.dma_start(qS[SR:SR + 2, pair % SLOTS, :, :].bitcast(F32),
                                     nmT[:, pair % 2, :].bitcast(F32)).then_inc(rows[pair % 2], 16)

                    def load_residual(t, b):
                        ob.wait_full(sp, t, "t-1")
                        alone(sp, passed)
                        sp.wait_ge(xin_stored, 16 * (b + 1))
                        alone(sp, passed)
                        sp.dma_start(otok[:], of_batch(xr_dram, b)).then_inc(res_loaded, 16)

                    def store_xr(t, b):
                        ob.wait_moved(sp, t, "wo-1")
                        alone(sp, passed)
                        sp.dma_start(of_batch(xr_dram, b), otok[:]).then_inc(xr_stored, 16)

                    def turn(t, tail, att, nxt, qkv, mix):
                        for p in range(NPAIR):
                            if p == 4 and qkv is not None and att is None:
                                store_qk(t, qkv)
                            if of_pair(att, nxt, p + 1) is not None:
                                max_rows(t, (p + 1) % NPAIR, p + 1)
                            if p == 4 and qkv is not None and att is not None:
                                store_qk(t, qkv)
                            if p == 1 and tail is not None:
                                load_residual(t, tail)
                            if of_pair(att, nxt, p + 4) is not None:
                                stack(*of_pair(att, nxt, p + 4))
                            if p == 3 and tail is not None:
                                store_xr(t, tail)

                    all_turns(sp, turn)
                    sp.wait_ge(xr_stored, 16 * B)

                @block.gpsimd
                def _(pool):
                    pool.dma_start(x[:], of_batch(x_dram, 0)).then_inc(x_loaded, 16)
                    nc.gpsimd.memset(ident[:], 0.0)
                    nc.gpsimd.memset(mask_q[:], 0.0)
                    nc.gpsimd.memset(mask_k[:], 0.0)
                    nc.gpsimd.memset(minus_half[:], -0.5)
                    nc.gpsimd.memset(xi[:, :, 0:3], 0.0).then_inc(pool_pre, 1)
                    pool.wait_ge(pool_pre, 1)
                    nc.gpsimd.affine_select(out=ident[:], in_=ident[:], compare_op=ALU.not_equal, fill=1.0,
                                            base=0, pattern=[[-1, P]], channel_multiplier=1)
                    nc.gpsimd.affine_select(out=mask_q[:], in_=mask_q[:], compare_op=ALU.is_ge, fill=MASKED,
                                            base=0, pattern=[[-1, P]], channel_multiplier=1)
                    nc.gpsimd.affine_select(out=mask_k[:], in_=mask_k[:], compare_op=ALU.is_ge, fill=MASKED,
                                            base=0, pattern=[[1, P]], channel_multiplier=-1).then_inc(pool_pre, 1)
                    pool.wait_ge(pool_pre, 2)
                    nc.gpsimd.tensor_copy(ident16[:], ident[:]).then_inc(consts, 1)
                    link, xlink, ulink = Links(pool, pool_mix, 7), Links(pool, pool_x, 6), Links(pool, pool_u, 1)
                    tt, ts = nc.gpsimd.tensor_tensor, nc.gpsimd.tensor_scalar
                    half = minus_half

                    def two_norms(link, m_v, r0, rs, eps_out):
                        var, e, t = m_v[:, :, 1], sm[:, 6, :], sm[:, 7, :]
                        link(ts(e, var, EPS_LN, None, op0=ALU.add))
                        link(tt(r0, e, half[:], ALU.pow))
                        link(tt(t, var, r0, ALU.mult))
                        link(tt(e, t, r0, ALU.mult))
                        alone(pool, passed)
                        link(ts(t, e, eps_out, None, op0=ALU.add))
                        link(tt(e, t, half[:], ALU.pow))
                        tt(rs, e, r0, ALU.mult).then_inc(scales, 1)

                    def normed(dst, src, m_v, scale):
                        for i in range(NT):
                            last = ts(dst[:, i, :], src[:, i, :], m_v[:, i, 0:1], sm[:, scale, i:i + 1],
                                      op0=ALU.subtract, op1=ALU.mult)
                        return last

                    def load_x(b):
                        pool.wait_ge(x1_ready, b)
                        alone(pool, passed)
                        pool.dma_start(x[:], of_batch(x_dram, b)).then_inc(x_loaded, 16)

                    def scales_of_x(b):
                        pool.wait_ge(stats, b * 3 + 1)
                        alone(pool, passed)
                        two_norms(xlink, mv, sm[:, 0, :], sm[:, 1, :], EPS_LN)

                    def make_u(b):
                        if not is_first(b):
                            pool.wait_ge(x1_stored, 16 * b)
                            alone(pool, passed)
                        ulink.batch(b)
                        ulink(normed(u, x, mv, 0))
                        for i in range(NT):
                            last = tt(u[:, i, :], u[:, i, :], out_b[:], ALU.add)
                        last.then_inc(ub_ready, 1)

                    def place_v(t, b, tail):
                        fb.wait_moved(pool, t - 1, "v3")
                        fb.wait_moved(pool, t - 1, "v2")
                        fb.wait_moved(pool, t - 1, "v1")
                        if tail is not None:
                            ob.wait_full(pool, t, "pv-0")
                        alone(pool, passed)
                        for i in range(NT):
                            last = nc.gpsimd.tensor_copy(v[:, i, :, 0:HD], v2[:, i, :].rearrange("p (h d) -> p h d", d=HD))
                        last.then_inc(v_placed, 1)

                    def turn(t, tail, att, nxt, qkv, mix):
                        if is_first(mix):
                            xlink.batch(mix)
                            scales_of_x(mix)
                            pool.wait_ge(rest_loaded, 16 * 5)
                        if mix is not None:
                            make_u(mix)
                        if is_first(mix):
                            nc.gpsimd.memset(v[:], 1.0)
                        if att is not None:
                            place_v(t, att, tail)
                        if mix is not None:
                            b = mix
                            link.batch(b)
                            pool.wait_ge(silu_done, b + 1)
                            for c in range(IC):
                                last = tt(sz[:, c, :], sz[:, c, :], xc[:, c, :], ALU.mult)
                            last.then_inc(p_ready, 1)
                            pool.wait_ge(stats, b * 3 + 2)
                            alone(pool, passed)
                            link(ts(sm[:, 6, :], mvf[:, :, 1], EPS_LN, None, op0=ALU.add))
                            tt(sm[:, 2, :], sm[:, 6, :], half[:], ALU.pow).then_inc(scales, 1)
                            if has_next(b):
                                load_x(b + 1)
                            pool.wait_ge(stats, b * 3 + 3)
                            alone(pool, passed)
                            two_norms(link, mv1, sm[:, 3, :], sm[:, 4, :], EPS_RMS)
                            if has_next(b):
                                xlink.batch(b + 1)
                                scales_of_x(b + 1)
                            normed(xin, u, mv1, 3).then_inc(xin_ready, 1)
                            pool.dma_start(of_batch(x1_dram, b), u[:]).then_inc(x1_stored, 16)
                            pool.wait_ge(xin_ready, b + 1)
                            alone(pool, passed)
                            pool.dma_start(of_batch(xr_dram, b), xin).then_inc(xin_stored, 16)

                    all_turns(pool, turn)
                    pool.wait_ge(x1_stored, 16 * B)
                    pool.wait_ge(xin_stored, 16 * B)

                @block.scalar
                def _(act):
                    activation, copy = nc.scalar.activation, ACT.Copy
                    for s in fb.moved + ob.moved:
                        act.sem_inc(s, 1)
                    act.sem_inc(exp_done, 2)
                    act.wait_ge(w_loaded, 16 * 2)
                    activation(win_h[:], win_f, copy).then_inc(w_hi, 1)

                    def move_hi(t, use, dst, w, ready):
                        bank = fb.wait_full(act, t, use)
                        activation(dst, bank[:], copy, scale=w).then_inc(ready, 1)

                    def in_proj(t, m):
                        bank = fb.wait_full(act, t, f"in{m}")
                        dst = xi[:, m, 3:] if m < IC else sz[:, m - IC, :]
                        fb.now_moved(activation(dst, bank[:], ACT.Identity, bias=b_in[:, m:m + 1]), f"in{m}")

                    def silus(t, b):
                        act.wait_ge(conv_done, b + 1)
                        for m in range(3):
                            fb.wait_moved(act, t, f"in{2 * IC - 1 - m}")
                        activation(sz[:], sz[:], ACT.Silu)
                        activation(xc[:], xc[:], ACT.Silu).then_inc(silu_done, 1)

                    def gate(t):
                        bank = fb.wait_full(act, t, "gate0")
                        fb.now_moved(activation(th[:], bank[:], ACT.Tanh, scale=0.5), "gate0")

                    def raw_and_squares(t, b, i):
                        bank = fb.wait_full(act, t, f"qk{i}")
                        activation(qk_raw[:, i, :], bank[:], copy)
                        act.wait_ge(sq_summed, b * NT + i + 1)
                        fb.now_moved(activation(sq[:, i % 2, :], bank[:], ACT.Square), f"qk{i}")

                    def qk_transposed(t, b, c):
                        if c >= 2 or not is_first(b):
                            act.wait_ge(qk_out[c % 2], b * 64 + (c // 2) * 32)
                        move_hi(t, f"qt{c}", qkT[:, c % 2, 0, :], at["qn_w"] if c < 2 else at["kn_w"], qk_hi)

                    def values(t, b, i):
                        bank = fb.wait_full(act, t, f"v{i}")
                        if i == 0 and not is_first(b):
                            act.wait_ge(v_placed, b)
                        fb.now_moved(activation(v2[:, i, :], bank[:, 0:D], copy), f"v{i}")

                    def minus_max(t, b, pair, slot_pair):
                        bank = ob.wait_full(act, t, f"mt{slot_pair - 1}")
                        if pair >= 2 or not is_first(b):
                            act.wait_ge(rows[pair % 2], b * (NPAIR * 8) + (pair // 2) * 16)
                        ob.now_moved(activation(nmT[:, pair % 2, :], bank[0:16, 0:P], copy), f"mt{slot_pair - 1}")

                    def exps(b, pair, n):
                        k = pair * UNITS + n
                        act.wait_ge(st_full, b * PU + k + 1)
                        activation(pt[:, k % PTS, :], st_bank[k % 2][:], ACT.Exp).then_inc(exp_done, 1)

                    def o_move(t, use, dst):
                        bank = ob.wait_full(act, t, use)
                        ob.now_moved(activation(dst, bank[:], copy), use)

                    def turn(t, tail, att, nxt, qkv, mix):
                        for slot in range(PU):
                            p, n = slot // UNITS, slot % UNITS
                            if att is not None:
                                exps(att, p, n)
                            if tail is not None:
                                if due(ODD, "pv-", slot):
                                    o_move(t, "pv-0", oTs[:])
                                for c in due(ODD, "t-", slot):
                                    o_move(t, f"t-{c}", oT[:, c, :])
                            if att is not None:
                                for g in due(ODD, "pv", slot):
                                    o_move(t, f"pv{g}", oTs[:])
                            if n == MT and of_pair(att, nxt, p + 1) is not None:
                                minus_max(t, *of_pair(att, nxt, p + 1), p + 1)
                            if mix is not None:
                                for c in due(FRONT, "zt", slot):
                                    move_hi(t, f"zt{c}", zT_h[:, c, :], at["norm_w"][:, c:c + 1], z_hi)
                                for m in due(FRONT, "in", slot):
                                    if is_first(mix) and m == 0:
                                        act.wait_ge(w_ready, 1)
                                    in_proj(t, m)
                                if is_first(mix) and slot == FRONT["in"][-1]:
                                    act.wait_ge(rest_loaded, 16 * 5)
                                    activation(wqkv_h[:], wqkv_f, copy).then_inc(w_hi, 1)
                            if qkv is not None:
                                for c in due(FRONT, "ht", slot):
                                    move_hi(t, f"ht{c}", zT_h[:, c, :], at["n1_w"][:, c:c + 1], h_hi)
                            if mix is not None and slot == SILU:
                                silus(t, mix)
                            if mix is not None and due(FRONT, "gate", slot):
                                gate(t)
                            if qkv is not None:
                                for i in due(FRONT, "qk", slot):
                                    raw_and_squares(t, qkv, i)
                            if qkv is not None:
                                for i in due(FRONT, "v", slot):
                                    values(t, qkv, i)
                                for c in due(FRONT, "qt", slot):
                                    qk_transposed(t, qkv, c)

                    all_turns(act, turn)

                @block.vector
                def _(dve):
                    link, qlink = Links(dve, dve_mix, 2 + 7 + 1), Links(dve, dve_qk, 11)
                    xlink = Links(dve, dve_x, 1)
                    tt, ts, stt = nc.vector.tensor_tensor, nc.vector.tensor_scalar, nc.vector.scalar_tensor_tensor
                    dve.sem_inc(mx_read, 2)
                    dve.sem_inc(sq_summed, 2)

                    def clear_stacks():
                        nc.vector.memset(qS[:].bitcast(F32), 0.0)
                        nc.vector.memset(kS[0:SR].bitcast(F32), 0.0)
                        nc.vector.memset(kS[SR:P].bitcast(F32), 1.0)

                    def first_weights():
                        dve.wait_ge(w_hi, 1)
                        tt(win_l[:], win_f, win_h[:].bitcast(F32), ALU.subtract).then_inc(w_lo, 1)

                    def biases():
                        dve.wait_ge(bias_mm, 1)
                        tt(b_in[:], mx_bank[0][:, 0:2 * IC], at["in_b"], ALU.add).then_inc(w_ready, 1)

                    def other_weights():
                        dve.wait_ge(rest_loaded, 16 * 5)
                        ts(wout[:], wout[:], 0.5, None, op0=ALU.mult)
                        ts(d2[:], at["D"], 2.0, 1.0, op0=ALU.mult, op1=ALU.add)
                        ts(at["qn_w"], at["qn_w"], float(HD) ** -0.5, None, op0=ALU.mult)
                        nc.vector.tensor_reduce(gate_col[:], wc, AX.X, ALU.add).then_inc(dve_pre, 1)
                        dve.wait_ge(dve_pre, 1)
                        for c in range(IC):
                            ts(wgate[:, c, :], gate_col[:, c:c + 1].to_broadcast([P, P]), 1.0 / HD, None, op0=ALU.mult)

                    def qkv_weights():
                        dve.wait_ge(w_hi, 2)
                        tt(wqkv_l[:], wqkv_f, wqkv_h[:].bitcast(F32), ALU.subtract)

                    def normed(dst, src, m_v, scale):
                        for i in range(NT):
                            last = ts(dst[:, i, :], src[:, i, :], m_v[:, i, 0:1], sm[:, scale, i:i + 1],
                                      op0=ALU.subtract, op1=ALU.mult)
                        return last

                    def row_stats(link, src, m_v):
                        for i in range(NT):
                            last = nc.vector.bn_stats(st6[:, i, :], src[:, i, :])
                        link(last)
                        alone(dve, passed)
                        for i in range(NT):
                            last = nc.vector.bn_aggr(m_v[:, i, :], st6[:, i, :])
                        last.then_inc(stats, 1)

                    def norm_in(b):
                        dve.wait_ge(x_loaded, 16 * (b + 1))
                        xlink.batch(b)
                        row_stats(xlink, x, mv)

                    def make_z(b):
                        dve.wait_ge(scales, b * 3 + 1)
                        normed(z, x, mv, 1).then_inc(z_ready, 1)

                    def move_lo(t, use, dst, hi, w, ready, count):
                        bank = fb.wait_full(dve, t, use)
                        dve.wait_ge(ready, count)
                        fb.now_moved(stt(dst, bank[:], w, hi.bitcast(F32), ALU.mult, ALU.subtract), use)

                    def conv(t, b, step):
                        if step == 0 and not is_first(b):
                            dve.wait_ge(xin_stored, 16 * b)
                        j = step % 4
                        for m in range(2 * (step // 4), 2 * (step // 4) + 2):
                            w = at["conv_w"][:, 4 * m + j:4 * m + j + 1]
                            if j == 0:
                                fb.wait_moved(dve, t, f"in{m}")
                                last = ts(xc[:, m, :], xi[:, m, 0:T], w, at["conv_b"][:, m:m + 1], op0=ALU.mult, op1=ALU.add)
                            else:
                                last = stt(xc[:, m, :], xi[:, m, j:j + T], w, xc[:, m, :], ALU.mult, ALU.add)
                        if step < 7:
                            link(last)
                        else:
                            last.then_inc(conv_done, 1)

                    def y(t, b):
                        fb.wait_moved(dve, t, "gate0")
                        dve.wait_ge(p_ready, b + 1)
                        for c in range(IC):
                            last = stt(sz[:, c, :], th[:], d2[:, c:c + 1], sz[:, c, :], ALU.add, ALU.mult)
                        last.then_inc(y_ready, 1)

                    def mixer_out(t, b, k):
                        dve.wait_ge(ub_ready, b + 1)
                        bank = fb.wait_full(dve, t, f"out{k}")
                        fb.now_moved(tt(z[:, 2 * k:2 * k + 2, :], bank[:].rearrange("p (i d) -> p i d", d=D),
                                        u[:, 2 * k:2 * k + 2, :], ALU.add), f"out{k}")

                    def out_stats(t):
                        fb.wait_moved(dve, t, "out0")
                        fb.wait_moved(dve, t, "out1")
                        row_stats(link, z, mvf)

                    def make_x1(b):
                        dve.wait_ge(scales, b * 3 + 2)
                        link(normed(z, z, mvf, 2))

                    def add_x1(b, i):
                        ins = tt(u[:, 2 * i:2 * i + 2, :], x[:, 2 * i:2 * i + 2, :], z[:, 2 * i:2 * i + 2, :], ALU.add)
                        if i == 1:
                            ins.then_inc(x1_ready, 1)

                    def x1_stats(b):
                        dve.wait_ge(x1_ready, b + 1)
                        row_stats(link, u, mv1)

                    def make_h(b):
                        dve.wait_ge(scales, b * 3 + 3)
                        normed(hz, u, mv1, 4).then_inc(hz_ready, 1)

                    def sum_squares(t, i):
                        fb.wait_moved(dve, t, f"qk{i}")
                        nc.vector.tensor_reduce(ms[:, i * 2 * H:(i + 1) * 2 * H], sq[:, i % 2, :].rearrange("p (h d) -> p h d", d=HD),
                                                AX.X, ALU.add).then_inc(sq_summed, 1)

                    def guess_rsqrt(b):
                        dve.wait_ge(sq_summed, b * NT + NT + 2)
                        qlink(ts(ms[:], ms[:], 1.0 / HD, EPS_RMS, op0=ALU.mult, op1=ALU.add))
                        qlink(ts(rqk[:].bitcast(I32), ms[:].bitcast(I32), -0.5, float(0x5f3759df), op0=ALU.mult, op1=ALU.add))

                    def newton(b, step):
                        qlink(tt(nt[:], rqk[:], rqk[:], ALU.mult))
                        qlink(stt(nt[:], nt[:], -0.5, ms[:], ALU.mult, ALU.mult))
                        qlink(stt(rqk[:], nt[:], 1.5, rqk[:], ALU.add, ALU.mult))

                    def scale_qk():
                        for i in range(NT):
                            a = qk_raw[:, i, :].rearrange("p (h d) -> p h d", d=HD)
                            last = tt(a, a, rqk[:, i * 2 * H:(i + 1) * 2 * H].unsqueeze(2).to_broadcast([P, 2 * H, HD]), ALU.mult)
                        last.then_inc(qk_normed, 1)

                    def maxima(b, pair, n):
                        k = pair * UNITS + n
                        dve.wait_ge(mx_full, b * PU + k + 1)
                        t, m = mx_bank[k % 2], mxs[:, pair % 2, :]
                        if n == 4:
                            last = nc.vector.tensor_reduce(m.rearrange("p (h i) -> p h i", h=2)[:, :, 1],
                                                           t[:].rearrange("p (h c) -> p h c", h=2), AX.X, ALU.max)
                        else:
                            for h, i, c, w in MAX_UNITS[n]:
                                last = nc.vector.tensor_reduce(m[:, h * 4 + i:h * 4 + i + 1], t[:, c:c + w], AX.X, ALU.max)
                        last.then_inc(mx_read, 1)

                    def minus_max(b, pair):
                        k, m = b * NPAIR + pair, mxs[:, pair % 2, :]
                        dve.wait_ge(mx_read, b * PU + (pair + 1) * UNITS + 2)
                        ts(nm[:, pair % 2, 0:8], m, -1.0, None, op0=ALU.mult).then_inc(nm_ready, 1)
                        dve.wait_ge(nm_ready, 2 * k + 1)
                        stt(nm[:, pair % 2, 8:16], m, -1.0, nm[:, pair % 2, 0:8].bitcast(F32),
                            ALU.mult, ALU.subtract).then_inc(nm_ready, 1)

                    def o_norm(t, b, g, use):
                        bank = ob.wait_full(dve, t, use)[:].rearrange("p (i q e) -> p i q e", q=4, e=32)
                        if g == 0 and not is_first(b):
                            dve.wait_ge(xr_stored, 16 * b)
                        nc.vector.reciprocal(rc[:], bank[:, :, :, HD]).then_inc(o_sums, 1)
                        dve.wait_ge(o_sums, 4 * b + g + 1)
                        for e in range(2):
                            pair = 2 * g + e
                            dst = otok[:].rearrange("p i (h f) -> p i h f", h=2)[:, :, :, HD * pair:HD * (pair + 1)]
                            last = tt(dst, bank[:, :, 2 * e:2 * e + 2, 0:HD],
                                      rc[:, :, 2 * e:2 * e + 2].unsqueeze(3).to_broadcast([P, NT, 2, HD]), ALU.mult)
                        ob.now_moved(last, use)

                    def wo_add(t, b, k):
                        bank = ob.wait_full(dve, t, f"wo-{k}")
                        dve.wait_ge(res_loaded, 16 * (b + 1))
                        dst = otok[:, 2 * k:2 * k + 2, ZM:]
                        ob.now_moved(tt(dst, bank[:, 0:2 * DO].rearrange("p (i d) -> p i d", d=DO), dst, ALU.add), f"wo-{k}")

                    def turn(t, tail, att, nxt, qkv, mix):
                        if mix is not None:
                            link.batch(mix)
                        if is_first(mix):
                            norm_in(mix)
                            first_weights()
                            make_z(mix)
                        if qkv is not None:
                            qlink.batch(qkv)
                        for slot in range(PU):
                            p, n = slot // UNITS, slot % UNITS
                            if of_pair(att, nxt, p + 2) is not None:
                                maxima(*of_pair(att, nxt, p + 2), n)
                                if n == 4:
                                    minus_max(*of_pair(att, nxt, p + 2))
                            if tail is not None:
                                if due(ODD, "ot-", slot):
                                    o_norm(t, tail, 3, "ot-0")
                                for k in due(ODD, "wo-", slot):
                                    wo_add(t, tail, k)
                            if att is not None:
                                for g in due(ODD, "ot", slot):
                                    o_norm(t, att, g, f"ot{g}")
                            if mix is not None:
                                if is_first(mix):
                                    if slot == FRONT["in"][0]:
                                        biases()
                                        other_weights()
                                    if slot == SILU:
                                        qkv_weights()
                                        clear_stacks()
                                if slot == Y:
                                    y(t, mix)
                                if slot == STATS and has_next(mix):
                                    norm_in(mix + 1)
                                if slot == NORM and has_next(mix):
                                    make_z(mix + 1)
                                for c in due(FRONT, "zt", slot):
                                    move_lo(t, f"zt{c}", zT_l[:, c, :], zT_h[:, c, :], at["norm_w"][:, c:c + 1],
                                            z_hi, mix * KC + c + 1)
                            if qkv is not None:
                                for c in due(FRONT, "ht", slot):
                                    move_lo(t, f"ht{c}", zT_l[:, c, :], zT_h[:, c, :], at["n1_w"][:, c:c + 1],
                                            h_hi, qkv * KC + c + 1)
                                for i in due(FRONT, "qk", slot - 1):
                                    sum_squares(t, i)
                                if slot == GUESS:
                                    guess_rsqrt(qkv)
                                for k in range(3):
                                    if slot == (GUESS, *NEWTON)[k]:
                                        newton(qkv, k)
                                if slot == SCALE:
                                    scale_qk()
                                for c in due(FRONT, "qt", slot):
                                    w = at["qn_w"] if c < 2 else at["kn_w"]
                                    move_lo(t, f"qt{c}", qkT[:, c % 2, 1, :], qkT[:, c % 2, 0, :], w, qk_hi, qkv * 4 + c + 1)
                            if mix is not None:
                                step = slot - FRONT["in"][1] - 1
                                if 0 <= step < 8:
                                    conv(t, mix, step)
                                for k in due(FRONT, "out", slot - 1):
                                    mixer_out(t, mix, k)
                                if slot == STATS_OUT:
                                    out_stats(t)
                                if slot == X1:
                                    make_x1(mix)
                                if slot in (X1 + 1, X1 + 2):
                                    add_x1(mix, slot - X1 - 1)
                                if slot == X1 + 3:
                                    x1_stats(mix)
                                if slot == HZ:
                                    make_h(mix)

                    all_turns(dve, turn)

                @block.tensor
                def _(pe):
                    mm = nc.tensor.matmul

                    def split(out_ap, stat, mov):
                        for c in range(KC):
                            (sh, sl), (mh, ml) = stat(c), mov(c)
                            for s, m in ((sh, mh), (sh, ml), (sl, mh)):
                                last = mm(out_ap, s, m, start=(c == 0 and s is sh and m is mh), stop=(c == KC - 1 and s is sl))
                        return last

                    def transposes(bank, sources):
                        for i, src in enumerate(sources):
                            last = nc.tensor.transpose(bank[:, i * P:(i + 1) * P], src, ident[:])
                        return last

                    pe.wait_ge(w_loaded, 16 * 2)
                    for m in range(2 * IC):
                        for c in range(KC):
                            last = mm(mx_bank[0][:, m:m + 1], win_f[:, c, m * P:(m + 1) * P], at["norm_b"][:, c:c + 1],
                                      start=(c == 0), stop=(c == KC - 1))
                    last.then_inc(bias_mm, 1)
                    pe.wait_ge(consts, 1)
                    pe.wait_ge(w_lo, 1)

                    def z_transposes(t, b, c, src, name, ready):
                        if c == 0:
                            pe.wait_ge(ready, b + 1)
                        bank = fb.wait_free(pe, t, f"{name}{c}")
                        fb.now_full(transposes(bank, [src[:, i, c * P:(c + 1) * P] for i in range(NT)]), f"{name}{c}")

                    def in_proj(t, m):
                        if m == 0:
                            for c in range(KC):
                                fb.wait_moved(pe, t, f"zt{c}")
                        bank = fb.wait_free(pe, t, f"in{m}")
                        cols = slice(m * P, (m + 1) * P)
                        fb.now_full(split(bank[:], lambda c: (win_h[:, c, cols], win_l[:, c, cols]),
                                          lambda c: (zT_h[:, c, :], zT_l[:, c, :])), f"in{m}")

                    def gate(t, b):
                        pe.wait_ge(silu_done, b + 1)
                        bank = fb.wait_free(pe, t, "gate0")
                        for c in range(IC):
                            last = mm(bank[:], wgate[:, c, :], xc[:, c, :], start=(c == 0), stop=(c == IC - 1))
                        fb.now_full(last, "gate0")

                    def out_proj(t, b, k, i):
                        if k == 0 and i == 0:
                            pe.wait_ge(y_ready, b + 1)
                        bank = fb.wait_free(pe, t, f"out{k}") if i == 0 else fb.tile(f"out{k}")
                        tok = slice((2 * k + i) * P, (2 * k + i + 1) * P)
                        for c in range(IC):
                            last = mm(bank[:, i * D:(i + 1) * D], sz[:, c, tok], wout[:, c, :], start=(c == 0), stop=(c == IC - 1))
                        if i == 1:
                            fb.now_full(last, f"out{k}")

                    def qkv_product(t, use, i, cols):
                        bank = fb.wait_free(pe, t, use)
                        tok = slice(i * P, (i + 1) * P)
                        n = cols.stop - cols.start
                        fb.now_full(split(bank[:, 0:n], lambda c: (zT_h[:, c, tok], zT_l[:, c, tok]),
                                          lambda c: (wqkv_h[:, c, cols], wqkv_l[:, c, cols])), use)

                    def qk(t, i):
                        if i == 0:
                            for c in range(KC):
                                fb.wait_moved(pe, t, f"ht{c}")
                        qkv_product(t, f"qk{i}", i, slice(0, 2 * D))

                    def qk_transposes(t, b, c):
                        if c == 0:
                            pe.wait_ge(qk_normed, b + 1)
                        bank = fb.wait_free(pe, t, f"qt{c}")
                        fb.now_full(transposes(bank, [qk_raw[:, i, c * P:(c + 1) * P] for i in range(NT)]), f"qt{c}")

                    def scores_for_max(b, pair, n):
                        s, k = pair % SLOTS, pair * UNITS + n
                        if n == 0:
                            pe.wait_ge(stacked[s], b * (NPAIR // SLOTS * 32) + (pair // SLOTS + 1) * 32)
                        pe.wait_ge(mx_read, b * PU + k + 1)
                        t = mx_bank[k % 2]
                        for h, i, c, w in MAX_UNITS[n]:
                            mm(t[:, c:c + w], qS[0:SR, s, h, i * P:(i + 1) * P], kS[0:SR, s, h, 0:w], start=True, stop=False)
                            last = mm(t[:, c + i * P:c + w], ident16[:], mask_q[:], start=False, stop=True)
                        last.then_inc(mx_full, 1)

                    def max_transposed(t, b, pair, slot_pair):
                        pe.wait_ge(nm_ready, 2 * (b * NPAIR + pair) + 2)
                        bank = ob.wait_free(pe, t, f"mt{slot_pair - 1}")
                        ob.now_full(nc.tensor.transpose(bank[0:16, 0:P], nm[:, pair % 2, :].bitcast(F32), ident[:]), f"mt{slot_pair - 1}")

                    def scores(b, pair, n):
                        s, k = pair % SLOTS, pair * UNITS + n
                        if n == 0:
                            pe.wait_ge(rows[pair % 2], b * (NPAIR * 8) + (pair // 2 + 1) * 16)
                        pe.wait_ge(exp_done, b * PU + k + 1)
                        t = st_bank[k % 2]
                        for h, j, c, w in ST_UNITS[n]:
                            mm(t[:, c:c + w], kS[0:SR + 2, s, h, j * P:(j + 1) * P], qS[0:SR + 2, s, h, j * P:T], start=True, stop=False)
                            last = mm(t[:, c:c + P], ident16[:], mask_k[:], start=False, stop=True)
                        last.then_inc(st_full, 1)

                    def values_summed(t, b, g, use):
                        pe.wait_ge(exp_done, b * PU + (2 * g + 2) * UNITS + 2)
                        if g == 0:
                            pe.wait_ge(v_placed, b + 1)
                        bank = ob.wait_free(pe, t, use)
                        for j in range(NT):
                            for q in range(4):
                                pair, h = 2 * g + q // 2, q % 2
                                n, c, w = pt_at[h, j]
                                last = mm(bank[32 * q:32 * (q + 1), j * P:T], v[:, j, h * CH + pair, :],
                                          pt[:, (pair * UNITS + n) % PTS, c:c + w], start=(j == 0), stop=(j == NT - 1))
                        ob.now_full(last, use)

                    def o_back(t, pv, use):
                        ob.wait_moved(pe, t, pv)
                        bank = ob.wait_free(pe, t, use)
                        ob.now_full(transposes(bank, [oTs[:, i * P:(i + 1) * P] for i in range(NT)]), use)

                    def o_transposed(t, c):
                        if c == 0:
                            ob.wait_moved(pe, t, "ot-0")
                        bank = ob.wait_free(pe, t, f"t-{c}")
                        ob.now_full(transposes(bank, [otok[:, i, c * P:(c + 1) * P] for i in range(NT)]), f"t-{c}")

                    def o_proj(t, k):
                        if k == 0:
                            for c in range(KC):
                                ob.wait_moved(pe, t, f"t-{c}")
                        bank = ob.wait_free(pe, t, f"wo-{k}")
                        for i in range(2):
                            tok = slice((2 * k + i) * P, (2 * k + i + 1) * P)
                            for c in range(KC):
                                last = mm(bank[:, i * DO:(i + 1) * DO], oT[:, c, tok], wo[:, c, :], start=(c == 0), stop=(c == KC - 1))
                        ob.now_full(last, f"wo-{k}")

                    def turn(t, tail, att, nxt, qkv, mix):
                        fb.start(pe, t)
                        ob.start(pe, t)
                        for slot in range(PU):
                            p, n = slot // UNITS, slot % UNITS
                            if att is not None:
                                scores(att, p, n)
                            if of_pair(att, nxt, p + 2) is not None:
                                scores_for_max(*of_pair(att, nxt, p + 2), n)
                            if tail is not None:
                                if due(ODD, "pv-", slot):
                                    values_summed(t, tail, 3, "pv-0")
                                if due(ODD, "ot-", slot):
                                    o_back(t, "pv-0", "ot-0")
                                for c in due(ODD, "t-", slot):
                                    o_transposed(t, c)
                                for k in due(ODD, "wo-", slot):
                                    o_proj(t, k)
                            if att is not None:
                                for g in due(ODD, "pv", slot):
                                    values_summed(t, att, g, f"pv{g}")
                                for g in due(ODD, "ot", slot):
                                    o_back(t, f"pv{g}", f"ot{g}")
                            if n == MT and of_pair(att, nxt, p + 1) is not None:
                                max_transposed(t, *of_pair(att, nxt, p + 1), p + 1)
                            if mix is not None:
                                for c in due(FRONT, "zt", slot):
                                    z_transposes(t, mix, c, z, "zt", z_ready)
                                for m in due(FRONT, "in", slot):
                                    in_proj(t, m)
                            if qkv is not None:
                                for c in due(FRONT, "ht", slot):
                                    z_transposes(t, qkv, c, hz, "ht", hz_ready)
                            if mix is not None and due(FRONT, "gate", slot):
                                gate(t, mix)
                            if qkv is not None:
                                for i in due(FRONT, "qk", slot):
                                    qk(t, i)
                                for i in due(FRONT, "v", slot):
                                    qkv_product(t, f"v{i}", i, slice(2 * D, 3 * D))
                                for c in due(FRONT, "qt", slot):
                                    qk_transposes(t, qkv, c)
                            if mix is not None:
                                for i in range(2):
                                    for k in due(FRONT, "out", slot - i):
                                        out_proj(t, mix, k, i)
                        fb.finish(pe)
                        ob.finish(pe)

                    all_turns(pe, turn)

        experts(nc, ctx, d, banks, x1_dram, xr_dram, out_dram)


def experts(nc, ctx, d, banks, x1_dram, xr_dram, out_dram):
    B, _, NT, D = out_dram.shape
    T = NT * P
    KC = D // P
    HC = d["e0_down"].shape[1]
    DO = d["e0_down"].shape[2]
    ZM = D - DO
    E = 4
    LARGEST = 3.4028234663852886e38

    def sb(name, shape, dt=F32):
        return ctx.enter_context(nc.sbuf_tensor(name, shape, dt))

    def sem(name):
        return ctx.enter_context(nc.semaphore(name))

    UPS = ["e2_l1", "e0_up", "e2_l2", "e3_down", "e1_w1", "e1_w2", "e2_l3", "e3_up"]
    DOWNS = ["e0_down", "e1_down", "e2_l4", "e3_out"]
    up_h = {n: sb(n + "_h", [P, *d[n].shape[1:]], F32R) for n in UPS}
    up_l = {n: sb(n + "_l", [P, *d[n].shape[1:]], F32R) for n in UPS}
    down = {n: sb(n + "_sb", [P, HC, DO]) for n in DOWNS}
    gate_w = sb("gate_w_sb", [P, KC, E])
    n2_w = sb("n2_w_sb", [P, KC])
    ident = sb("ident2", [P, P])
    minus_half = sb("minus_half2", [P, NT])

    hid = [sb(f"hidden{e}", [P, HC, T]) for e in range(4)]
    gates, exact = sb("gates", [P, 2, T]), sb("exact", [P, 2, T])
    stage = {"e2_l1": hid[0][:, 0:2, :], "e0_up": hid[0][:, 2:4, :], "e2_l2": hid[1][:], "e3_down": sb("stage_e3", [P, KC, D])[:],
             "e1_w1": gates[:], "e1_w2": hid[3][:, 0:2, :], "e2_l3": hid[2][:], "e3_up": hid[3][:, 2:4, :]}
    h1 = sb("h1_h", [P, HC, T], F32R), sb("h1_l", [P, HC, T], F32R)
    h2 = sb("h2_h", [P, HC, T], F32R), sb("h2_l", [P, HC, T], F32R)
    h3 = sb("h3_h", [P, KC, T], F32R), sb("h3_l", [P, KC, T], F32R)
    xf = sb("xf_h", [P, KC, T], F32R), sb("xf_l", [P, KC, T], F32R)
    xr = sb("xr_sb", [P, 2, NT, D])
    x1 = sb("x1_sb", [P, 2, NT, D])
    xz = sb("xz", [P, NT, D])
    ssx, e1, r2, rf, ef = (sb(n, [P, NT]) for n in ("ssx", "e_rms", "r_rms", "r_f", "e_f"))
    st6, mvf = sb("st6_f", [P, NT, 6]), sb("mv_f", [P, NT, 2])
    raw, lg, dl, ex, pr, wts = (sb(n, [P, NT, E]) for n in ("raw", "lg", "dl", "ex", "pr", "wts"))
    finite = sb("finite", [P, NT, E], U32)
    beats = sb("beats", [P, NT, E, E])
    rank = sb("rank", [P, NT, E])
    m1, s1, i1, s2, i2 = (sb(n, [P, NT]) for n in ("m1", "s1", "i1", "s2", "i2"))

    up_units = [("e2_l1", m, "xf", "split") for m in range(HC)] + [("e0_up", m, "xf", 0) for m in range(HC)]
    up_units += [("e2_l2", m, "h1", "split") for m in range(HC)] + [("e3_down", m, "xf", "split") for m in range(KC)]
    for m in range(HC):
        up_units += [("e1_w1", m, "xf", "silu"), ("e1_w2", m, "xf", "times")]
    up_units += [("e2_l3", m, "h2", 2) for m in range(HC)] + [("e3_up", m, "h3", 3) for m in range(HC)]
    moving = {"xf": xf, "h1": h1, "h2": h2, "h3": h3}
    split_into = {"e2_l1": h1, "e2_l2": h2, "e3_down": h3}
    UB = Banks(banks[0:4], [sem(f"up_full{i}") for i in range(4)], [sem(f"up_moved{i}") for i in range(4)],
               2 + len(up_units))
    DB = Banks(banks[4:7], [sem(f"down_full{i}") for i in range(3)], [sem(f"down_moved{i}") for i in range(3)], 9)
    down_order = [0, 1, 3, 2]
    D_USE = {(e, k): 1 + 2 * n + k for n, e in enumerate(down_order) for k in range(2)}

    w_in = [sem(f"w_in{i}") for i in range(len(UPS))]
    down_loaded = sem("down_loaded")
    w2_loaded, consts2, w_hi2, w_lo2 = sem("w2_loaded"), sem("consts2"), sem("w_hi2"), sem("w_lo2")
    x_in = [sem("x_in0"), sem("x_in1")]
    sq_in, rms_scale, xz_ready, xf_hi = sem("sq_in"), sem("rms_scale"), sem("xz_ready"), sem("xf_hi")
    exact_ready, lo_ready = sem("exact_ready"), sem("lo_ready")
    shifted, ex_ready = sem("shifted"), sem("ex_ready")
    f_stats, f_scale, out_ready = sem("f_stats"), sem("f_scale"), sem("out_ready")
    stored = [sem("stored0"), sem("stored1")]
    dve2, pool_e1, pool_ef = sem("dve2"), sem("pool_e1"), sem("pool_ef")
    passed2 = sem("passed2")
    SPLITS = 2 * HC + KC

    def each_batch(eng, turn):
        with eng.Fori(0, B // 2 - 1) as k:
            turn(2 * k, 2 * k + 1, 0)
            turn(2 * k + 1, 2 * k + 2, 1)
        turn(B - 2, B - 1, 0)
        turn(B - 1, None, 1)

    with nc.Block() as block:

        @block.sync
        def _(sp):
            def load(b, par):
                sp.dma_start(xr[:, par, :, :], of_batch(xr_dram, b)).then_inc(x_in[par], 16)
                sp.dma_start(x1[:, par, :, :], of_batch(x1_dram, b)).then_inc(x_in[par], 16)

            load(0, 0)
            sp.dma_start(n2_w[:], d["n2_w"]).then_inc(w2_loaded, 16)
            sp.dma_start(gate_w[:], d["gate_w"]).then_inc(w2_loaded, 16)
            for n, s in zip(UPS, w_in):
                sp.dma_start(stage[n], d[n]).then_inc(s, 16)
            for n in DOWNS:
                sp.dma_start(down[n][:], d[n]).then_inc(down_loaded, 16)
            load(1, 1)
            with sp.Fori(0, B // 2 - 1) as k:
                for par in range(2):
                    b = 2 * k + par
                    sp.wait_ge(out_ready, b + 1)
                    alone(sp, passed2)
                    sp.dma_start(of_batch(out_dram, b), x1[:, par, :, :]).then_inc(stored[par], 16)
                    sp.wait_ge(stored[par], 16 * k + 16)
                    alone(sp, passed2)
                    load(b + 2, par)
            for par in range(2):
                sp.wait_ge(out_ready, B - 2 + par + 1)
                sp.dma_start(of_batch(out_dram, B - 2 + par), x1[:, par, :, :]).then_inc(stored[par], 16)
            for par in range(2):
                sp.wait_ge(stored[par], 16 * (B // 2))

        def wait_loaded(eng, b, par):
            eng.wait_ge(x_in[par], 16 * b - 16 * par + 32)

        @block.gpsimd
        def _(pool):
            nc.gpsimd.memset(ident[:], 0.0)
            nc.gpsimd.memset(minus_half[:], -0.5)
            nc.gpsimd.memset(beats[:], 0.0).then_inc(consts2, 1)
            pool.wait_ge(consts2, 1)
            nc.gpsimd.affine_select(out=ident[:], in_=ident[:], compare_op=ALU.not_equal, fill=1.0,
                                    base=0, pattern=[[-1, P]], channel_multiplier=1).then_inc(consts2, 1)
            tt, ts = nc.gpsimd.tensor_tensor, nc.gpsimd.tensor_scalar

            def head(b):
                pool.wait_ge(sq_in, b + 1)
                alone(pool, passed2)
                ts(e1[:], ssx[:], 1.0 / D, EPS_RMS, op0=ALU.mult, op1=ALU.add).then_inc(pool_e1, 1)
                pool.wait_ge(pool_e1, b + 1)
                tt(r2[:], e1[:], minus_half[:], ALU.pow).then_inc(rms_scale, 1)

            def turn(b, nxt, par):
                if nxt is not None:
                    head(nxt)
                pool.wait_ge(f_stats, b + 1)
                alone(pool, passed2)
                ts(ef[:], mvf[:, :, 1], EPS_LN, None, op0=ALU.add).then_inc(pool_ef, 1)
                pool.wait_ge(pool_ef, b + 1)
                tt(rf[:], ef[:], minus_half[:], ALU.pow).then_inc(f_scale, 1)

            head(0)
            each_batch(pool, turn)

        @block.scalar
        def _(act):
            activation, copy = nc.scalar.activation, ACT.Copy
            for s in UB.moved + DB.moved:
                act.sem_inc(s, 1)

            def head(b, par):
                wait_loaded(act, b, par)
                for i in range(NT):
                    ins = activation(xz[:, i, :], xr[:, par, i, :], ACT.Square, accum_out=ssx[:, i:i + 1])
                ins.then_inc(sq_in, 1)

            def move_xf_hi(b):
                for c in range(KC):
                    t = UB.wait_full(act, b, c)
                    activation(xf[0][:, c, :], t[:], copy, scale=n2_w[:, c:c + 1]).then_inc(xf_hi, 1)

            def up(b, n, count):
                name, m, _, kind = up_units[n]
                t = UB.wait_full(act, b, 2 + n)
                if kind == "split":
                    k = count["split"]
                    count["split"] += 1
                    act.wait_ge(lo_ready, b * SPLITS + k + 1)
                    activation(exact[:, k % 2, :], t[:], ACT.Gelu).then_inc(exact_ready, 1)
                    UB.now_moved(activation(split_into[name][0][:, m, :], t[:], ACT.Gelu), 2 + n)
                elif kind == "silu":
                    if m >= 2:
                        UB.wait_moved(act, b, 2 + n - 3)
                    UB.now_moved(activation(gates[:, m % 2, :], t[:], ACT.Silu), 2 + n)
                elif kind != "times":
                    UB.now_moved(activation(hid[kind][:, m, :], t[:], ACT.Gelu), 2 + n)

            def turn(b, nxt, par):
                count = {"split": 0}
                for n in range(3 * HC + KC):
                    up(b, n, count)
                act.wait_ge(shifted, b + 1)
                activation(ex[:], dl[:], ACT.Exp).then_inc(ex_ready, 1)
                if nxt is not None:
                    head(nxt, 1 - par)
                for n in range(3 * HC + KC, len(up_units)):
                    up(b, n, count)
                if nxt is not None:
                    move_xf_hi(nxt)

            def split_weights(names):
                for n in names:
                    act.wait_ge(w_in[UPS.index(n)], 16)
                    activation(up_h[n][:], stage[n], copy).then_inc(w_hi2, 1)

            head(0, 0)
            split_weights(UPS[0:2])
            act.wait_ge(w2_loaded, 16 * 2)
            move_xf_hi(0)
            split_weights(UPS[2:])
            each_batch(act, turn)

        @block.vector
        def _(dve):
            tt, ts, stt = nc.vector.tensor_tensor, nc.vector.tensor_scalar, nc.vector.scalar_tensor_tensor
            reduce = nc.vector.tensor_reduce
            link = Links(dve, dve2, 16)
            dve.sem_inc(lo_ready, 2)

            def head(b, par):
                dve.wait_ge(rms_scale, b + 1)
                wait_loaded(dve, b, par)
                for i in range(NT):
                    last = ts(xz[:, i, :], xr[:, par, i, :], r2[:, i:i + 1], None, op0=ALU.mult)
                last.then_inc(xz_ready, 1)

            def move_xf_lo(b):
                for c in range(KC):
                    t = UB.wait_full(dve, b, c)
                    dve.wait_ge(xf_hi, b * KC + c + 1)
                    UB.now_moved(stt(xf[1][:, c, :], t[:], n2_w[:, c:c + 1], xf[0][:, c, :].bitcast(F32),
                                     ALU.mult, ALU.subtract), c)

            def wide(a):
                return a.unsqueeze(2).to_broadcast([P, NT, E])

            def logits(b):
                t = DB.wait_full(dve, b, 0)
                nc.vector.memset(lg[:], 0.0)
                ins = nc.vector.tensor_copy(raw[:], t[:, 0:NT * E].rearrange("p (i e) -> p i e", e=E))
                DB.now_moved(ins, 0)
                DB.wait_moved(dve, b, 0)
                link(tt(finite[:], raw[:], raw[:], ALU.is_equal))
                alone(dve, passed2)
                link(nc.vector.copy_predicated(lg[:], finite[:], raw[:]))
                link(ts(lg[:], lg[:], LARGEST, -LARGEST, op0=ALU.min, op1=ALU.max))
                link(reduce(m1[:], lg[:], AX.X, ALU.max))
                tt(dl[:], lg[:], wide(m1[:]), ALU.subtract).then_inc(shifted, 1)

            def choose(b):
                dve.wait_ge(ex_ready, b + 1)
                link(reduce(s1[:], ex[:], AX.X, ALU.add))
                link(nc.vector.reciprocal(i1[:], s1[:]))
                link(tt(pr[:], ex[:], wide(i1[:]), ALU.mult))
                for e in range(E):
                    if e > 0:
                        last = tt(beats[:, :, e, 0:e], pr[:, :, 0:e], pr[:, :, e:e + 1].to_broadcast([P, NT, e]), ALU.is_ge)
                    if e < E - 1:
                        last = tt(beats[:, :, e, e + 1:], pr[:, :, e + 1:], pr[:, :, e:e + 1].to_broadcast([P, NT, E - 1 - e]), ALU.is_gt)
                link(last)
                link(reduce(rank[:], beats[:], AX.X, ALU.add))
                link(stt(wts[:], rank[:], 2.0, pr[:], ALU.is_lt, ALU.mult))
                link(reduce(s2[:], wts[:], AX.X, ALU.add))
                link(ts(s2[:], s2[:], 1e-8, None, op0=ALU.add))
                link(nc.vector.reciprocal(i2[:], s2[:]))
                link(tt(wts[:], wts[:], wide(i2[:]), ALU.mult))

            def up(b, n, count):
                name, m, _, kind = up_units[n]
                if kind == "split":
                    k = count["split"]
                    count["split"] += 1
                    dve.wait_ge(exact_ready, b * SPLITS + k + 1)
                    UB.wait_moved(dve, b, 2 + n)
                    tt(split_into[name][1][:, m, :], exact[:, k % 2, :], split_into[name][0][:, m, :].bitcast(F32),
                       ALU.subtract).then_inc(lo_ready, 1)
                elif kind == "times":
                    t = UB.wait_full(dve, b, 2 + n)
                    UB.wait_moved(dve, b, 1 + n)
                    UB.now_moved(tt(hid[1][:, m, :], t[:], gates[:, m % 2, :], ALU.mult), 2 + n)

            def combine(b, par):
                for n, e in enumerate(down_order):
                    for k in range(2):
                        t = DB.wait_full(dve, b, D_USE[e, k])
                        if n > 0:
                            DB.wait_moved(dve, b, D_USE[down_order[n - 1], k])
                        for i in range(2):
                            acc = xr[:, par, 2 * k + i, ZM:]
                            last = stt(acc, t[:, i * DO:(i + 1) * DO], wts[:, 2 * k + i, e:e + 1], acc, ALU.mult, ALU.add)
                        DB.now_moved(last, D_USE[e, k])

            def last_norm(b, par):
                for k in range(2):
                    DB.wait_moved(dve, b, D_USE[down_order[-1], k])
                for i in range(NT):
                    last = nc.vector.bn_stats(st6[:, i, :], xr[:, par, i, :])
                link(last)
                alone(dve, passed2)
                for i in range(NT):
                    last = nc.vector.bn_aggr(mvf[:, i, :], st6[:, i, :])
                last.then_inc(f_stats, 1)
                dve.wait_ge(f_scale, b + 1)
                for i in range(NT):
                    last = ts(xr[:, par, i, :], xr[:, par, i, :], mvf[:, i, 0:1], rf[:, i:i + 1], op0=ALU.subtract, op1=ALU.mult)
                link(last)
                tt(x1[:, par, :, :], x1[:, par, :, :], xr[:, par, :, :], ALU.add).then_inc(out_ready, 1)

            def turn(b, nxt, par):
                link.batch(b)
                count = {"split": 0}
                logits(b)
                for n in range(3 * HC + KC):
                    up(b, n, count)
                choose(b)
                if nxt is not None:
                    head(nxt, 1 - par)
                for n in range(3 * HC + KC, len(up_units)):
                    up(b, n, count)
                if nxt is not None:
                    move_xf_lo(nxt)
                combine(b, par)
                last_norm(b, par)

            def split_weights(first, last):
                for n in range(first, last):
                    dve.wait_ge(w_hi2, n + 1)
                    tt(up_l[UPS[n]][:], stage[UPS[n]], up_h[UPS[n]][:].bitcast(F32), ALU.subtract).then_inc(w_lo2, 1)

            dve.wait_ge(consts2, 2)
            head(0, 0)
            split_weights(0, 2)
            dve.wait_ge(w2_loaded, 16 * 2)
            move_xf_lo(0)
            split_weights(2, len(UPS))
            each_batch(dve, turn)

        @block.tensor
        def _(pe):
            mm = nc.tensor.matmul

            def xf_transposes(b):
                pe.wait_ge(xz_ready, b + 1)
                for c in range(KC):
                    t = UB.wait_free(pe, b, c)
                    for i in range(NT):
                        last = nc.tensor.transpose(t[:, i * P:(i + 1) * P], xz[:, i, c * P:(c + 1) * P], ident[:])
                    UB.now_full(last, c)

            def gate(b):
                for c in range(KC):
                    UB.wait_moved(pe, b, c)
                t = DB.wait_free(pe, b, 0)
                for i in range(NT):
                    for c in range(KC):
                        for s in range(2):
                            last = mm(t[:, i * E:(i + 1) * E], xf[s][:, c, i * P:(i + 1) * P].bitcast(F32), gate_w[:, c, :],
                                      start=(c == 0 and s == 0), stop=(c == KC - 1 and s == 1))
                DB.now_full(last, 0)

            def up(b, n):
                name, m, source, _ = up_units[n]
                if m == 0:
                    pe.wait_ge(w_lo2, UPS.index(name) + 1)
                if m == 0 and source == "h1":
                    pe.wait_ge(lo_ready, b * SPLITS + HC + 2)
                if m == 0 and source == "h2":
                    pe.wait_ge(lo_ready, b * SPLITS + 2 * HC + 2)
                if m == 0 and source == "h3":
                    pe.wait_ge(lo_ready, b * SPLITS + SPLITS + 2)
                t = UB.wait_free(pe, b, 2 + n)
                cols, chunks = slice(m * P, (m + 1) * P), d[name].shape[1]
                for c in range(chunks):
                    for j, (s, v) in enumerate(((0, 0), (0, 1), (1, 0))):
                        w = (up_h, up_l)[s][name][:, c, cols]
                        last = mm(t[:], w, moving[source][v][:, c, :], start=(c == 0 and j == 0), stop=(c == chunks - 1 and j == 2))
                UB.now_full(last, 2 + n)

            def downs(b, e):
                units = [n for n, u in enumerate(up_units) if u[3] == (e if e != 1 else "times")]
                for n in {(2 + n) % UB.n: n for n in units}.values():
                    UB.wait_moved(pe, b, 2 + n)
                pe.wait_ge(down_loaded, 16 * len(DOWNS))
                w = down[DOWNS[e]]
                for k in range(2):
                    t = DB.wait_free(pe, b, D_USE[e, k])
                    for i in range(2):
                        tok = slice((2 * k + i) * P, (2 * k + i + 1) * P)
                        for c in range(HC):
                            last = mm(t[:, i * DO:(i + 1) * DO], hid[e][:, c, tok], w[:, c, :], start=(c == 0), stop=(c == HC - 1))
                    DB.now_full(last, D_USE[e, k])

            def turn(b, nxt, par):
                gate(b)
                for n in range(len(up_units)):
                    up(b, n)
                if nxt is not None:
                    xf_transposes(nxt)
                for e in down_order:
                    downs(b, e)

            pe.wait_ge(consts2, 2)
            pe.wait_ge(w2_loaded, 16 * 2)
            xf_transposes(0)
            each_batch(pe, turn)


_FFN = ["e0_up", "e0_down", "e1_w1", "e1_w2", "e1_down", "e2_l1", "e2_l2", "e2_l3", "e2_l4", "e3_down", "e3_up", "e3_out"]


def kernel(**inputs):
    import numpy as np
    import concourse.bacc as bacc
    from concourse.bass_utils import run_bass_kernel_spmd

    a = {n[3:]: np.asarray(v) for n, v in inputs.items()}

    def by_partition(w):
        return np.ascontiguousarray(w.reshape(w.shape[0] // P, P, -1).transpose(1, 0, 2))

    def columns(v):
        return v.reshape(-1, P).T

    zm = 64
    conv = a["attn_conv_w"][:, 0, :].reshape(-1, P, 4).transpose(1, 0, 2).reshape(P, -1)
    arrays = {
        "x": np.ascontiguousarray(a["attn_x"]),
        "in_w": by_partition(a["attn_in_w"].T),
        "wqkv": by_partition(np.concatenate([a["ffn_wq"].T, a["ffn_wk"].T, a["ffn_wv"].T], axis=1)),
        "out_w": by_partition(a["attn_out_w"].T),
        "wo": by_partition(a["ffn_wo"].T[:, zm:]),
        "xproj_w": by_partition(a["attn_xproj_w"].T),
        "vecs": np.ascontiguousarray(np.concatenate([
            columns(a["attn_norm_w"]), columns(a["attn_norm_b"]), columns(a["attn_in_b"]), conv,
            columns(a["attn_conv_b"]), columns(a["attn_D"]), columns(a["ffn_n1_w"]),
            np.tile(a["ffn_qn_w"], 8)[:, None], np.tile(a["ffn_kn_w"], 8)[:, None]], axis=1)),
        "out_b": np.ascontiguousarray(np.broadcast_to(a["attn_out_b"], (P, a["attn_out_b"].shape[0]))),
        "gate_w": by_partition(a["ffn_gate_w"].T),
        "n2_w": np.ascontiguousarray(columns(a["ffn_n2_w"])),
    }
    for n in _FFN:
        w = a["ffn_" + n].T
        arrays[n] = by_partition(w[:, zm:] if n in ("e0_down", "e1_down", "e2_l4", "e3_out") else w)

    nc = bacc.Bacc("TRN2", target_bir_lowering=False, num_devices=1)
    d = {n: nc.dram_tensor("in_" + n, v.shape, F32, kind="ExternalInput").ap() for n, v in arrays.items()}
    shape = arrays["x"].shape
    scratch = [nc.dram_tensor(n, shape, F32, kind="Internal").ap() for n in ("x1_dram", "xr_dram")]
    heads = (shape[0], 8, 2, 16, 2, shape[1]), (shape[0], 8, 16, 2, 2, shape[1])
    scratch += [nc.dram_tensor(n, s, F32, kind="Internal").ap() for n, s in zip(("q_dram", "k_dram"), heads)]
    out = nc.dram_tensor("out", shape, F32, kind="ExternalOutput").ap()
    mixer_attention_experts(nc, d, scratch, out)
    r = run_bass_kernel_spmd(nc, [{"in_" + n: v for n, v in arrays.items()}], core_ids=[0])
    return r.results[0]["out"]
```
